# Optimizing a Trainium2 kernel written in Bass

```python
import numpy as np
import jax
import jax.numpy as jnp

def _softmax(x, axis=-1):
    return jax.nn.softmax(x, axis=axis)

def _gelu(x):
    return jax.nn.gelu(x, approximate=True)

def _silu(x):
    return jax.nn.silu(x)

def _sigmoid(x):
    return jax.nn.sigmoid(x)

def _layernorm(x, axis=-1, eps=1e-05):
    m = jnp.mean(x, axis=axis, keepdims=True)
    v = jnp.var(x, axis=axis, keepdims=True)
    return (x - m) / jnp.sqrt(v + eps)

def _scatter_add(tgt, idx, src, axis=0):
    return tgt.at[idx].add(src)

def _segment_sum(src, seg, n):
    return jax.ops.segment_sum(src, seg, n)
kernel_name = 'mk_gps_d1_gnn_r8_f167b3'

def setup_inputs(seed: int=0):
    np.random.seed(seed)
    _w = jnp.asarray

    def _rec_inputs():
        import jax
        import jax.numpy as jnp
        _gk = jax.random.key(seed)
        x = -0.0001126 + 1 * jax.random.normal(jax.random.fold_in(_gk, 1), (1250, 768), jnp.float32)
        _s = jax.random.randint(jax.random.fold_in(_gk, 2), (20000,), 0, 1250, jnp.int32)
        _d = jax.random.randint(jax.random.fold_in(_gk, 3), (20000,), 0, 1250, jnp.int32)
        _loop = jnp.arange(1250, dtype=jnp.int32)
        src = jnp.concatenate([_s, _d, _loop])
        dst = jnp.concatenate([_d, _s, _loop])
        _o = jnp.argsort(dst, stable=True)
        src = src[_o]
        dst = dst[_o]
        return (x, src, dst)
    x, src, dst = _rec_inputs()

    def _L0_gnn_setup():
        import jax, jax.numpy as jnp
        import numpy as np
        N = 1250
        E = 12500
        D = 768
        H = 1536
        EPS_MSG = 1e-07
        EPS_BN = 1e-05

        def segment_softmax(logits, seg, num_segments):
            m = jax.ops.segment_max(logits, seg, num_segments=num_segments)
            m = jnp.where(jnp.isfinite(m), m, 0.0)
            e = jnp.exp(logits - m[seg])
            s = jax.ops.segment_sum(e, seg, num_segments=num_segments)
            return e / (s[seg] + 1e-16)
        key = jax.random.key(seed)
        ks = jax.random.split(key, 8)
        x = jax.random.normal(ks[0], (N, D), dtype=jnp.float32)
        edge_index = jax.random.randint(ks[1], (2, E), 0, N, dtype=jnp.int32)
        batch = jnp.zeros((N,), dtype=jnp.int32)
        t = jnp.asarray(1.0, dtype=jnp.float32)
        s1 = 1.0 / np.sqrt(D)
        s2 = 1.0 / np.sqrt(H)
        W1 = jax.random.uniform(ks[2], (D, H), jnp.float32, -s1, s1)
        b1 = jax.random.uniform(ks[3], (H,), jnp.float32, -s1, s1)
        bn_gamma = jnp.ones((H,), jnp.float32)
        bn_beta = jnp.zeros((H,), jnp.float32)
        bn_mean = jnp.zeros((H,), jnp.float32)
        bn_var = jnp.ones((H,), jnp.float32)
        W2 = jax.random.uniform(ks[4], (H, D), jnp.float32, -s2, s2)
        b2 = jax.random.uniform(ks[5], (D,), jnp.float32, -s2, s2)
        return {'x': x, 'edge_index': edge_index, 'batch': batch, 't': t, 'W1': W1, 'b1': b1, 'bn_gamma': bn_gamma, 'bn_beta': bn_beta, 'bn_mean': bn_mean, 'bn_var': bn_var, 'W2': W2, 'b2': b2}
    _L0_gnn_all = _L0_gnn_setup()
    _L0_gnn_in = {k: v for k, v in _L0_gnn_all.items() if k in ('t', 'W1', 'b1', 'bn_gamma', 'bn_beta', 'bn_mean', 'bn_var', 'W2', 'b2')}
    del _L0_gnn_all

    def _L0_mix_setup():
        import jax, jax.numpy as jnp
        import numpy as np
        DIM = 768
        HEADS = 12
        DH = DIM // HEADS
        M = 256
        EPS = 0.0001

        def softmax_kernel(data, proj, is_query):
            data_normalizer = data.shape[-1] ** (-0.25)
            ratio = proj.shape[0] ** (-0.5)
            data_dash = jnp.einsum('bhsd,md->bhsm', data_normalizer * data, proj)
            diag = 0.5 * data_normalizer ** 2 * jnp.sum(data * data, axis=-1, keepdims=True)
            if is_query:
                stab = jnp.max(data_dash, axis=-1, keepdims=True)
            else:
                stab = jnp.max(data_dash, axis=(-2, -1), keepdims=True)
            stab = jax.lax.stop_gradient(stab)
            return ratio * (jnp.exp(data_dash - diag - stab) + EPS)
        key = jax.random.key(seed)
        kx, kq, kk, kv, ko, kp = jax.random.split(key, 6)
        B, S = (8, 512)
        w_scale = DIM ** (-0.5)
        return {'x': jax.random.normal(kx, (B, S, DIM), jnp.float32), 'Wq': jax.random.normal(kq, (DIM, DIM), jnp.float32) * w_scale, 'Wk': jax.random.normal(kk, (DIM, DIM), jnp.float32) * w_scale, 'Wv': jax.random.normal(kv, (DIM, DIM), jnp.float32) * w_scale, 'Wo': jax.random.normal(ko, (DIM, DIM), jnp.float32) * w_scale, 'proj': jax.random.normal(kp, (M, DH), jnp.float32)}
    _L0_mix_all = _L0_mix_setup()
    _L0_mix_in = {k: v for k, v in _L0_mix_all.items() if k in ('Wq', 'Wk', 'Wv', 'Wo', 'proj')}
    del _L0_mix_all

    def _L0_ffn_setup():
        import jax, jax.numpy as jnp
        import numpy as np
        S, B, DIM = (1024, 4, 768)
        N_EXPERTS = 8
        HID = 256
        key = jax.random.key(seed)
        ks = jax.random.split(key, 6)
        scale = 0.02
        return {'hidden_states': jax.random.normal(ks[0], (S, B, DIM), dtype=jnp.float32), 'router_w': jax.random.normal(ks[1], (DIM, N_EXPERTS), dtype=jnp.float32) * scale, 'router_b': jnp.zeros((N_EXPERTS,), dtype=jnp.float32), 'w1': jax.random.normal(ks[2], (N_EXPERTS, DIM, HID), dtype=jnp.float32) * scale, 'w2': jax.random.normal(ks[3], (N_EXPERTS, DIM, HID), dtype=jnp.float32) * scale, 'w3': jax.random.normal(ks[4], (N_EXPERTS, HID, DIM), dtype=jnp.float32) * scale}
    _L0_ffn_all = _L0_ffn_setup()
    _L0_ffn_in = {k: v for k, v in _L0_ffn_all.items() if k in ('router_w', 'router_b', 'w1', 'w2', 'w3')}
    del _L0_ffn_all
    return {'x': x, 'src': src, 'dst': dst, 'L0_gnn_t': _L0_gnn_in['t'], 'L0_gnn_W1': _L0_gnn_in['W1'], 'L0_gnn_b1': _L0_gnn_in['b1'], 'L0_gnn_bn_gamma': _L0_gnn_in['bn_gamma'], 'L0_gnn_bn_beta': _L0_gnn_in['bn_beta'], 'L0_gnn_bn_mean': _L0_gnn_in['bn_mean'], 'L0_gnn_bn_var': _L0_gnn_in['bn_var'], 'L0_gnn_W2': _L0_gnn_in['W2'], 'L0_gnn_b2': _L0_gnn_in['b2'], 'L0_mix_Wq': _L0_mix_in['Wq'], 'L0_mix_Wk': _L0_mix_in['Wk'], 'L0_mix_Wv': _L0_mix_in['Wv'], 'L0_mix_Wo': _L0_mix_in['Wo'], 'L0_mix_proj': _L0_mix_in['proj'], 'L0_ffn_router_w': _L0_ffn_in['router_w'], 'L0_ffn_router_b': _L0_ffn_in['router_b'], 'L0_ffn_w1': _L0_ffn_in['w1'], 'L0_ffn_w2': _L0_ffn_in['w2'], 'L0_ffn_w3': _L0_ffn_in['w3']}

def reference(x, src, dst, L0_gnn_t, L0_gnn_W1, L0_gnn_b1, L0_gnn_bn_gamma, L0_gnn_bn_beta, L0_gnn_bn_mean, L0_gnn_bn_var, L0_gnn_W2, L0_gnn_b2, L0_mix_Wq, L0_mix_Wk, L0_mix_Wv, L0_mix_Wo, L0_mix_proj, L0_ffn_router_w, L0_ffn_router_b, L0_ffn_w1, L0_ffn_w2, L0_ffn_w3):
    import jax
    import jax.numpy as jnp

    def _L0_gnn_ref(x, edge_index, batch, t, W1, b1, bn_gamma, bn_beta, bn_mean, bn_var, W2, b2):
        import jax, jax.numpy as jnp
        import numpy as np
        N = 1250
        E = 12500
        D = 768
        H = 1536
        EPS_MSG = 1e-07
        EPS_BN = 1e-05

        def segment_softmax(logits, seg, num_segments):
            m = jax.ops.segment_max(logits, seg, num_segments=num_segments)
            m = jnp.where(jnp.isfinite(m), m, 0.0)
            e = jnp.exp(logits - m[seg])
            s = jax.ops.segment_sum(e, seg, num_segments=num_segments)
            return e / (s[seg] + 1e-16)
        src, dst = (edge_index[0], edge_index[1])
        msg = jax.nn.relu(x[src]) + EPS_MSG
        alpha = segment_softmax(msg * t, dst, N)
        agg = jax.ops.segment_sum(msg * alpha, dst, num_segments=N)
        out = agg + x
        z = out @ W1 + b1
        z = (z - bn_mean) * jax.lax.rsqrt(bn_var + EPS_BN) * bn_gamma + bn_beta
        z = jax.nn.relu(z)
        z = z @ W2 + b2
        return x + z

    def _L0_mix_ref(x, Wq, Wk, Wv, Wo, proj):
        import jax, jax.numpy as jnp
        import numpy as np
        DIM = 768
        HEADS = 12
        DH = DIM // HEADS
        M = 256
        EPS = 0.0001

        def softmax_kernel(data, proj, is_query):
            data_normalizer = data.shape[-1] ** (-0.25)
            ratio = proj.shape[0] ** (-0.5)
            data_dash = jnp.einsum('bhsd,md->bhsm', data_normalizer * data, proj)
            diag = 0.5 * data_normalizer ** 2 * jnp.sum(data * data, axis=-1, keepdims=True)
            if is_query:
                stab = jnp.max(data_dash, axis=-1, keepdims=True)
            else:
                stab = jnp.max(data_dash, axis=(-2, -1), keepdims=True)
            stab = jax.lax.stop_gradient(stab)
            return ratio * (jnp.exp(data_dash - diag - stab) + EPS)
        B, S, _ = x.shape

        def split_heads(t):
            return t.reshape(B, S, HEADS, DH).transpose(0, 2, 1, 3)
        q = split_heads(x @ Wq)
        k = split_heads(x @ Wk)
        v = split_heads(x @ Wv)
        qp = softmax_kernel(q, proj, is_query=True)
        kp = softmax_kernel(k, proj, is_query=False)
        k_sum = jnp.sum(kp, axis=2)
        d_inv = 1.0 / jnp.einsum('bhsm,bhm->bhs', qp, k_sum)
        ctx = jnp.einsum('bhsm,bhsd->bhmd', kp, v)
        out = jnp.einsum('bhsm,bhmd,bhs->bhsd', qp, ctx, d_inv)
        out = out.transpose(0, 2, 1, 3).reshape(B, S, DIM)
        return out @ Wo

    def _L0_ffn_ref(hidden_states, router_w, router_b, w1, w2, w3):
        import jax, jax.numpy as jnp
        import numpy as np
        S, B, DIM = (1024, 4, 768)
        N_EXPERTS = 8
        HID = 256
        s, b, h = hidden_states.shape
        route = jax.nn.softmax(hidden_states @ router_w + router_b, axis=2)
        max_prob = jnp.max(route, axis=2).reshape(-1, 1)
        max_ind = jnp.argmax(route, axis=2).reshape(-1)
        x = hidden_states.reshape(-1, h)
        out = jnp.zeros_like(x)
        for e in range(N_EXPERTS):
            mask = (max_ind == e)[:, None]
            xe = jnp.where(mask, x, 0.0)
            oe = jax.nn.silu(xe @ w1[e]) * (xe @ w2[e]) @ w3[e]
            out = out + jnp.where(mask, oe, 0.0)
        out = out.astype(jnp.bfloat16) * max_prob
        return out.reshape(s, b, h)
    edge_index = jnp.stack([src, dst])
    batch0 = jnp.zeros((1250,), jnp.int32)
    xn = _layernorm(x, axis=-1)
    x = x + _L0_gnn_ref(xn, edge_index, batch0, L0_gnn_t, L0_gnn_W1, L0_gnn_b1, L0_gnn_bn_gamma, L0_gnn_bn_beta, L0_gnn_bn_mean, L0_gnn_bn_var, L0_gnn_W2, L0_gnn_b2) + _L0_mix_ref(xn[None], L0_mix_Wq, L0_mix_Wk, L0_mix_Wv, L0_mix_Wo, L0_mix_proj)[0]
    x = x + _L0_ffn_ref(_layernorm(x, axis=-1)[None], L0_ffn_router_w, L0_ffn_router_b, L0_ffn_w1, L0_ffn_w2, L0_ffn_w3)[0]
    return x

_drawn_inputs = setup_inputs


def setup_inputs(seed=0):
    import zlib

    import numpy as np

    out = dict(_drawn_inputs(seed))
    spreads = {'L0_gnn_bn_gamma': (1.0, 0.2),
     'L0_gnn_bn_beta': (0.0, 0.41),
     'L0_gnn_bn_mean': (0.0, 0.382),
     'L0_gnn_bn_var': (1.0, 0.6),
     'L0_ffn_router_b': (0.0, 0.8)}
    factors = {'L0_gnn_b1': 8.0,
     'L0_gnn_b2': 7.981,
     'L0_mix_Wq': 8.0,
     'L0_mix_Wk': 8.0,
     'L0_mix_Wv': 3.879,
     'L0_mix_Wo': 4.174,
     'L0_mix_proj': 8.0,
     'L0_ffn_router_w': 8.0,
     'L0_ffn_w1': 8.0,
     'L0_ffn_w2': 8.0,
     'L0_ffn_w3': 8.0}
    for name, (base, spread) in spreads.items():
        noise = np.random.default_rng([zlib.crc32(name.encode()), seed]).standard_normal(out[name].shape)
        drawn = base * np.exp(spread * noise) if base else spread * noise
        out[name] = jnp.asarray(drawn.astype(out[name].dtype))
    for name, factor in factors.items():
        out[name] = (out[name] * factor).astype(out[name].dtype)
    return out
```

```python
import concourse.bass as bass
from concourse import mybir
from contextlib import ExitStack

F32, F32R = mybir.dt.float32, mybir.dt.float32r
BF16, FP16, I32 = mybir.dt.bfloat16, mybir.dt.float16, mybir.dt.int32
ALU = mybir.AluOpType
ACT = mybir.ActivationFunctionType
X_AXIS = mybir.AxisListType.X


class Chain:

    def __init__(self, eng, sem):
        self.eng, self.sem, self.start, self.n = eng, sem, 0, 0

    def at(self, start):
        self.start, self.n = start, 0

    def __call__(self, ins):
        self.n += 1
        ins.then_inc(self.sem, 1)
        self.eng.wait_ge(self.sem, self.start + self.n)


def build(nc, x, src, dst, t, W1, b1, gamma, beta, mean, var, W2, b2, Wq, Wk, Wv, Wo, proj,
          router_w, router_b, w1, w2, w3, out, debug=None):
    N, D = x.shape
    P = 125
    BLK = N // P
    PAIRS = BLK // 2
    K = D // 128
    M, DH = proj.shape
    HEADS = D // DH
    HP = HEADS // 2
    RATIO = M ** -0.5
    NORM = DH ** -0.25
    EPS = 1e-4
    BANKS = [(0, 512), (512, 1024), (1024, N)]
    E = src.shape[0]
    ET = 324
    EG = ET // 2
    ER, PADV = ET // 3, 5000
    HID = W1.shape[1]
    HC = HID // 128
    HALF = D // 2
    NE, _, FH = w1.shape
    FC = FH // 128
    SB = 17
    SLOTS = SB * 128
    SHIFT = 60.0
    assert ET * 128 >= E and SB == (N + NE * 127) // 128 and PADV > N
    assert N == P * BLK and BLK == 2 * PAIRS and D == 128 * K and M == 256 and DH == 64 and HEADS == 2 * K

    ctx = ExitStack()
    with ctx:
        def sem(name):
            return ctx.enter_context(nc.semaphore(name))

        def sems(name, n):
            return [sem(f"{name}{i}") for i in range(n)]

        ARENA = 212800
        arena = ctx.enter_context(nc.sbuf_tensor("arena", [128, ARENA], mybir.dt.uint8))
        base_off = nc.sbuf_base - ARENA

        def at(name, shape, dt, off):
            size = 2 if dt in (BF16, FP16) else 4
            for n in shape[1:]:
                size *= n
            assert off % 32 == 0 and off + size <= ARENA, (name, off, size)
            return nc.alloc_sbuf_tensor_at(name, shape, dt, offset=base_off + off)

        class Region:

            def __init__(self, start, end):
                self.at, self.end = start, end

            def __call__(self, name, shape, dt):
                size = 2 if dt in (BF16, FP16) else 4
                for n in shape[1:]:
                    size *= n
                place = at(name, shape, dt, self.at)
                self.at += -(-size // 32) * 32
                assert self.at <= self.end, (name, self.at, self.end)
                return place

        O_X = 15360
        O_T = O_X + 60032
        O_V = O_T + 30720
        O_C = O_V + 33024
        O_W = O_C + 60064
        const = Region(0, O_X)
        ident = const("ident", [128, 128], F32)
        ones = const("ones", [128, 128], F32)
        eps5 = const("eps5", [128, 1], F32)
        ind = const("ind", [128, 2], F32)
        stats = const("stats", [128, BLK, 12], F32)
        meanvar = const("meanvar", [128, BLK, 2], F32)
        stdev = const("stdev", [128, BLK], F32)
        rstd = const("rstd", [128, BLK], F32)
        kdiag = const("kdiag", [128, BLK, 2], F32)
        stab = const("stab", [128, 2], F32)
        km = const("km", [128, 2], F32)
        gmx = const("gmx", [128, 1], F32)
        dg = const("dg", [128, 2], F32)
        kbias = const("kbias", [128, 2, BLK], F32)
        qmx = const("qmx", [128, 2, 2], F32)
        qbias = const("qbias", [128, 2, 2], F32)
        rden = const("rden", [128, 2, 2], F32)
        qdiag = const("qdiag", [128, BLK, 2], F32)
        tri = const("tri", [128, 128], F32)
        dcol = const("dcol", [128, ET], F32)
        scol = const("scol", [128, ET], F32)
        iota = const("iota", [128, N], FP16)
        zeros = const("zeros", [128, 512], BF16)
        gidx = const("gidx", [16, EG, 2], F32)
        blo = const("blo", [16, 1], F32)
        tmm = const("tmm", [128, 2, 3], F32)
        emax = const("emax", [16, 2], F32)
        elim = const("elim", [16, 3], F32)
        limf = const("limf", [1, 32], F32)
        limi = const("limi", [1, 32], I32)
        bnr = const("bnr", [128, 128], F32)
        bnc = const("bnc", [128, 5, HC], F32)
        bns = const("bns", [128, 3, HC], F32)
        tb = const("tb", [128, 1], F32)
        gmax = const("gmax", [128, 1], F32)
        mrow = const("mrow", [1, 8], F32)
        mbias = const("mbias", [128, 1], F32)

        rw = const("rw", [128, K, NE], F32)
        rb = const("rb", [1, NE], F32)
        logit = const("logit", [128, BLK, NE], F32)
        prob = const("prob", [128, BLK], F32)
        best = const("best", [128, BLK], F32)
        pos = const("pos", [128, BLK], F32)
        quo = const("quo", [128, BLK], F32)
        k128 = const("k128", [128, SB], F32)
        upto = const("upto", [128, SB], F32)
        down = const("down", [128, NE], F32)
        nblk = const("nblk", [128, NE], F32)
        endb = const("endb", [128, NE], F32)
        tokid = const("tokid", [128, BLK], I32)
        idxt = const("idxt", [128, BLK], I32)
        idxy = const("idxy", [128, BLK], I32)
        tok = const("tok", [128, SB], I32)
        expf = const("expf", [1, SB], F32)
        expi = const("expi", [1, SB], I32)

        r_x = Region(O_X, O_T)
        XTh = r_x("XTh", [128, K, N], F32R)
        XTl = r_x("XTl", [128, K, N], F32R)
        attT = at("attT", [128, K, N], F32, O_T)
        r_c = Region(O_C, O_W)
        xin = r_c("xin", [128, BLK, D], F32)
        xn = r_c("xn", [128, 2, D], F32)
        b2row = r_c("b2row", [128, D], F32)
        res = r_c("res", [128, 2, D], F32)
        praw = r_c("praw", [128, 2, 128], F32)
        pscaled = r_c("pscaled", [128, 2 * M], F32)
        edi = r_c("edi", [128, 2, 3, 128], I32)
        edf = r_c("edf", [128, 2, 3, 128], F32)
        emask = r_c("emask", [16, 2, ET], F32)
        r_v = Region(O_V, O_C)
        wraw = r_v("wraw", [128, 3, K, 128], F32)
        wh = r_v("wh", [128, 3, K, 128], F32R)
        wl = r_v("wl", [128, 3, K, 128], F32R)
        V = r_v("V", [128, BLK, 2, DH + 1], F32)
        r_c = Region(O_C, O_W)
        KTh = r_c("KTh", [128, N], F32R)
        KTl = r_c("KTl", [128, N], F32R)
        QTh = r_c("QTh", [128, N], F32R)
        QTl = r_c("QTl", [128, N], F32R)
        VT = r_c("VT", [128, N], F32)
        sq = r_c("sq", [128, N], F32)
        kp = r_c("kp", [128, 2, BLK, M], F32)
        att = r_c("att", [128, BLK, 128], F32)
        r_w = Region(O_W, ARENA)
        qe = r_w("qe", [128, 2, 2, M], F32)
        qpT = r_w("qpT", [128, 2, 2, 2, P], F32)
        ctxs = r_w("ctxs", [128, 2, 2, DH + 1], F32)
        projh = r_w("projh", [128, 2 * M], F32R)
        projl = r_w("projl", [128, 2 * M], F32R)

        CT = at("CT", [128, BLK, N], F32R, O_C)
        crow = at("crow", [128, 2, N], F32, O_C + 50016)
        r_w = Region(O_W, ARENA)
        ohs = r_w("ohs", [128, 2, N], BF16)
        ohd = r_w("ohd", [128, 2, 128], BF16)
        r_v = Region(O_V, O_V + 3 * 9216)
        woh = r_v("woh", [128, K, HALF], F32R)
        wol = r_v("wol", [128, K, HALF], F32R)
        woraw = r_v("woraw", [128, K, HALF], F32)
        atth = at("atth", [128, 2, K, P], F32R, O_C + 50016)
        attl = at("attl", [128, 2, K, P], F32R, O_W)
        rtile = at("rtile", [128, 2, HALF], F32, O_W + 8192)

        r_t = Region(O_T, O_C)
        parts = [[r_t(f"{n}{u}", [128, BLK, 128], F32R) for n in ("Eh", "El", "Mh", "Ml")] for u in range(2)]
        Ef = r_t("Ef", [128, BLK, 128], F32)
        msg = r_t("msg", [128, 2, BLK, 128], F32)
        w1raw = r_t("w1raw", [128, 2, K, 128], F32)
        r_w = Region(O_W, ARENA)
        rec = r_w("rec", [128, N], F32)
        agg = r_w("agg", [128, N], F32)

        r_t = Region(O_T, O_T + 12288)
        w1h = r_t("w1h", [128, 2, K, 128], F32R)
        w1l = r_t("w1l", [128, 2, K, 128], F32R)
        HT = at("HT", [128, HC, N], F32, O_C)
        w2h = [at("w2h0", [128, HC, HALF], F32R, O_T + 12288), at("w2h1", [128, HC, HALF], F32R, O_X)]
        w2l = [at("w2l0", [128, HC, HALF], F32R, O_T + 30720), at("w2l1", [128, HC, HALF], F32R, O_X + 18432)]
        hth = [at("hth0", [128, HC, P], F32R, O_T + 49152), at("hth1", [128, HC, P], F32R, O_X + 36864)]
        htl = [at("htl0", [128, HC, P], F32R, O_T + 55168), at("htl1", [128, HC, P], F32R, O_X + 42880)]
        w2raw = at("w2raw", [128, 2, 3, HALF], F32, O_W)
        rtile2 = at("rtile2", [128, 2, HALF], F32, O_W + 9216)
        x1 = at("x1", [128, BLK, D], F32, O_T + 12288)
        xn2 = at("xn2", [128, 2, D], F32, O_T + 43008)
        r_x = Region(O_X + 49152, O_T)
        xn2T = r_x("xn2T", [128, 2, K, P], F32)
        stats2 = r_x("stats2", [128, BLK, 12], F32)
        mv2 = r_x("mv2", [128, BLK, 2], F32)
        sd2 = r_x("sd2", [128, BLK], F32)
        cmpk = r_x("cmpk", [128, BLK, 16], F32)
        cmpe = r_x("cmpe", [128, NE, BLK], F32)
        cmpb = r_x("cmpb", [1, SB, NE], F32)
        sume = r_x("sume", [128, BLK, NE], F32)
        onehot = r_x("onehot", [128, BLK, NE], F32)
        carry = r_x("carry", [128, BLK + 1, NE], F32)

        w12raw = [at("w12raw0", [128, K, 2 * FH], F32, O_X), None]
        w3raw = [at("w3raw0", [128, FC, D], F32, O_X + 12288), None]
        w12h = [at("w12h0", [128, K, 2 * FH], F32R, O_X + 18432), None]
        w12l = [at("w12l0", [128, K, 2 * FH], F32R, O_X + 30720), None]
        w3h = [at("w3h0", [128, FC, D], F32R, O_X + 43008), None]
        w3l = [at("w3l0", [128, FC, D], F32R, O_T), None]
        r_f = Region(O_T + 49152, ARENA)
        w12raw[1] = r_f("w12raw1", [128, K, 2 * FH], F32)
        w3raw[1] = r_f("w3raw1", [128, FC, D], F32)
        w12h[1] = r_f("w12h1", [128, K, 2 * FH], F32R)
        w12l[1] = r_f("w12l1", [128, K, 2 * FH], F32R)
        w3h[1] = r_f("w3h1", [128, FC, D], F32R)
        w3l[1] = r_f("w3l1", [128, FC, D], F32R)
        xg = r_f("xg", [128, 2, D], F32)
        xgh = r_f("xgh", [128, 2, K, 128], F32R)
        xgl = r_f("xgl", [128, 2, K, 128], F32R)
        gate = r_f("gate", [128, FH], F32)
        hid = r_f("hid", [128, FH], F32)
        hidh = r_f("hidh", [128, FC, 128], F32R)
        hidl = r_f("hidl", [128, FC, 128], F32R)
        yb = r_f("yb", [128, 2, D], BF16)
        yg = r_f("yg", [128, 2, D], BF16)

        PS = ctx.enter_context(nc.psum_tensor("PS", [128, 4096], F32))
        PA = PS[:, 0:1536]
        PB = PS[:, 1536:3072]

        def bank(i):
            return PS[:, 512 * i:512 * (i + 1)]

        xn_d = nc.dram_tensor("xn_scratch", (N, D), F32).ap()
        res_d = nc.dram_tensor("res_scratch", (N, D), F32).ap()

        def blocks(ap):
            return ap.rearrange("(b p) d -> p b d", p=P)

        x_b, xn_b, res_b = blocks(x), blocks(xn_d), blocks(res_d)

        tok_d = nc.dram_tensor("token_of_slot", (SLOTS, 1), I32).ap()
        xn2_d = nc.dram_tensor("xn2_scratch", (N, D), F32).ap()
        y_d = nc.dram_tensor("expert_out_scratch", (SLOTS, D), BF16).ap()

        def cols_by_k(w):
            return w.rearrange("(k p) n -> p k n", p=128)

        s_x = sems("s_x", PAIRS)
        s_cst = sem("s_cst")
        s_par = sem("s_par")
        s_pre = sem("s_pre")
        EDGE_COLS, BN_ROWS, EDGE_ROWS, LIMITS, PROJ_T, MAX_T, STAB = range(1, 8)
        s_prd = sem("s_prd")
        EDGE_F, EDGE_COL_D, EDGE_MM, EDGE_EL, BN_D, LIM_I, PROJ_D, GMAX_D, MROW_D, STAB_D = 1, 3, 5, 6, 7, 8, 9, 10, 11, 12
        s_var = sem("s_var")
        s_sd = sem("s_sd")
        s_xn = sem("s_xn")
        s_xt = sem("s_xt")
        s_xth = sem("s_xth")
        s_xtl = sem("s_xtl")
        s_res = sem("s_res")
        s_xst = sems("s_xst", 2)
        s_rst = sems("s_rst", 2)
        c_dve = sem("c_dve")
        c_pool = sem("c_pool")

        s_turn = sem("s_turn")
        s_wl = sem("s_wl")
        s_wsp = sem("s_wsp")
        s_wok = sem("s_wok")
        s_kps = sem("s_kps")
        s_kh = sem("s_kh")
        s_kl = sem("s_kl")
        s_vps = sem("s_vps")
        s_vt = sem("s_vt")
        s_qps = sem("s_qps")
        s_qh = sem("s_qh")
        s_ql = sem("s_ql")
        s_kd = sem("s_kd")
        s_kcp = sem("s_kcp")
        s_kdc = sem("s_kdc")
        s_kdg = sem("s_kdg")
        s_ksum = sem("s_ksum")
        s_kmT = sem("s_kmT")
        s_dg = sem("s_dg")
        s_stb = sem("s_stb")
        s_kb = sem("s_kb")
        s_ke = sem("s_ke")
        s_kp = sem("s_kp")
        s_vtp = sem("s_vtp")
        s_v = sem("s_v")
        s_cx = sem("s_cx")
        s_cxs = sem("s_cxs")
        s_qdg = sem("s_qdg")
        s_qd = sem("s_qd")
        s_qb = sem("s_qb")
        s_qe = sem("s_qe")
        s_qt = sem("s_qt")
        s_qp = sem("s_qp")
        s_o = sem("s_o")
        s_at = sem("s_at")
        s_aT = sem("s_aT")
        s_as = sem("s_as")
        s_out = sem("s_out")
        s_pad = sem("s_pad")
        s_e = sem("s_e")
        s_bnv = sem("s_bnv")
        s_oh = sems("s_oh", 2)
        s_ohf = sems("s_ohf", 2)
        s_cn = sem("s_cn")
        s_cr = sem("s_cr")
        s_ct = sem("s_ct")
        s_cs = sem("s_cs")
        s_wor = sem("s_wor")
        s_woh = sem("s_woh")
        s_wol = sem("s_wol")
        s_ath = sem("s_ath")
        s_atl = sem("s_atl")
        s_ow = sem("s_ow")
        s_rl = sems("s_rl", 2)
        s_ro = sem("s_ro")
        s_rs = sems("s_rs", 2)
        s_ml = sems("s_ml", 2)
        s_ms = sem("s_ms")
        s_ex = sem("s_ex")
        s_eh = sem("s_eh")
        s_mm = sem("s_mm")
        s_mh = sem("s_mh")
        s_ep = sem("s_ep")
        s_sum = sem("s_sum")
        s_sumr = sem("s_sumr")
        s_ag = sem("s_ag")
        s_agh = sem("s_agh")
        s_agl = sem("s_agl")
        s_w1r = sems("s_w1r", 2)
        s_w1h = sem("s_w1h")
        s_w1l = sem("s_w1l")
        s_z = sem("s_z")
        s_h = sem("s_h")
        s_w2r = sems("s_w2r", 2)
        s_w2h = sem("s_w2h")
        s_w2l = sem("s_w2l")
        s_hth = sem("s_hth")
        s_htl = sem("s_htl")
        s_o2 = sem("s_o2")
        s_r2l = sems("s_r2l", 2)
        s_r2 = sem("s_r2")
        s_r2s = sems("s_r2s", 2)
        s_x1l = sem("s_x1l")
        s_v2 = sem("s_v2")
        s_sd2 = sem("s_sd2")
        s_xn2 = sem("s_xn2")
        s_xn2s = sems("s_xn2s", 2)
        s_x2t = sem("s_x2t")
        s_x2s = sem("s_x2s")
        s_rw = sem("s_rw")
        s_lg = sem("s_lg")
        s_lgs = sem("s_lgs")
        s_se = sem("s_se")
        s_route = sem("s_route")
        SHIFTED, ONE_HOT, EXPERTS, SLOTS_D = range(1, 5)
        s_rk = sem("s_rk")
        s_ts = sem("s_ts")
        s_tl = sem("s_tl")
        s_fr = sems("s_fr", 2)
        s_frf = sems("s_frf", 2)
        s_fh = sem("s_fh")
        s_fl = sem("s_fl")
        s_f3h = sem("s_f3h")
        s_f3 = sem("s_f3")
        s_g = sems("s_g", 2)
        s_gt = sem("s_gt")
        s_gh = sem("s_gh")
        s_gl = sem("s_gl")
        s_up = sem("s_up")
        s_sg = sem("s_sg")
        s_hd = sem("s_hd")
        s_ht = sem("s_ht")
        s_hh = sem("s_hh")
        s_hl = sem("s_hl")
        s_y = sem("s_y")
        s_yb = sem("s_yb")
        s_ys = sems("s_ys", 2)
        s_yg = sems("s_yg", 2)
        s_fin = sem("s_fin")

        block = ctx.enter_context(nc.Block())

        @block.sync
        def _(sp):
            for i in range(PAIRS):
                sp.dma_start(xin[0:112, 2 * i:2 * i + 2, :], x_b[0:112, 2 * i:2 * i + 2, :]).then_inc(s_x[i], 16)
                sp.dma_start(xin[112:P, 2 * i:2 * i + 2, :], x_b[112:P, 2 * i:2 * i + 2, :]).then_inc(s_x[i], 16)
            sp.wait_ge(s_pad, 1)
            for i, e in enumerate((dst, src)):
                full = E // 128 - 2 * ER
                sp.dma_start(edi[0:ER, i, 0:2], e[0:2 * ER * 128].rearrange("(g r e) -> r g e", g=2, r=ER)).then_inc(s_e, 16)
                sp.dma_start(edi[0:full, i, 2], e[2 * ER * 128:E // 128 * 128].rearrange("(r e) -> r e", e=128)).then_inc(s_e, 16)
                sp.dma_start(edi[full:full + 1, i, 2, 0:E % 128], e[E // 128 * 128:E].rearrange("(a e) -> a e", a=1)).then_inc(s_e, 16)

            def load_w2(i):
                if i >= 2:
                    sp.wait_ge(s_w2l, i - 1)
                sp.dma_start(w2raw[:, i % 2], cols_by_k(W2)[:, 3 * (i % 4):3 * (i % 4) + 3, HALF * (i // 4):HALF * (i // 4) + HALF])\
                    .then_inc(s_w2r[i % 2], 16)

            with sp.Fori(0, HP) as j:
                sp.wait_ge(s_wsp, j + 1)
                for n, w in enumerate((Wk, Wv, Wq)):
                    sp.dma_start(wraw[:, n], cols_by_k(w)[:, :, bass.ds(j * 128, 128)]).then_inc(s_wl, 16)
            sp.wait_ge(s_cst, 16)
            sp.dma_start(tok_d.rearrange("(p b) o -> p (b o)", b=SB), zeros[:, 0:2 * SB].bitcast(I32)).then_inc(s_rw, 16)
            sp.dma_start(rw[:], router_w.rearrange("(k p) e -> p k e", p=128)).then_inc(s_rw, 16)
            sp.dma_start(rb[:], router_b.rearrange("(a e) -> a e", a=1)).then_inc(s_rw, 16)
            for i in range(2):
                sp.wait_ge(s_rst[i], 32 * PAIRS)
            sp.wait_ge(s_qps, HP + 1)
            sp.dma_start(woraw[:], cols_by_k(Wo)[:, :, 0:HALF]).then_inc(s_wor, 16)

            def residual(n, tile, landed, stored):
                if n < 2 * BLK:
                    h, b = n // BLK, n % BLK
                    if n >= 2:
                        sp.wait_ge(stored[n % 2], 16 * (n // 2))
                    sp.dma_start(tile[0:P, n % 2], res_b[:, b, HALF * h:HALF * h + HALF]).then_inc(landed[n % 2], 16)

            sp.wait_ge(s_cn, BLK)
            residual(0, rtile, s_rl, s_rs)
            for n in range(2 * BLK):
                h, b = n // BLK, n % BLK
                if n == 1:
                    sp.wait_ge(s_wol, 1)
                    sp.dma_start(woraw[:], cols_by_k(Wo)[:, :, HALF:D]).then_inc(s_wor, 16)
                residual(n + 1, rtile, s_rl, s_rs)
                sp.wait_ge(s_ro, n + 1)
                sp.dma_start(res_b[:, b, HALF * h:HALF * h + HALF], rtile[0:P, n % 2]).then_inc(s_rs[n % 2], 16)
            for i in range(2):
                sp.wait_ge(s_xst[i], 32 * PAIRS)
            for c in range(K):
                if c >= 2:
                    sp.wait_ge(s_ep, c - 1)
                sp.dma_start(msg[0:P, c % 2], xn_b[:, :, 128 * c:128 * c + 128]).then_inc(s_ml[c % 2], 16)
                if c < 2:
                    sp.dma_start(w1raw[:, c], cols_by_k(W1)[:, :, 128 * c:128 * c + 128]).then_inc(s_w1r[c], 16)
            for m in range(2, HC):
                sp.wait_ge(s_w1l, m - 1)
                sp.dma_start(w1raw[:, m % 2], cols_by_k(W1)[:, :, 128 * m:128 * m + 128]).then_inc(s_w1r[m % 2], 16)
                if m == 4:
                    for i in range(2):
                        load_w2(i)
                if 5 <= m < 7:
                    load_w2(m - 3)
            for i in range(2):
                sp.wait_ge(s_rs[i], 16 * BLK)
            for i in range(4, 6):
                load_w2(i)

            def store_norm2(b):
                sp.wait_ge(s_xn2, b + 1)
                sp.dma_start(blocks(xn2_d)[:, b], xn2[0:P, b % 2]).then_inc(s_xn2s[b % 2], 16)

            residual(0, rtile2, s_r2l, s_r2s)
            for n in range(2 * BLK):
                h, b = n // BLK, n % BLK
                if n in (1, 2):
                    load_w2(n + 5)
                if h == 0:
                    residual(n + 1, rtile2, s_r2l, s_r2s)
                elif n + 1 < 2 * BLK:
                    sp.wait_ge(s_r2, n)
                    sp.dma_start(rtile2[0:P, (n + 1) % 2], res_b[:, b + 1, HALF:D]).then_inc(s_r2l[(n + 1) % 2], 16)
                if n >= BLK + 2:
                    store_norm2(n - BLK - 2)
                if h == 0:
                    sp.wait_ge(s_r2, n + 1)
                    sp.dma_start(res_b[:, b, 0:HALF], rtile2[0:P, n % 2]).then_inc(s_r2s[n % 2], 16)
                if n == BLK:
                    for i in range(2):
                        sp.wait_ge(s_r2s[i], 16 * (BLK // 2))
                    sp.wait_ge(s_o2, BLK)
                    sp.dma_start(x1[0:P, :, 0:HALF], res_b[:, :, 0:HALF]).then_inc(s_x1l, 16)
            for b in range(BLK - 2, BLK):
                store_norm2(b)
            for i in range(2):
                sp.sem_inc(s_frf[i], 1)
            sp.wait_ge(s_route, EXPERTS)

            def load_expert(n, u, i):
                e = nc.sync.value_load(expi[0:1, bass.ds(n, 1)], min_val=0, max_val=NE - 1)
                sp.wait_ge(s_frf[u], i + 1)
                sp.dma_start(w12raw[u][:, :, 0:FH], w1[bass.ds(e, 1)].rearrange("a (k p) h -> p (a k) h", p=128)).then_inc(s_fr[u], 16)
                sp.dma_start(w12raw[u][:, :, FH:2 * FH], w2[bass.ds(e, 1)].rearrange("a (k p) h -> p (a k) h", p=128)).then_inc(s_fr[u], 16)
                sp.dma_start(w3raw[u][:], w3[bass.ds(e, 1)].rearrange("a (k p) h -> p (a k) h", p=128)).then_inc(s_fr[u], 16)

            with sp.Fori(0, SB // 2) as i:
                for u in range(2):
                    load_expert(i * 2 + u, u, i)
            load_expert(SB - 1, 0, SB // 2)
            for b in range(BLK):
                sp.wait_ge(s_fin, b + 1)
                sp.dma_start(blocks(out)[0:112, b], x1[0:112, b]).then_inc(s_out, 16)
                sp.dma_start(blocks(out)[112:P, b], x1[112:P, b]).then_inc(s_out, 16)
            sp.wait_ge(s_out, 32 * BLK)
            if debug == "count":
                sp.wait_ge(s_cs, 30)
                sp.dma_start(blocks(out), CT[0:P, :, 482:1250].bitcast(F32)).then_inc(s_out, 16)
                sp.wait_ge(s_out, 16)
            if debug == "att":
                sp.wait_ge(s_as, HP * BLK)
                sp.dma_start(out[0:128 * 9, :].rearrange("(k p) n -> p k n", p=128)[:, 0:6, :], attT[:, :, 0:768]).then_inc(s_out, 16)
                sp.wait_ge(s_out, 16)

        @block.gpsimd
        def _(pool):
            chain = Chain(pool, c_pool)
            nc.gpsimd.memset(ident[:], 0.0).then_inc(c_pool, 1)
            nc.gpsimd.memset(ones[:], 1.0).then_inc(c_pool, 1)
            nc.gpsimd.iota(iota[:], [[1, N]], base=0, channel_multiplier=0, allow_small_or_imprecise_dtypes=True).then_inc(s_cst, 1)
            nc.gpsimd.iota(gidx[:], [[1, EG], [0, 2]], base=0, channel_multiplier=0, allow_small_or_imprecise_dtypes=True).then_inc(s_cst, 1)
            nc.gpsimd.iota(blo[:], [[0, 1]], base=0, channel_multiplier=P, allow_small_or_imprecise_dtypes=True).then_inc(s_cst, 1)
            nc.gpsimd.memset(zeros[:], 0.0).then_inc(s_cst, 1)
            nc.gpsimd.iota(k128[:], [[128, SB]], base=0, channel_multiplier=0, allow_small_or_imprecise_dtypes=True).then_inc(s_cst, 1)
            nc.gpsimd.iota(upto[:], [[1, SB]], base=0, channel_multiplier=0, allow_small_or_imprecise_dtypes=True).then_inc(s_cst, 1)
            nc.gpsimd.iota(down[:], [[-1, NE]], base=NE, channel_multiplier=0, allow_small_or_imprecise_dtypes=True).then_inc(s_cst, 1)
            nc.gpsimd.iota(tokid[:], [[P, BLK]], base=0, channel_multiplier=1).then_inc(s_cst, 1)
            nc.gpsimd.memset(eps5[:], 1e-5).then_inc(s_cst, 1)
            nc.gpsimd.memset(V[:, :, :, DH:DH + 1], 1.0).then_inc(s_cst, 1)
            pool.wait_ge(c_pool, 2)
            nc.gpsimd.affine_select(out=ident[:], in_=ident[:], compare_op=ALU.not_equal, fill=1.0, base=0,
                                    pattern=[[-1, 128]], channel_multiplier=1).then_inc(s_cst, 1)
            nc.gpsimd.affine_select(out=tri[:], in_=ones[:], compare_op=ALU.is_gt, fill=0.0, base=0,
                                    pattern=[[1, 128]], channel_multiplier=-1).then_inc(s_cst, 1)
            pool.wait_ge(s_par, 144)
            chain.at(2)
            for b in range(BLK):
                pool.wait_ge(s_xn, b + 1)
                if b >= 2:
                    pool.wait_ge(s_rst[b % 2], 32 * (b // 2))
                chain(nc.gpsimd.tensor_tensor(res[0:P, b % 2], xin[0:P, b], xn[0:P, b % 2], ALU.add))
                nc.gpsimd.tensor_tensor(res[0:P, b % 2], res[0:P, b % 2], b2row[0:P, :], ALU.add).then_inc(s_res, 1)
            pool.sem_inc(s_wsp, 1)
            with pool.Fori(0, HP) as j:
                pool.wait_ge(s_wl, 48 * j + 48)
                pool.wait_ge(s_qps, j + 1)
                pool.sem_inc(s_turn, 1)
                chain.at(2 + BLK + j)
                chain(nc.gpsimd.tensor_copy(wh[:], wraw[:]))
                nc.gpsimd.tensor_tensor(wl[:], wraw[:], wh[:].bitcast(F32), ALU.subtract).then_inc(s_wok, 1)
                pool.wait_ge(s_wok, j + 1)
                pool.sem_inc(s_wsp, 1)
            pool.wait_ge(s_wor, 16)
            nc.gpsimd.tensor_copy(woh[:], woraw[:]).then_inc(s_woh, 1)
            pool.wait_ge(s_woh, 1)
            nc.gpsimd.tensor_tensor(wol[:], woraw[:], woh[:].bitcast(F32), ALU.subtract).then_inc(s_wol, 1)
            pool.wait_ge(s_rw, 48)
            pool.wait_ge(s_route, SLOTS_D)
            for b in range(BLK):
                nc.gpsimd.indirect_dma_start(out=tok_d, out_offset=bass.IndirectOffsetOnAxis(ap=idxt[0:P, b:b + 1], axis=0),
                                             in_=tokid[0:P, b:b + 1], in_offset=None).then_inc(s_ts, 16)
            pool.wait_ge(s_ts, 16 * BLK)
            pool.dma_start(tok[:], tok_d.rearrange("(p b) o -> p (b o)", b=SB)).then_inc(s_tl, 16)
            for i in range(2):
                pool.wait_ge(s_xn2s[i], 16 * PAIRS)
            pool.wait_ge(s_tl, 16)

            def gather(n):
                if n < SB:
                    if n >= 2:
                        pool.wait_ge(s_gt, n - 1)
                    nc.gpsimd.indirect_dma_start(out=xg[:, n % 2, :], out_offset=None, in_=xn2_d,
                                                 in_offset=bass.IndirectOffsetOnAxis(ap=tok[:, n:n + 1], axis=0)).then_inc(s_g[n % 2], 16)

            gather(0)
            for n in range(SB):
                u = n % 2
                gather(n + 1)
                pool.wait_ge(s_fr[u], 48 * (n // 2 + 1))
                if n >= 2:
                    pool.wait_ge(s_y, n + 1)
                nc.gpsimd.tensor_copy(w3h[u][:], w3raw[u][:]).then_inc(s_f3h, 1)
                pool.wait_ge(s_f3h, n + 1)
                nc.gpsimd.tensor_tensor(w3l[u][:], w3raw[u][:], w3h[u][:].bitcast(F32), ALU.subtract).then_inc(s_f3, 1)
            for i in range(2):
                pool.wait_ge(s_ys[i], 16 * (SB // 2 + 2 - i))
            for b in range(BLK):
                if b >= 2:
                    pool.wait_ge(s_fin, b - 1)
                nc.gpsimd.indirect_dma_start(out=yg[0:P, b % 2, :], out_offset=None, in_=y_d,
                                             in_offset=bass.IndirectOffsetOnAxis(ap=idxy[0:P, b:b + 1], axis=0)).then_inc(s_yg[b % 2], 16)

        @block.scalar
        def _(act):
            act.dma_start(b2row[0:P, :], b2.rearrange("(a n) -> a n", a=1).to_broadcast([P, D])).then_inc(s_par, 16)
            for dup in range(2):
                act.dma_start(praw[:, :, 64 * dup:64 * dup + 64], proj.rearrange("(c p) d -> p c d", p=128)).then_inc(s_par, 16)
            for i, row in enumerate((gamma, beta, mean, var, b1)):
                act.dma_start(bnr[HC * i:HC * i + HC, :], row.rearrange("(a n) -> a n", n=128)).then_inc(s_par, 16)
            act.dma_start(tb[:], t.rearrange("(a n) -> a n", a=1).to_broadcast([128, 1])).then_inc(s_par, 16)
            act.wait_ge(s_cst, 16)

            def deviation(h):
                act.wait_ge(s_var, PAIRS * (h + 1))
                nc.scalar.activation(stdev[0:P, PAIRS * h:PAIRS * (h + 1)], meanvar[0:P, PAIRS * h:PAIRS * (h + 1), 1],
                                     ACT.Sqrt, bias=eps5[0:P, :]).then_inc(s_sd, 1)

            def store(b):
                act.wait_ge(s_xn, b + 1)
                act.dma_start(xn_b[0:112, b], xn[0:112, b % 2]).then_inc(s_xst[b % 2], 16)
                act.dma_start(xn_b[112:P, b], xn[112:P, b % 2]).then_inc(s_xst[b % 2], 16)

            def store_res(b):
                act.wait_ge(s_res, b + 1)
                act.dma_start(res_b[0:112, b], res[0:112, b % 2]).then_inc(s_rst[b % 2], 16)
                act.dma_start(res_b[112:P, b], res[112:P, b % 2]).then_inc(s_rst[b % 2], 16)

            deviation(0)
            for b in range(BLK):
                if b == PAIRS:
                    deviation(1)
                    act.wait_ge(s_pre, BN_ROWS)
                    nc.scalar.activation(bns[:, 0, :], bank(7)[:, 3 * HC:4 * HC], ACT.Sqrt, bias=eps5[:]).then_inc(s_bnv, 1)
                store(b)
                for i in range(2):
                    act.wait_ge(s_xt, 2 * b + i + 1)
                    nc.scalar.activation(XTh[:, 3 * i:3 * i + 3, P * b:P * b + P],
                                         bank(2 * (b % 2) + i)[:, 0:375].rearrange("p (k n) -> p k n", k=3),
                                         ACT.Copy).then_inc(s_xth, 1)
                if b >= 1:
                    store_res(b - 1)
            store_res(BLK - 1)
            for i in range(2):
                act.wait_ge(s_xst[i], 32 * PAIRS)
                act.wait_ge(s_rst[i], 32 * PAIRS)

            def norm2(b):
                act.wait_ge(s_v2, b + 1)
                nc.scalar.activation(sd2[0:P, b:b + 1], mv2[0:P, b, 1:2], ACT.Sqrt, bias=eps5[0:P, :]).then_inc(s_sd2, 1)
                act.wait_ge(s_x2t, b + 1)
                if b >= 2:
                    act.wait_ge(s_lg, b - 1)
                for c in range(2):
                    ins = nc.scalar.activation(xn2T[:, b % 2, 3 * c:3 * c + 3], bank(2 + c)[:, 0:375].rearrange("p (k n) -> p k n", k=3),
                                               ACT.Copy)
                ins.then_inc(s_x2s, 1)

            with act.Fori(0, HP) as j:
                act.wait_ge(s_kps, j + 1)
                for c0, c1 in BANKS:
                    nc.scalar.activation(KTh[:, c0:c1], PB[:, c0:c1], ACT.Copy)
                    nc.scalar.activation(sq[:, c0:c1], PB[:, c0:c1], ACT.Square).then_inc(s_kh, 1)
                act.wait_ge(s_vps, j + 1)
                nc.scalar.activation(VT[:], PA[:, 0:N], ACT.Copy).then_inc(s_vt, 1)
                for b in range(BLK):
                    act.wait_ge(s_kd, BLK * j + b + 1)
                    nc.scalar.activation(kp[0:P, :, b, :], bank(6 + b % 2)[0:P, :].rearrange("p (a m) -> p a m", a=2),
                                         ACT.Copy).then_inc(s_kcp, 1)
                act.wait_ge(s_kdg, j + 1)
                act.wait_ge(s_qps, j + 2)
                for c0, c1 in BANKS:
                    nc.scalar.activation(QTh[:, c0:c1], PB[:, c0:c1], ACT.Copy)
                    nc.scalar.activation(sq[:, c0:c1], PB[:, c0:c1], ACT.Square).then_inc(s_qh, 1)
                act.wait_ge(s_vtp, j + 1)
                nc.scalar.activation(V[0:P, 0:8, :, 0:DH], PA[0:P, 0:1024].rearrange("p (b a d) -> p b a d", b=8, a=2),
                                     ACT.Copy)
                nc.scalar.activation(V[0:P, 8:BLK, :, 0:DH], PA[0:P, 1024:1280].rearrange("p (b a d) -> p b a d", b=2, a=2),
                                     ACT.Copy).then_inc(s_v, 1)
                act.wait_ge(s_kb, j + 1)
                for a in range(2):
                    for b in range(BLK):
                        ins = nc.scalar.activation(kp[0:P, a, b, :], kp[0:P, a, b, :], ACT.Exp, bias=kbias[0:P, a, b:b + 1])
                    ins.then_inc(s_ke, 1)
                act.wait_ge(s_cx, j + 1)
                nc.scalar.activation(ctxs[:], bank(3)[:, 0:260].rearrange("p (a c d) -> p a c d", a=2, c=2),
                                     ACT.Copy).then_inc(s_cxs, 1)

                def put_attT(b):
                    act.wait_ge(s_aT, BLK * j + b + 1)
                    nc.scalar.activation(attT[:, bass.ds(j, 1), P * b:P * b + P],
                                         bank(4 + b % 2)[:, 0:P].rearrange("p (a n) -> p a n", a=1),
                                         ACT.Copy).then_inc(s_as, 1)

                for u in range(BLK):
                    act.wait_ge(s_qb, BLK * j + u + 1)
                    if u >= 2:
                        act.wait_ge(s_qt, BLK * j + u - 1)
                    for a in range(2):
                        ins = nc.scalar.activation(qe[0:P, u % 2, a, :], bank(6 + u % 2)[0:P, M * a:M * a + M],
                                                   ACT.Exp, bias=qbias[0:P, u % 2, a:a + 1])
                    ins.then_inc(s_qe, 1)
                    if u >= 4:
                        put_attT(u - 4)
                for b in range(BLK - 4, BLK):
                    put_attT(b)

            def put_counts(b):
                for i in range(3):
                    n = min(4, BLK - 4 * i)
                    act.wait_ge(s_ct, 3 * b + i + 1)
                    nc.scalar.activation(CT[0:P, 4 * i:4 * i + n, P * b:P * b + P],
                                         bank(6 + (3 * b + i) % 2)[0:P, 0:P * n].rearrange("p (s n) -> p s n", s=n),
                                         ACT.Copy).then_inc(s_cs, 1)

            for b in range(BLK):
                act.wait_ge(s_cn, b + 1)
                if b >= 2:
                    act.wait_ge(s_ct, 3 * (b - 1))
                nc.scalar.activation(crow[0:P, b % 2, :], PS[0:P, 1536 * (b % 2):1536 * (b % 2) + N], ACT.Copy).then_inc(s_cr, 1)
                if b >= 1:
                    put_counts(b - 1)
            put_counts(BLK - 1)
            for n in range(2 * BLK):
                b = n % BLK
                if n == BLK:
                    act.wait_ge(s_wor, 32)
                    act.wait_ge(s_ow, BLK)
                    nc.scalar.activation(woh[:], woraw[:], ACT.Copy).then_inc(s_woh, 1)
                if n >= 2:
                    act.wait_ge(s_ow, n - 1)
                nc.scalar.activation(atth[:, n % 2], attT[:, :, P * b:P * b + P], ACT.Copy).then_inc(s_ath, 1)

            def exponentials(c):
                if c >= K:
                    return
                u = c % 2
                act.wait_ge(s_ms, c + 1)
                if c >= 1:
                    act.wait_ge(s_ep, c)
                nc.scalar.activation(Ef[0:P], msg[0:P, u], ACT.Exp, bias=mbias[0:P, :], scale=tb[0:P, :]).then_inc(s_ex, 1)
                if c >= 2:
                    act.wait_ge(s_sum, 2 * (c - 1))
                act.wait_ge(s_ex, c + 1)
                nc.scalar.activation(parts[u][0][0:P], Ef[0:P], ACT.Copy).then_inc(s_eh, 1)
                act.wait_ge(s_mm, c + 1)
                nc.scalar.activation(parts[u][2][0:P], msg[0:P, u], ACT.Copy).then_inc(s_mh, 1)

            act.wait_ge(s_prd, STAB_D)
            exponentials(0)
            for c in range(K):
                exponentials(c + 1)
                act.wait_ge(s_ag, c + 1)
                nc.scalar.activation(XTh[:, c, :], agg[:], ACT.Copy).then_inc(s_agh, 1)

            def w1_parts(m):
                if m < HC:
                    act.wait_ge(s_w1r[m % 2], 16 * (m // 2 + 1))
                    if m < 2:
                        act.wait_ge(s_sum, 2 * (K - 1))
                    else:
                        act.wait_ge(s_z, m - 1)
                    nc.scalar.activation(w1h[:, m % 2], w1raw[:, m % 2], ACT.Copy).then_inc(s_w1h, 1)

            def w2_parts(i):
                act.wait_ge(s_w2r[i % 2], 16 * (i // 2 + 1))
                nc.scalar.activation(w2h[i // 4][:, 3 * (i % 4):3 * (i % 4) + 3, :], w2raw[:, i % 2], ACT.Copy).then_inc(s_w2h, 1)

            w1_parts(0)
            for m in range(HC):
                w1_parts(m + 1)
                act.wait_ge(s_z, m + 1)
                nc.scalar.activation(HT[:, m, :], PS[:, 1536 * (m % 2):1536 * (m % 2) + N], ACT.Relu,
                                     bias=bns[:, 2, m:m + 1], scale=bns[:, 1, m:m + 1]).then_inc(s_h, 1)
                if 4 <= m < 8:
                    w2_parts(m - 4)

            def hidden_parts(n):
                if n < 2 * BLK:
                    b = n % BLK
                    if n >= 2:
                        act.wait_ge(s_o2, n - 1)
                    nc.scalar.activation(hth[n % 2][:], HT[:, :, P * b:P * b + P], ACT.Copy).then_inc(s_hth, 1)

            act.wait_ge(s_h, HC)
            hidden_parts(0)
            hidden_parts(1)
            for i in range(4, 8):
                w2_parts(i)
                hidden_parts(i - 2)
            for n in range(6, 2 * BLK):
                hidden_parts(n)
                if n >= BLK + 2:
                    norm2(n - BLK - 2)
            norm2(BLK - 2)
            norm2(BLK - 1)
            act.wait_ge(s_route, SHIFTED)
            nc.scalar.activation(sume[0:P], sume[0:P], ACT.Exp).then_inc(s_se, 1)

            def expert_parts(n, u, i):
                act.wait_ge(s_fr[u], i * 48 + 48)
                act.wait_ge(s_y, n + 1)
                nc.scalar.activation(w12h[u][:], w12raw[u][:], ACT.Copy).then_inc(s_fh, 1)

            def rows_parts(n, u):
                act.wait_ge(s_gt, n + 1)
                act.wait_ge(s_up, n + 1)
                for c in range(2):
                    ins = nc.scalar.activation(xgh[:, u, 3 * c:3 * c + 3], bank(c)[:, 0:384].rearrange("p (k n) -> p k n", k=3), ACT.Copy)
                ins.then_inc(s_gh, 1)

            def expert(n, u):
                act.wait_ge(s_up, n + 3)
                nc.scalar.activation(gate[:], bank(2)[:, 0:FH], ACT.Silu).then_inc(s_sg, 1)

            def expert_hidden(n, u):
                act.wait_ge(s_ht, n + 1)
                act.wait_ge(s_y, n + 2)
                nc.scalar.activation(hidh[:], bank(3)[:, 0:FH].rearrange("p (k n) -> p k n", k=FC), ACT.Copy).then_inc(s_hh, 1)

            def expert_out(n, u, i):
                act.wait_ge(s_y, n + 3)
                act.wait_ge(s_ys[u], i * 16 + 16)
                for c in range(2):
                    ins = nc.scalar.activation(yb[:, u, HALF * c:HALF * c + HALF], bank(4 + c)[:, 0:HALF], ACT.Copy)
                ins.then_inc(s_yb, 1)
                act.wait_ge(s_yb, n + 1)
                act.dma_start(y_d.rearrange("(b p) d -> p b d", p=128)[:, bass.ds(n, 1), :], yb[:, u:u + 1, :]).then_inc(s_ys[u], 16)

            for i in range(2):
                act.sem_inc(s_ys[i], 16)

            def expert_turn(n, u, i, last=False):
                expert(n, u)
                expert_out(n - 1, 1 - u, i if u else i - 1)
                expert_hidden(n, u)
                if not last:
                    rows_parts(n + 1, 1 - u)
                    expert_parts(n + 1, 1 - u, i + 1 if u else i)

            rows_parts(0, 0)
            expert_parts(0, 0, 0)
            expert(0, 0)
            expert_hidden(0, 0)
            rows_parts(1, 1)
            expert_parts(1, 1, 0)
            expert_turn(1, 1, 0)
            with act.Fori(1, SB // 2) as i:
                for u in range(2):
                    expert_turn(i * 2 + u, u, i)
            expert_turn(SB - 1, 0, SB // 2, last=True)
            expert_out(SB - 1, 0, SB // 2)

        @block.vector
        def _(dve):
            chain = Chain(dve, c_dve)
            for a in range(2):
                for c in range(2):
                    nc.vector.memset(ind[64 * a:64 * a + 64, c:c + 1], 0.5 * NORM * NORM if a == c else 0.0).then_inc(s_cst, 1)

            nc.vector.memset(edi[:], PADV).then_inc(s_pad, 1)

            def edges_to_float():
                dve.wait_ge(s_e, 96)
                nc.vector.tensor_copy(edf[0:ER], edi[0:ER]).then_inc(s_prd, 1)

            def edge_columns():
                dve.wait_ge(s_pre, EDGE_COLS)
                for i in range(2):
                    nc.vector.tensor_copy((dcol, scol)[i][:], bank(4 + i)[:, 0:ET]).then_inc(s_prd, 1)
                nc.vector.tensor_reduce(tmm[0:ER, 0, :], edf[0:ER, 0], X_AXIS, ALU.min).then_inc(s_prd, 1)
                nc.vector.tensor_reduce(tmm[0:ER, 1, :], edf[0:ER, 0], X_AXIS, ALU.max).then_inc(s_prd, 1)

            def edge_ranges():
                dve.wait_ge(s_pre, EDGE_ROWS)
                chain(nc.vector.tensor_scalar(emask[0:BLK, 0], bank(5)[0:BLK, 0:ET], blo[0:BLK], None, ALU.is_ge))
                chain(nc.vector.tensor_scalar(emask[0:BLK, 1], bank(4)[0:BLK, 0:ET], blo[0:BLK], float(P), ALU.subtract, ALU.is_lt))
                chain(nc.vector.tensor_tensor(emask[0:BLK, 0], emask[0:BLK, 0], emask[0:BLK, 1], ALU.mult))
                g = gidx[0:BLK].rearrange("p g t -> p (g t)")
                chain(nc.vector.scalar_tensor_tensor(out=emask[0:BLK, 1], in0=g, scalar=1.0, in1=emask[0:BLK, 0],
                                                     op0=ALU.add, op1=ALU.mult))
                chain(nc.vector.reduce_max(emax[0:BLK, 0:1], emask[0:BLK, 1], X_AXIS))
                chain(nc.vector.tensor_scalar(emask[0:BLK, 1], g, -1.0, float(EG), ALU.mult, ALU.add))
                chain(nc.vector.tensor_tensor(emask[0:BLK, 1], emask[0:BLK, 1], emask[0:BLK, 0], ALU.mult))
                chain(nc.vector.reduce_max(emax[0:BLK, 1:2], emask[0:BLK, 1], X_AXIS))
                chain(nc.vector.tensor_scalar(elim[0:BLK, 1:2], emax[0:BLK, 0:1], 1.0, None, ALU.max))
                chain(nc.vector.tensor_scalar(elim[0:BLK, 0:1], emax[0:BLK, 1:2], -1.0, float(EG), ALU.mult, ALU.add))
                chain(nc.vector.tensor_scalar(elim[0:BLK, 2:3], elim[0:BLK, 1:2], -1.0, None, ALU.add))
                chain(nc.vector.tensor_tensor(elim[0:BLK, 0:1], elim[0:BLK, 0:1], elim[0:BLK, 2:3], ALU.min))
                nc.vector.tensor_tensor(elim[0:BLK, 2:3], elim[0:BLK, 1:2], elim[0:BLK, 0:1], ALU.subtract).then_inc(s_prd, 1)

            def edge_limits():
                dve.wait_ge(s_pre, LIMITS)
                chain(nc.vector.tensor_copy(limf[0:1, 0:30], bank(7)[0:1, 64:94]))
                chain(nc.vector.tensor_tensor(limf[0:1, 20:30], limf[0:1, 20:30], limf[0:1, 0:10], ALU.subtract))
                nc.vector.tensor_copy(limi[0:1, 0:30], limf[0:1, 0:30]).then_inc(s_prd, 1)

            def batch_norm():
                dve.wait_ge(s_bnv, 1)
                chain(nc.vector.tensor_copy(bnc[:], bank(7)[:, 0:5 * HC].rearrange("p (a c) -> p a c", a=5)))
                chain(nc.vector.reciprocal(bns[:, 0, :], bns[:, 0, :]))
                chain(nc.vector.tensor_tensor(bns[:, 1, :], bns[:, 0, :], bnc[:, 0, :], ALU.mult))
                chain(nc.vector.tensor_tensor(bnc[:, 4, :], bnc[:, 4, :], bnc[:, 2, :], ALU.subtract))
                chain(nc.vector.tensor_tensor(bnc[:, 4, :], bnc[:, 4, :], bns[:, 1, :], ALU.mult))
                nc.vector.tensor_tensor(bns[:, 2, :], bnc[:, 4, :], bnc[:, 1, :], ALU.add).then_inc(s_prd, 1)

            def normalise(b):
                if b >= 2:
                    dve.wait_ge(s_xst[b % 2], 32 * (b // 2))
                    dve.wait_ge(s_res, b - 1)
                    dve.wait_ge(s_xt, 2 * (b - 1))
                nc.vector.tensor_scalar(xn[0:P, b % 2], xin[0:P, b], meanvar[0:P, b, 0:1], rstd[0:P, b:b + 1],
                                        ALU.subtract, ALU.mult).then_inc(s_xn, 1)

            def low_parts(b):
                for i in range(2):
                    dve.wait_ge(s_xth, 2 * b + i + 1)
                    nc.vector.tensor_tensor(XTl[:, 3 * i:3 * i + 3, P * b:P * b + P],
                                            bank(2 * (b % 2) + i)[:, 0:375].rearrange("p (k n) -> p k n", k=3),
                                            XTh[:, 3 * i:3 * i + 3, P * b:P * b + P].bitcast(F32),
                                            ALU.subtract).then_inc(s_xtl, 1)

            for h in range(2):
                for b in range(PAIRS * h, PAIRS * (h + 1)):
                    dve.wait_ge(s_x[b // 2], 32)
                    for i in range(2):
                        chain(nc.vector.bn_stats(stats[0:P, b, 6 * i:6 * i + 6], xin[0:P, b, 384 * i:384 * i + 384]))
                    nc.vector.bn_aggr(meanvar[0:P, b, :], stats[0:P, b, :]).then_inc(s_var, 1)
                dve.wait_ge(s_sd, h + 1)
                chain(nc.vector.reciprocal(rstd[0:P, PAIRS * h:PAIRS * (h + 1)], stdev[0:P, PAIRS * h:PAIRS * (h + 1)]))
                for b in range(PAIRS * h, PAIRS * (h + 1)):
                    normalise(b)
                    if b >= 1:
                        low_parts(b - 1)
                    {0: edges_to_float, 2: edge_columns, 4: edge_ranges, 6: batch_norm, 7: edge_limits}.get(b, lambda: None)()
            low_parts(BLK - 1)
            dve.wait_ge(s_pre, PROJ_T)
            chain(nc.vector.memset(pscaled[:], 0.0))
            for a in range(2):
                chain(nc.vector.tensor_scalar(pscaled[64 * a:64 * a + 64, M * a:M * a + M], bank(6)[64 * a:64 * a + 64, 0:M],
                                              NORM, None, ALU.mult))
            chain(nc.vector.tensor_copy(projh[:], pscaled[:]))
            nc.vector.tensor_tensor(projl[:], pscaled[:], projh[:].bitcast(F32), ALU.subtract).then_inc(s_prd, 1)
            dve.wait_ge(s_prd, PROJ_D)
            nc.vector.reduce_max(gmax[:], XTh[:].bitcast(F32).rearrange("p k n -> p (k n)"), X_AXIS).then_inc(s_prd, 1)

            def route():
                grid = [P, BLK, NE]
                dve.wait_ge(s_lgs, BLK)
                chain(nc.vector.reduce_max(best[0:P], logit[0:P], X_AXIS))
                chain(nc.vector.tensor_tensor(logit[0:P], logit[0:P], best[0:P].unsqueeze(2).to_broadcast(grid), ALU.subtract))
                nc.vector.tensor_copy(sume[0:P], logit[0:P]).then_inc(s_route, 1)
                chain(nc.vector.tensor_scalar(logit[0:P], logit[0:P], 0.0, None, ALU.is_equal))
                chain(nc.vector.tensor_tensor(logit[0:P], logit[0:P], down[0:P].unsqueeze(1).to_broadcast(grid), ALU.mult))
                chain(nc.vector.reduce_max(best[0:P], logit[0:P], X_AXIS))
                nc.vector.tensor_tensor(onehot[0:P], logit[0:P], best[0:P].unsqueeze(2).to_broadcast(grid), ALU.is_equal).then_inc(s_route, 1)
                dve.wait_ge(s_se, 1)
                chain(nc.vector.reduce_sum(prob[0:P], sume[0:P], X_AXIS))
                chain(nc.vector.reciprocal(prob[0:P], prob[0:P]))
                dve.wait_ge(s_rk, 1)
                chain(nc.vector.memset(carry[0:P, 0], 0.0))
                for b in range(BLK):
                    chain(nc.vector.tensor_tensor(carry[0:P, b + 1], carry[0:P, b], bank(6)[0:P, NE * b:NE * b + NE], ALU.add))
                chain(nc.vector.tensor_tensor(cmpe[0:P], carry[0:P, BLK].unsqueeze(2).to_broadcast([P, NE, BLK]),
                                              k128[0:P, 0:BLK].unsqueeze(1).to_broadcast([P, NE, BLK]), ALU.is_gt))
                chain(nc.vector.reduce_sum(nblk[0:P], cmpe[0:P], X_AXIS))
                chain(nc.vector.tensor_copy(endb[0:P, 0:1], nblk[0:P, 0:1]))
                for e in range(1, NE):
                    chain(nc.vector.tensor_tensor(endb[0:P, e:e + 1], endb[0:P, e - 1:e], nblk[0:P, e:e + 1], ALU.add))
                chain(nc.vector.tensor_tensor(cmpb[:], upto[0:1].unsqueeze(2).to_broadcast([1, SB, NE]),
                                              endb[0:1].unsqueeze(1).to_broadcast([1, SB, NE]), ALU.is_ge))
                chain(nc.vector.reduce_sum(expf[:], cmpb[:], X_AXIS))
                chain(nc.vector.tensor_scalar(expf[:], expf[:], float(NE - 1), None, ALU.min))
                nc.vector.tensor_copy(expi[:], expf[:]).then_inc(s_route, 1)
                chain(nc.vector.tensor_tensor(nblk[0:P], endb[0:P], nblk[0:P], ALU.subtract))
                chain(nc.vector.tensor_scalar(nblk[0:P], nblk[0:P], 128.0, None, ALU.mult))
                chain(nc.vector.tensor_tensor(sume[0:P], bank(5)[0:P, 0:BLK * NE].rearrange("p (b e) -> p b e", b=BLK), carry[0:P, 0:BLK], ALU.add))
                chain(nc.vector.tensor_tensor(sume[0:P], sume[0:P], nblk[0:P].unsqueeze(1).to_broadcast(grid), ALU.add))
                chain(nc.vector.tensor_tensor(sume[0:P], sume[0:P], onehot[0:P], ALU.mult))
                chain(nc.vector.reduce_sum(pos[0:P], sume[0:P], X_AXIS))
                chain(nc.vector.tensor_copy(idxy[0:P], pos[0:P]))
                chain(nc.vector.tensor_tensor(cmpk[0:P], pos[0:P].unsqueeze(2).to_broadcast([P, BLK, SB - 1]),
                                              k128[0:P, 1:SB].unsqueeze(1).to_broadcast([P, BLK, SB - 1]), ALU.is_ge))
                chain(nc.vector.reduce_sum(quo[0:P], cmpk[0:P], X_AXIS))
                chain(nc.vector.tensor_scalar(quo[0:P], quo[0:P], 1.0 - 128.0 * SB, None, ALU.mult))
                chain(nc.vector.scalar_tensor_tensor(out=pos[0:P], in0=pos[0:P], scalar=float(SB), in1=quo[0:P], op0=ALU.mult, op1=ALU.add))
                nc.vector.tensor_copy(idxt[0:P], pos[0:P]).then_inc(s_route, 1)

            def stabiliser():
                dve.wait_ge(s_pre, MAX_T)
                chain(nc.vector.reduce_max(mrow[0:1, 0:1], bank(7)[0:1, 0:128], X_AXIS))
                chain(nc.vector.tensor_scalar(mrow[0:1, 1:2], mrow[0:1, 0:1], 0.0, 1e-7, ALU.max, ALU.add))
                chain(nc.vector.tensor_tensor(mrow[0:1, 2:3], mrow[0:1, 1:2], tb[0:1, :], ALU.mult))
                chain(nc.vector.scalar_tensor_tensor(out=mrow[0:1, 3:4], in0=tb[0:1, :], scalar=1e-7, in1=mrow[0:1, 2:3],
                                                     op0=ALU.mult, op1=ALU.max))
                nc.vector.tensor_scalar(mrow[0:1, 4:5], mrow[0:1, 3:4], -1.0, SHIFT, ALU.mult, ALU.add).then_inc(s_prd, 1)

            first = chain.n
            PER = 3 + 2 * BLK

            with dve.Fori(0, HP) as j:
                chain.at(j * PER + first)
                for n, (c0, c1) in enumerate(BANKS):
                    dve.wait_ge(s_kh, 3 * j + n + 1)
                    nc.vector.tensor_tensor(KTl[:, c0:c1], PB[:, c0:c1], KTh[:, c0:c1].bitcast(F32), ALU.subtract).then_inc(s_kl, 1)
                dve.wait_ge(s_kdg, j + 1)
                nc.vector.tensor_copy(kdiag[0:P], bank(5)[0:P, 256:276].rearrange("p (b a) -> p b a", a=2)).then_inc(s_kdc, 1)
                dve.wait_ge(s_kcp, BLK * j + BLK)
                for a in range(2):
                    ins = nc.vector.reduce_max(km[0:P, a:a + 1], kp[0:P, a].rearrange("p b m -> p (b m)"), X_AXIS)
                ins.then_inc(s_ksum, 1)
                for n, (c0, c1) in enumerate(BANKS):
                    dve.wait_ge(s_qh, 3 * j + n + 1)
                    nc.vector.tensor_tensor(QTl[:, c0:c1], PB[:, c0:c1], QTh[:, c0:c1].bitcast(F32), ALU.subtract).then_inc(s_ql, 1)
                dve.wait_ge(s_kmT, j + 1)
                chain(nc.vector.reduce_max(gmx[0:2, :], bank(6)[0:2, 0:P], X_AXIS))
                nc.vector.tensor_scalar(dg[0:2, :], ident[0:2, 0:2], gmx[0:2, :], None, ALU.mult).then_inc(s_dg, 1)
                dve.wait_ge(s_stb, j + 1)
                chain(nc.vector.tensor_copy(stab[0:P, :], bank(7)[0:P, 0:2]))
                for a in range(2):
                    ins = nc.vector.tensor_scalar(kbias[0:P, a, :], kdiag[0:P, :, a], stab[0:P, a:a + 1], -1.0, ALU.add, ALU.mult)
                ins.then_inc(s_kb, 1)
                for a in range(2):
                    dve.wait_ge(s_ke, 2 * j + a + 1)
                    nc.vector.tensor_scalar(kp[0:P, a], kp[0:P, a], EPS, RATIO, ALU.add, ALU.mult).then_inc(s_kp, 1)
                dve.wait_ge(s_qdg, j + 1)
                chain(nc.vector.tensor_copy(qdiag[0:P], bank(5)[0:P, 256:276].rearrange("p (b a) -> p b a", a=2)))

                def bias(u):
                    dve.wait_ge(s_qd, BLK * j + u + 1)
                    chain(nc.vector.reduce_max(qmx[0:P, u % 2], bank(6 + u % 2)[0:P, :].rearrange("p (a m) -> p a m", a=2), X_AXIS))
                    nc.vector.scalar_tensor_tensor(out=qbias[0:P, u % 2, :], in0=qmx[0:P, u % 2], scalar=-1.0,
                                                   in1=qdiag[0:P, u, :], op0=ALU.mult,
                                                   op1=ALU.subtract).then_inc(s_qb, 1)

                def features(u):
                    dve.wait_ge(s_qt, BLK * j + u + 1)
                    if u >= 2:
                        dve.wait_ge(s_o, BLK * j + u - 1)
                    nc.vector.tensor_scalar(qpT[:, u % 2], bank(1 + u % 2)[:, 0:4 * P].rearrange("p (a c n) -> p a c n", a=2, c=2),
                                            EPS, RATIO, ALU.add, ALU.mult).then_inc(s_qp, 1)

                def normal(u):
                    o = bank(3 * (u % 2))[0:P, 0:130].rearrange("p (a d) -> p a d", a=2)
                    dve.wait_ge(s_o, BLK * j + u + 1)
                    chain(nc.vector.reciprocal(rden[0:P, u % 2], o[:, :, DH]))
                    nc.vector.tensor_tensor(att[0:P, u, :].rearrange("p (a d) -> p a d", a=2), o[:, :, 0:DH],
                                            rden[0:P, u % 2].unsqueeze(2).to_broadcast([P, 2, DH]), ALU.mult).then_inc(s_at, 1)

                for u in range(BLK + 4):
                    if u < BLK:
                        bias(u)
                    if 2 <= u < BLK + 2:
                        features(u - 2)
                    if u >= 4:
                        normal(u - 4)
                assert chain.n == PER, (chain.n, PER)
            chain.at(first + HP * PER)
            for b in range(BLK):
                turn0, turn1, offset = (nc.vector.value_load(limi[0:1, BLK * i + b:BLK * i + b + 1], min_val=lo, max_val=hi)
                                        for i, (lo, hi) in enumerate(((0, b * EG), (0, (b + 1) * EG), (-b * EG, EG))))
                with dve.Fori(turn0, turn1) as n:
                    g = nc.s_assert_within(n + offset, 0, EG - 1, skip_runtime_bounds_check_because="turns map to groups first .. end - 1 of the block, all within the list")
                    for u in range(2):
                        dve.wait_ge(s_ohf[u], n + 1)
                        nc.vector.tensor_scalar(ohd[:, u, 0:P], iota[:, P * b:P * b + P], dcol[:, bass.ds(g * 2 + u, 1)], None, ALU.is_equal)
                        nc.vector.tensor_scalar(ohs[:, u, :], iota[:], scol[:, bass.ds(g * 2 + u, 1)], None, ALU.is_equal).then_inc(s_oh[u], 1)
                if b == 0:
                    stabiliser()
                if b == 1:
                    dve.wait_ge(s_pre, STAB)
                    nc.vector.tensor_copy(mbias[:], bank(7)[:, 0:1]).then_inc(s_prd, 1)

            for n in range(2 * BLK + 2):
                if n == BLK:
                    dve.wait_ge(s_woh, 2)
                    nc.vector.tensor_tensor(wol[:], woraw[:], woh[:].bitcast(F32), ALU.subtract).then_inc(s_wol, 1)
                if n < 2 * BLK:
                    b = n % BLK
                    dve.wait_ge(s_ath, n + 1)
                    nc.vector.tensor_tensor(attl[:, n % 2], attT[:, :, P * b:P * b + P], atth[:, n % 2].bitcast(F32),
                                            ALU.subtract).then_inc(s_atl, 1)
                if n >= 2:
                    o = n - 2
                    dve.wait_ge(s_ow, o + 1)
                    dve.wait_ge(s_rl[o % 2], 16 * (o // 2 + 1))
                    nc.vector.tensor_tensor(rtile[0:P, o % 2], rtile[0:P, o % 2], bank(o % 2)[0:P, 0:HALF], ALU.add).then_inc(s_ro, 1)

            def exponentials(c):
                if c >= K:
                    return
                u = c % 2
                dve.wait_ge(s_ml[u], 16 * (c // 2 + 1))
                nc.vector.tensor_scalar(msg[0:P, u], msg[0:P, u], 0.0, 1e-7, ALU.max, ALU.add).then_inc(s_ms, 1)
                dve.wait_ge(s_ex, c + 1)
                nc.vector.tensor_tensor(msg[0:P, u], Ef[0:P], msg[0:P, u], ALU.mult).then_inc(s_mm, 1)
                dve.wait_ge(s_eh, c + 1)
                nc.vector.tensor_tensor(parts[u][1][0:P], Ef[0:P], parts[u][0][0:P].bitcast(F32), ALU.subtract)
                dve.wait_ge(s_mh, c + 1)
                nc.vector.tensor_tensor(parts[u][3][0:P], msg[0:P, u], parts[u][2][0:P].bitcast(F32), ALU.subtract).then_inc(s_ep, 1)

            for i in range(2):
                dve.wait_ge(s_rs[i], 16 * BLK)
            exponentials(0)
            for c in range(K):
                exponentials(c + 1)
                dve.wait_ge(s_sum, 2 * c + 1)
                chain(nc.vector.tensor_scalar(rec[:], PS[:, 0:N], 1e-37, None, ALU.max))
                nc.vector.sem_inc(s_sumr, 1)
                chain(nc.vector.reciprocal(rec[:], rec[:]))
                dve.wait_ge(s_sum, 2 * c + 2)
                chain(nc.vector.tensor_tensor(agg[:], PS[:, 1536:1536 + N], rec[:], ALU.mult))
                nc.vector.sem_inc(s_sumr, 1)
                chain(nc.vector.tensor_tensor(agg[:], agg[:], XTh[:, c, :].bitcast(F32), ALU.add))
                nc.vector.tensor_tensor(agg[:], agg[:], XTl[:, c, :].bitcast(F32), ALU.add).then_inc(s_ag, 1)
                dve.wait_ge(s_agh, c + 1)
                chain(nc.vector.tensor_tensor(XTl[:, c, :], agg[:], XTh[:, c, :].bitcast(F32), ALU.subtract))
            nc.vector.sem_inc(s_agl, 1)

            def w1_parts(m):
                if m < HC:
                    dve.wait_ge(s_w1h, m + 1)
                    nc.vector.tensor_tensor(w1l[:, m % 2], w1raw[:, m % 2], w1h[:, m % 2].bitcast(F32), ALU.subtract).then_inc(s_w1l, 1)

            def w2_parts(i):
                k = 3 * (i % 4)
                dve.wait_ge(s_w2h, i + 1)
                nc.vector.tensor_tensor(w2l[i // 4][:, k:k + 3, :], w2raw[:, i % 2], w2h[i // 4][:, k:k + 3, :].bitcast(F32),
                                        ALU.subtract).then_inc(s_w2l, 1)

            for m in range(HC):
                w1_parts(m)
                if 5 <= m < 9:
                    w2_parts(m - 5)

            def hidden_parts(n):
                if n < 2 * BLK:
                    b = n % BLK
                    dve.wait_ge(s_hth, n + 1)
                    nc.vector.tensor_tensor(htl[n % 2][:], HT[:, :, P * b:P * b + P], hth[n % 2][:].bitcast(F32), ALU.subtract).then_inc(s_htl, 1)

            def second_layer(n):
                h, b = n // BLK, n % BLK
                dve.wait_ge(s_o2, n + 1)
                dve.wait_ge(s_r2l[n % 2], 16 * (n // 2 + 1))
                where = rtile2[0:P, n % 2] if h == 0 else x1[0:P, b, HALF:D]
                nc.vector.tensor_tensor(where, rtile2[0:P, n % 2], bank(n % 2)[0:P, 0:HALF], ALU.add).then_inc(s_r2, 1)

            def norm2(b):
                if b == 0:
                    dve.wait_ge(s_x1l, 16)
                dve.wait_ge(s_r2, BLK + b + 1)
                for i in range(2):
                    chain(nc.vector.bn_stats(stats2[0:P, b, 6 * i:6 * i + 6], x1[0:P, b, HALF * i:HALF * i + HALF]))
                nc.vector.bn_aggr(mv2[0:P, b, :], stats2[0:P, b, :]).then_inc(s_v2, 1)
                dve.wait_ge(s_sd2, b + 1)
                chain(nc.vector.reciprocal(sd2[0:P, b:b + 1], sd2[0:P, b:b + 1]))
                if b >= 2:
                    dve.wait_ge(s_xn2s[b % 2], 16 * (b // 2))
                    dve.wait_ge(s_x2t, b - 1)
                nc.vector.tensor_scalar(xn2[0:P, b % 2], x1[0:P, b], mv2[0:P, b, 0:1], sd2[0:P, b:b + 1],
                                        ALU.subtract, ALU.mult).then_inc(s_xn2, 1)

            def logits(b):
                dve.wait_ge(s_lg, b + 1)
                nc.vector.tensor_copy(logit[0:P, b, :], bank(4)[0:P, 0:NE]).then_inc(s_lgs, 1)

            hidden_parts(0)
            hidden_parts(1)
            for i in range(4, 8):
                w2_parts(i)
                second_layer(i - 4)
                hidden_parts(i - 2)
            for n in range(6, 2 * BLK + 2):
                hidden_parts(n)
                second_layer(n - 2)
                if n >= BLK + 2:
                    norm2(n - BLK - 2)
                if n >= BLK + 3:
                    logits(n - BLK - 3)
            logits(BLK - 1)
            route()

            def expert_parts(n, u):
                dve.wait_ge(s_fh, n + 1)
                nc.vector.tensor_tensor(w12l[u][:], w12raw[u][:], w12h[u][:].bitcast(F32), ALU.subtract).then_inc(s_fl, 1)

            def rows_parts(n, u):
                dve.wait_ge(s_gh, n + 1)
                for c in range(2):
                    ins = nc.vector.tensor_tensor(xgl[:, u, 3 * c:3 * c + 3], bank(c)[:, 0:384].rearrange("p (k n) -> p k n", k=3),
                                                  xgh[:, u, 3 * c:3 * c + 3].bitcast(F32), ALU.subtract)
                ins.then_inc(s_gl, 1)

            def expert_hidden(n):
                dve.wait_ge(s_sg, n + 1)
                nc.vector.tensor_tensor(hid[:], gate[:], bank(2)[:, FH:2 * FH], ALU.mult).then_inc(s_hd, 1)
                dve.wait_ge(s_hh, n + 1)
                nc.vector.tensor_tensor(hidl[:], bank(3)[:, 0:FH].rearrange("p (k n) -> p k n", k=FC), hidh[:].bitcast(F32),
                                        ALU.subtract).then_inc(s_hl, 1)

            def expert_turn(n, u, i, last=False):
                expert_hidden(n)
                if not last:
                    rows_parts(n + 1, 1 - u)
                    expert_parts(n + 1, 1 - u)
                dve.wait_ge(s_fl, n + 1)
                dve.wait_ge(s_f3, n + 1)
                nc.vector.sem_inc(s_frf[u], 1)

            rows_parts(0, 0)
            expert_parts(0, 0)
            with dve.Fori(0, SB // 2) as i:
                for u in range(2):
                    expert_turn(i * 2 + u, u, i)
            expert_turn(SB - 1, 0, SB // 2, last=True)
            for b in range(BLK):
                dve.wait_ge(s_yg[b % 2], 16 * (b // 2 + 1))
                nc.vector.scalar_tensor_tensor(out=x1[0:P, b], in0=yg[0:P, b % 2], scalar=prob[0:P, b:b + 1], in1=x1[0:P, b],
                                               op0=ALU.mult, op1=ALU.add).then_inc(s_fin, 1)

        @block.tensor
        def _(pe):
            pe.wait_ge(s_cst, 16)
            for b in range(BLK):
                pe.wait_ge(s_xn, b + 1)
                for i in range(2):
                    if b >= 2:
                        pe.wait_ge(s_xtl, 2 * (b - 2) + i + 1)
                    for c in range(3):
                        ins = nc.tensor.transpose(bank(2 * (b % 2) + i)[:, P * c:P * c + P],
                                                  xn[0:P, b % 2, 384 * i + 128 * c:384 * i + 128 * c + 128], ident[0:P, 0:P])
                    ins.then_inc(s_xt, 1)
                if b == 1:
                    pe.wait_ge(s_prd, EDGE_F)
                    for i in range(2):
                        for g in range(3):
                            ins = nc.tensor.transpose(bank(4 + i)[:, ER * g:ER * g + ER], edf[0:ER, i, g, :], ident[0:ER, 0:ER])
                    ins.then_inc(s_pre, 1)
                    pe.wait_ge(s_par, 144)
                    nc.tensor.transpose(bank(7)[:, 0:5 * HC], bnr[0:5 * HC, :], ident[0:5 * HC, 0:5 * HC]).then_inc(s_pre, 1)
                if b == 3:
                    pe.wait_ge(s_prd, EDGE_MM)
                    for i in range(2):
                        for g in range(3):
                            ins = nc.tensor.matmul(bank(4 + i)[0:BLK, ER * g:ER * g + ER], tmm[0:ER, i, g:g + 1].to_broadcast([ER, BLK]),
                                                   ident[0:ER, 0:ER], start=True, stop=True)
                    ins.then_inc(s_pre, 1)
                if b == 6:
                    pe.wait_ge(s_prd, EDGE_EL)
                    pe.wait_ge(s_prd, BN_D)
                    nc.tensor.matmul(bank(7)[0:1, 64:64 + BLK], elim[0:BLK, 2:3], tri[0:BLK, 0:BLK], start=True, stop=True)
                    nc.tensor.matmul(bank(7)[0:1, 64 + BLK:64 + 2 * BLK], elim[0:BLK, 2:3], tri[0:BLK, 0:BLK], start=True, stop=False)
                    nc.tensor.matmul(bank(7)[0:1, 64 + BLK:64 + 2 * BLK], elim[0:BLK, 2:3], ident[0:BLK, 0:BLK], start=False, stop=True)
                    ins = nc.tensor.matmul(bank(7)[0:1, 64 + 2 * BLK:64 + 3 * BLK], elim[0:BLK, 0:1], ident[0:BLK, 0:BLK], start=True, stop=True)
                    ins.then_inc(s_pre, 1)
            pe.wait_ge(s_par, 144)
            for c in range(2):
                ins = nc.tensor.transpose(bank(6)[:, 128 * c:128 * c + 128], praw[:, c, :], ident[:])
            ins.then_inc(s_pre, 1)
            pe.wait_ge(s_xtl, 2 * BLK)
            pe.wait_ge(s_prd, PROJ_D)

            def project(j, n, where, done):
                for c0, c1 in BANKS:
                    for k in range(K):
                        if n == 2 and c0 == 1024 and k == 0:
                            pe.wait_ge(s_kdc, j + 1)
                        for w, xt in ((wh, XTh), (wh, XTl), (wl, XTh)):
                            ins = nc.tensor.matmul(where[:, c0:c1], w[:, n, k, :], xt[:, k, c0:c1],
                                                   start=(k == 0 and w is wh and xt is XTh), stop=(k == K - 1 and w is wl))
                ins.then_inc(done, 1)

            pe.sem_inc(s_qps, 1)
            with pe.Fori(0, HP) as j:
                pe.wait_ge(s_wok, j + 1)
                project(j, 0, PB, s_kps)
                project(j, 1, PA, s_vps)

                def dash(u, th, tl):
                    for q, w in ((th, projh), (th, projl), (tl, projh)):
                        ins = nc.tensor.matmul(bank(6 + u % 2)[0:P, :], q[:, P * u:P * u + P], w[:],
                                               start=(q is th and w is projh), stop=(q is tl))
                    return ins

                def diag():
                    for b in range(BLK):
                        ins = nc.tensor.matmul(bank(5)[0:P, 256 + 2 * b:258 + 2 * b], sq[:, P * b:P * b + P], ind[:], start=True, stop=True)
                    return ins

                pe.wait_ge(s_kl, 3 * j + 3)
                for u in range(BLK):
                    if u >= 2:
                        pe.wait_ge(s_kcp, BLK * j + u - 1)
                    dash(u, KTh, KTl).then_inc(s_kd, 1)
                diag().then_inc(s_kdg, 1)
                project(j, 2, PB, s_qps)
                pe.wait_ge(s_ksum, j + 1)
                nc.tensor.transpose(bank(6)[0:2, 0:P], km[0:P, :], ident[0:P, 0:P]).then_inc(s_kmT, 1)
                pe.wait_ge(s_vt, j + 1)
                for b in range(BLK):
                    ins = nc.tensor.transpose(PA[0:P, 128 * b:128 * b + 128], VT[:, P * b:P * b + P], ident[:])
                ins.then_inc(s_vtp, 1)
                pe.wait_ge(s_dg, j + 1)
                nc.tensor.matmul(bank(7)[0:P, 0:2], ones[0:2, 0:P], dg[0:2, :], start=True, stop=True).then_inc(s_stb, 1)
                pe.wait_ge(s_ql, 3 * j + 3)
                diag().then_inc(s_qdg, 1)
                pe.wait_ge(s_kb, j + 1)
                for u in range(2):
                    dash(u, QTh, QTl).then_inc(s_qd, 1)
                pe.wait_ge(s_v, j + 1)
                for a in range(2):
                    pe.wait_ge(s_kp, 2 * j + a + 1)
                    for c in range(2):
                        g = 2 * a + c
                        for b in range(BLK):
                            ins = nc.tensor.matmul(bank(3)[:, 65 * g:65 * g + 65], kp[0:P, a, b, 128 * c:128 * c + 128], V[0:P, b, a, :],
                                                   start=(b == 0), stop=(b == BLK - 1))
                ins.then_inc(s_cx, 1)

                def turn(u):
                    pe.wait_ge(s_qe, BLK * j + u + 1)
                    for a in range(2):
                        for c in range(2):
                            g = 2 * a + c
                            ins = nc.tensor.transpose(bank(1 + u % 2)[:, P * g:P * g + P], qe[0:P, u % 2, a, 128 * c:128 * c + 128], ident[0:P, 0:P])
                    ins.then_inc(s_qt, 1)

                def attend(u):
                    pe.wait_ge(s_qp, BLK * j + u + 1)
                    if u >= 2:
                        pe.wait_ge(s_at, BLK * j + u - 1)
                    if u == 0:
                        pe.wait_ge(s_cxs, j + 1)
                    for a in range(2):
                        for c in range(2):
                            ins = nc.tensor.matmul(bank(3 * (u % 2))[0:P, 65 * a:65 * a + 65], qpT[:, u % 2, a, c, :], ctxs[:, a, c, :], start=(c == 0), stop=(c == 1))
                    ins.then_inc(s_o, 1)

                def turn_att(b):
                    pe.wait_ge(s_at, BLK * j + b + 1)
                    if b == 1:
                        pe.wait_ge(s_qb, BLK * j + 1)
                    if b >= 2:
                        pe.wait_ge(s_as, BLK * j + b - 1)
                    nc.tensor.transpose(bank(4 + b % 2)[:, 0:P], att[0:P, b, :], ident[0:P, 0:P]).then_inc(s_aT, 1)

                for u in range(2, BLK + 4):
                    if u < BLK:
                        pe.wait_ge(s_qe, BLK * j + u - 1)
                        dash(u, QTh, QTl).then_inc(s_qd, 1)
                    if u - 2 < BLK:
                        turn(u - 2)
                    if 0 <= u - 3 < BLK:
                        attend(u - 3)
                    if u >= 4:
                        turn_att(u - 4)
                pe.wait_ge(s_as, BLK * j + BLK)

            pe.wait_ge(s_prd, GMAX_D)
            nc.tensor.transpose(bank(7)[0:1, 0:128], gmax[:], ident[:]).then_inc(s_pre, 1)
            pe.wait_ge(s_prd, LIM_I)
            for u in range(2):
                pe.sem_inc(s_ohf[u], 1)

            def turn_counts(b):
                pe.wait_ge(s_cr, b + 1)
                for i in range(3):
                    if 3 * b + i >= 2:
                        pe.wait_ge(s_cs, 3 * b + i - 1)
                    for c in range(min(4, BLK - 4 * i)):
                        ins = nc.tensor.transpose(bank(6 + (3 * b + i) % 2)[0:P, P * c:P * c + P],
                                                  crow[0:P, b % 2, P * (4 * i + c):P * (4 * i + c) + P], ident[0:P, 0:P])
                    ins.then_inc(s_ct, 1)

            for b in range(BLK):
                turn0, turn1, offset = (nc.tensor.value_load(limi[0:1, BLK * i + b:BLK * i + b + 1], min_val=lo, max_val=hi)
                                        for i, (lo, hi) in enumerate(((0, b * EG), (0, (b + 1) * EG), (-b * EG, EG))))
                if b >= 2:
                    pe.wait_ge(s_cr, b - 1)
                counts = PS[0:P, 1536 * (b % 2):1536 * (b % 2) + 1536]
                for c in range(3):
                    nc.tensor.matmul(counts[:, 512 * c:512 * c + 512], zeros[:, 0:P], zeros[:], start=True, stop=False, skip_group_check=True)
                with pe.Fori(turn0, turn1) as n:
                    for u in range(2):
                        pe.wait_ge(s_oh[u], n + 1)
                        for c0, c1 in BANKS:
                            ins = nc.tensor.matmul(counts[:, c0:c1], ohd[:, u, 0:P], ohs[:, u, c0:c1], start=False, stop=False,
                                                   skip_group_check=True)
                        ins.then_inc(s_ohf[u], 1)
                for c in range(3):
                    ins = nc.tensor.matmul(counts[:, 512 * c:512 * c + 2], zeros[:, 0:P], zeros[:, 0:2], start=False, stop=True,
                                           skip_group_check=True)
                ins.then_inc(s_cn, 1)
                if b == 0:
                    pe.wait_ge(s_prd, MROW_D)
                    nc.tensor.matmul(bank(7)[:, 0:1], ones[0:1, :], mrow[0:1, 4:5], start=True, stop=True).then_inc(s_pre, 1)
                if b == 1:
                    pe.wait_ge(s_prd, STAB_D)
                if b >= 1:
                    turn_counts(b - 1)
            turn_counts(BLK - 1)

            for n in range(2 * BLK):
                if n % BLK == 0:
                    pe.wait_ge(s_wol, n // BLK + 1)
                pe.wait_ge(s_atl, n + 1)
                if n >= 2:
                    pe.wait_ge(s_ro, n - 1)
                for k in range(K):
                    for q, w in ((atth, woh), (atth, wol), (attl, woh)):
                        ins = nc.tensor.matmul(bank(n % 2)[0:P, 0:HALF], q[:, n % 2, k, :], w[:, k, :],
                                               start=(k == 0 and q is atth and w is woh), stop=(k == K - 1 and q is attl))
                ins.then_inc(s_ow, 1)

            pe.wait_ge(s_cs, 3 * BLK)
            pe.wait_ge(s_ro, 2 * BLK)
            for c in range(K):
                pe.wait_ge(s_ep, c + 1)
                for n, (pa, pb_) in enumerate(((0, 1), (2, 3))):
                    if c >= 1:
                        pe.wait_ge(s_sumr, 2 * c - 1 + n)
                    for s in range(BLK):
                        for q in (pa, pb_):
                            for c0, c1 in BANKS:
                                ins = nc.tensor.matmul(PS[:, 1536 * n + c0:1536 * n + c1], parts[c % 2][q][0:P, s, :], CT[0:P, s, c0:c1],
                                                       start=(s == 0 and q == pa), stop=(s == BLK - 1 and q == pb_))
                    ins.then_inc(s_sum, 1)

            pe.wait_ge(s_agl, 1)
            for m in range(HC):
                pe.wait_ge(s_w1l, m + 1)
                if m >= 2:
                    pe.wait_ge(s_h, m - 1)
                for k in range(K):
                    for w, q in ((w1h, XTh), (w1h, XTl), (w1l, XTh)):
                        for c0, c1 in BANKS:
                            ins = nc.tensor.matmul(PS[:, 1536 * (m % 2) + c0:1536 * (m % 2) + c1], w[:, m % 2, k, :], q[:, k, c0:c1],
                                                   start=(k == 0 and w is w1h and q is XTh), stop=(k == K - 1 and w is w1l))
                ins.then_inc(s_z, 1)

            def second_layer(n):
                h = n // BLK
                if n % BLK == 0:
                    pe.wait_ge(s_w2l, 4 * h + 4)
                pe.wait_ge(s_htl, n + 1)
                if n >= 2:
                    pe.wait_ge(s_r2, n - 1)
                for k in range(HC):
                    for i, (q, w) in enumerate(((hth, w2h), (hth, w2l), (htl, w2h))):
                        ins = nc.tensor.matmul(bank(n % 2)[0:P, 0:HALF], q[n % 2][:, k, :], w[h][:, k, :],
                                               start=(k == 0 and i == 0), stop=(k == HC - 1 and i == 2))
                ins.then_inc(s_o2, 1)

            def turn_norm2(b):
                pe.wait_ge(s_xn2, b + 1)
                if b >= 1:
                    pe.wait_ge(s_x2s, b)
                for k in range(K):
                    ins = nc.tensor.transpose(bank(2 + k // 3)[:, P * (k % 3):P * (k % 3) + P], xn2[0:P, b % 2, 128 * k:128 * k + 128], ident[0:P, 0:P])
                ins.then_inc(s_x2t, 1)

            def router(b):
                pe.wait_ge(s_x2s, b + 1)
                if b >= 1:
                    pe.wait_ge(s_lgs, b)
                for k in range(K):
                    nc.tensor.matmul(bank(4)[0:P, 0:NE], xn2T[:, b % 2, k, :], rw[:, k, :], start=(k == 0), stop=False)
                nc.tensor.matmul(bank(4)[0:P, 0:NE], ones[0:1, 0:P], rb[:], start=False, stop=True).then_inc(s_lg, 1)

            pe.wait_ge(s_h, HC)
            for n in range(2 * BLK):
                if n >= BLK + 3:
                    turn_norm2(n - BLK - 3)
                if n >= BLK + 4:
                    router(n - BLK - 4)
                second_layer(n)
            pe.wait_ge(s_rw, 48)
            for b in range(BLK - 3, BLK):
                turn_norm2(b)
                router(b - 1)
            router(BLK - 1)
            pe.wait_ge(s_route, ONE_HOT)
            hot = onehot[0:P].rearrange("p b e -> p (b e)")
            nc.tensor.matmul(bank(5)[0:P, 0:BLK * NE], tri[0:P, 0:P], hot, start=True, stop=True)
            nc.tensor.matmul(bank(6)[0:P, 0:BLK * NE], ones[0:P, 0:P], hot, start=True, stop=True).then_inc(s_rk, 1)

            def turn_rows(n, u, i):
                pe.wait_ge(s_g[u], i * 16 + 16)
                pe.wait_ge(s_gl, n + 1)
                for k in range(K):
                    ins = nc.tensor.transpose(bank(k // 3)[:, 128 * (k % 3):128 * (k % 3) + 128], xg[:, u, 128 * k:128 * k + 128], ident[:])
                ins.then_inc(s_gt, 1)

            def up(n, u):
                pe.wait_ge(s_gl, n + 2)
                pe.wait_ge(s_fl, n + 1)
                for k in range(K):
                    for i, (q, w) in enumerate(((xgh, w12h), (xgh, w12l), (xgl, w12h))):
                        ins = nc.tensor.matmul(bank(2)[:, :], q[:, u, k, :], w[u][:, k, :], start=(k == 0 and i == 0), stop=(k == K - 1 and i == 2))
                ins.then_inc(s_up, 1)

            def turn_hidden(n):
                pe.wait_ge(s_hd, n + 1)
                for k in range(FC):
                    ins = nc.tensor.transpose(bank(3)[:, 128 * k:128 * k + 128], hid[:, 128 * k:128 * k + 128], ident[:])
                ins.then_inc(s_ht, 1)

            def down_projection(n, u):
                pe.wait_ge(s_hl, n + 1)
                pe.wait_ge(s_f3, n + 1)
                if isinstance(n, int) and n >= 1:
                    pe.wait_ge(s_yb, n)
                for c in range(2):
                    for k in range(FC):
                        for i, (q, w) in enumerate(((hidh, w3h), (hidh, w3l), (hidl, w3h))):
                            ins = nc.tensor.matmul(bank(4 + c)[:, 0:HALF], q[:, k, :], w[u][:, k, HALF * c:HALF * c + HALF],
                                                   start=(k == 0 and i == 0), stop=(k == FC - 1 and i == 2))
                ins.then_inc(s_y, 1)

            pe.sem_inc(s_gl, 1)
            pe.sem_inc(s_up, 2)
            pe.sem_inc(s_y, 2)
            turn_rows(0, 0, 0)
            up(0, 0)
            turn_rows(1, 1, 0)
            turn_hidden(0)
            up(1, 1)
            down_projection(0, 0)
            turn_rows(2, 0, 1)
            turn_hidden(1)
            with pe.Fori(1, SB // 2) as i:
                for u in range(2):
                    n = i * 2 + u
                    up(n, u)
                    pe.wait_ge(s_yb, n - 1)
                    down_projection(n - 1, 1 - u)
                    turn_rows(n + 1, 1 - u, i + u)
                    turn_hidden(n)
            up(SB - 1, 0)
            down_projection(SB - 2, 1)
            turn_hidden(SB - 1)
            down_projection(SB - 1, 0)


_INS = ['x', 'src', 'dst', 'L0_gnn_t', 'L0_gnn_W1', 'L0_gnn_b1', 'L0_gnn_bn_gamma', 'L0_gnn_bn_beta', 'L0_gnn_bn_mean',
        'L0_gnn_bn_var', 'L0_gnn_W2', 'L0_gnn_b2', 'L0_mix_Wq', 'L0_mix_Wk', 'L0_mix_Wv', 'L0_mix_Wo', 'L0_mix_proj',
        'L0_ffn_router_w', 'L0_ffn_router_b', 'L0_ffn_w1', 'L0_ffn_w2', 'L0_ffn_w3']


def kernel(**inputs):
    import numpy as _np
    import concourse.bacc as _bacc
    from concourse import mybir as _mybir
    from concourse.bass_utils import run_bass_kernel_spmd as _run

    nc = _bacc.Bacc("TRN2", target_bir_lowering=False, num_devices=1)
    arrays, args = {}, []
    for name in _INS:
        a = _np.ascontiguousarray(inputs[name])
        if a.ndim == 0:
            a = a.reshape(1)
        arrays[f"in_{name}_dram"] = a
        args.append(nc.dram_tensor(f"in_{name}_dram", a.shape, _mybir.dt.from_np(a.dtype), kind="ExternalInput").ap())
    out = nc.dram_tensor("out_0_dram", (1250, 768), _mybir.dt.float32, kind="ExternalOutput").ap()
    build(nc, *args, out, debug=DEBUG)
    r = _run(nc, [arrays], core_ids=[0])
    return r.results[0]["out_0_dram"]


DEBUG = None
```

```python
import concourse.bass as bass
from concourse import mybir
from contextlib import ExitStack

F32, F32R = mybir.dt.float32, mybir.dt.float32r
BF16, FP16, I32 = mybir.dt.bfloat16, mybir.dt.float16, mybir.dt.int32
ALU = mybir.AluOpType
ACT = mybir.ActivationFunctionType
X_AXIS = mybir.AxisListType.X


class Chain:

    def __init__(self, eng, sem):
        self.eng, self.sem, self.start, self.n = eng, sem, 0, 0

    def at(self, start):
        self.start, self.n = start, 0

    def __call__(self, ins):
        self.n += 1
        ins.then_inc(self.sem, 1)
        self.eng.wait_ge(self.sem, self.start + self.n)


def build(nc, x, src, dst, t, W1, b1, gamma, beta, mean, var, W2, b2, Wq, Wk, Wv, Wo, proj,
          router_w, router_b, w1, w2, w3, out):
    N, D = x.shape
    P = 125
    BLK = N // P
    PAIRS = BLK // 2
    K = D // 128
    M, DH = proj.shape
    HEADS = D // DH
    HP = HEADS // 2
    RATIO = M ** -0.5
    NORM = DH ** -0.25
    EPS = 1e-4
    BANKS = [(0, 512), (512, 1024), (1024, N)]
    E = src.shape[0]
    ET = 324
    GT = 4
    EG = ET // GT
    ER, PADV = ET // 3, 5000
    HID = W1.shape[1]
    HC = HID // 128
    HALF = D // 2
    NE, _, FH = w1.shape
    FC = FH // 128
    SB = 17
    SLOTS = SB * 128
    SHIFT = 60.0
    assert ET * 128 >= E and SB == (N + NE * 127) // 128 and PADV > N
    assert N == P * BLK and BLK == 2 * PAIRS and D == 128 * K and M == 256 and DH == 64 and HEADS == 2 * K

    ctx = ExitStack()
    with ctx:
        def sem(name):
            return ctx.enter_context(nc.semaphore(name))

        def sems(name, n):
            return [sem(f"{name}{i}") for i in range(n)]

        ARENA = 212800
        arena = ctx.enter_context(nc.sbuf_tensor("arena", [128, ARENA], mybir.dt.uint8))
        base_off = nc.sbuf_base - ARENA

        def at(name, shape, dt, off):
            size = 2 if dt in (BF16, FP16) else 4
            for n in shape[1:]:
                size *= n
            assert off % 32 == 0 and off + size <= ARENA, (name, off, size)
            return nc.alloc_sbuf_tensor_at(name, shape, dt, offset=base_off + off)

        class Region:

            def __init__(self, start, end):
                self.at, self.end = start, end

            def __call__(self, name, shape, dt):
                size = 2 if dt in (BF16, FP16) else 4
                for n in shape[1:]:
                    size *= n
                place = at(name, shape, dt, self.at)
                self.at += -(-size // 32) * 32
                assert self.at <= self.end, (name, self.at, self.end)
                return place

        O_X = 15360
        O_T = O_X + 60032
        O_V = O_T + 30720
        O_C = O_V + 33024
        O_W = O_C + 60064
        const = Region(0, O_X)
        ident = const("ident", [128, 128], F32)
        ones = const("ones", [128, 128], F32)
        eps5 = const("eps5", [128, 1], F32)
        ind = const("ind", [128, 2], F32)
        stats = const("stats", [128, BLK, 12], F32)
        meanvar = const("meanvar", [128, BLK, 2], F32)
        stdev = const("stdev", [128, BLK], F32)
        rstd = const("rstd", [128, BLK], F32)
        kdiag = const("kdiag", [128, BLK, 2], F32)
        nstab = const("nstab", [128, 2], F32)
        kmax = const("kmax", [128, BLK, 2], F32)
        kneg = const("kneg", [128, BLK, 2], F32)
        kexp = const("kexp", [128, BLK, 2], F32)
        kfac = const("kfac", [128, BLK, 2], F32)
        vsum = const("vsum", [128, 2, DH + 1], F32)
        km = const("km", [128, 2], F32)
        gmx = const("gmx", [128, 1], F32)
        dg = const("dg", [128, 2], F32)
        qmx = const("qmx", [128, 2, 2], F32)
        qbias = const("qbias", [128, 2, 2], F32)
        rden = const("rden", [128, 2, 2], F32)
        qdiag = const("qdiag", [128, BLK, 2], F32)
        tri = const("tri", [128, 128], F32)
        dcol = const("dcol", [128, ET], F32)
        scol = const("scol", [128, ET], F32)
        iota = const("iota", [128, N], FP16)
        zeros = const("zeros", [128, 512], BF16)
        gidx = const("gidx", [16, EG, GT], F32)
        blo = const("blo", [16, 1], F32)
        tmm = const("tmm", [128, 2, 3], F32)
        emax = const("emax", [16, 2], F32)
        elim = const("elim", [16, 3], F32)
        limf = const("limf", [1, 32], F32)
        limi = const("limi", [1, 32], I32)
        bnr = const("bnr", [128, 128], F32)
        bnc = const("bnc", [128, 5, HC], F32)
        bns = const("bns", [128, 3, HC], F32)
        tb = const("tb", [128, 1], F32)
        gmax = const("gmax", [128, 1], F32)
        mrow = const("mrow", [1, 8], F32)
        mbias = const("mbias", [128, 1], F32)

        rw = const("rw", [128, K, NE], F32)
        rb = const("rb", [1, NE], F32)
        logit = const("logit", [128, BLK, NE], F32)
        prob = const("prob", [128, BLK], F32)
        best = const("best", [128, BLK], F32)
        pos = const("pos", [128, BLK], F32)
        quo = const("quo", [128, BLK], F32)
        k128 = const("k128", [128, SB], F32)
        upto = const("upto", [128, SB], F32)
        down = const("down", [128, NE], F32)
        nblk = const("nblk", [128, NE], F32)
        endb = const("endb", [128, NE], F32)
        tokid = const("tokid", [128, BLK], I32)
        idxt = const("idxt", [128, BLK], I32)
        idxy = const("idxy", [128, BLK], I32)
        tok = const("tok", [128, SB], I32)
        expf = const("expf", [1, SB], F32)
        expi = const("expi", [1, SB], I32)

        r_x = Region(O_X, O_T)
        XTh = r_x("XTh", [128, K, N], F32R)
        XTl = r_x("XTl", [128, K, N], F32R)
        attT = at("attT", [128, K, N], F32, O_T)
        r_c = Region(O_C, O_W)
        xin = r_c("xin", [128, BLK, D], F32)
        xn = r_c("xn", [128, 2, D], F32)
        b2row = r_c("b2row", [128, D], F32)
        res = r_c("res", [128, 2, D], F32)
        praw = r_c("praw", [128, 2, 128], F32)
        pscaled = r_c("pscaled", [128, 2 * M], F32)
        edi = r_c("edi", [128, 2, 3, 128], I32)
        edf = r_c("edf", [128, 2, 3, 128], F32)
        emask = r_c("emask", [16, 2, ET], F32)
        r_v = Region(O_V, O_C)
        wraw = r_v("wraw", [128, 3, K, 128], F32)
        wh = r_v("wh", [128, 3, K, 128], F32R)
        wl = r_v("wl", [128, 3, K, 128], F32R)
        V = r_v("V", [128, BLK, 2, DH + 1], F32)
        r_c = Region(O_C, O_W)
        KTh = r_c("KTh", [128, N], F32R)
        KTl = r_c("KTl", [128, N], F32R)
        QTh = r_c("QTh", [128, N], F32R)
        QTl = r_c("QTl", [128, N], F32R)
        VT = r_c("VT", [128, N], F32)
        sq = r_c("sq", [128, N], F32)
        kp = r_c("kp", [128, 2, BLK, M], F32)
        att = r_c("att", [128, BLK, 128], F32)
        r_w = Region(O_W, ARENA)
        qe = r_w("qe", [128, 2, 2, M], F32)
        qpT = r_w("qpT", [128, 2, 2, 2, P], F32)
        ctxs = r_w("ctxs", [128, 2, 2, DH + 1], F32)
        projh = r_w("projh", [128, 2 * M], F32R)
        projl = r_w("projl", [128, 2 * M], F32R)

        CT = at("CT", [128, BLK, N], F32R, O_C)
        crow = at("crow", [128, 2, N], F32, O_C + 50016)
        r_w = Region(O_W, ARENA)
        ohs = r_w("ohs", [128, GT, N], BF16)
        ohd = r_w("ohd", [128, GT, 128], BF16)
        r_v = Region(O_V, O_V + 3 * 9216)
        woh = r_v("woh", [128, K, HALF], F32R)
        wol = r_v("wol", [128, K, HALF], F32R)
        woraw = r_v("woraw", [128, K, HALF], F32)
        atth = at("atth", [128, 2, K, P], F32R, O_C + 50016)
        attl = at("attl", [128, 2, K, P], F32R, O_W)
        rtile = at("rtile", [128, 2, HALF], F32, O_W + 8192)

        r_t = Region(O_T, O_C)
        parts = [[r_t(f"{n}{u}", [128, BLK, 128], F32R) for n in ("Eh", "El", "Mh", "Ml")] for u in range(2)]
        Ef = r_t("Ef", [128, BLK, 128], F32)
        msg = r_t("msg", [128, 2, BLK, 128], F32)
        w1raw = r_t("w1raw", [128, 2, K, 128], F32)
        r_w = Region(O_W, ARENA)
        rec = r_w("rec", [128, N], F32)
        agg = r_w("agg", [128, N], F32)

        r_t = Region(O_T, O_T + 12288)
        w1h = r_t("w1h", [128, 2, K, 128], F32R)
        w1l = r_t("w1l", [128, 2, K, 128], F32R)
        HT = at("HT", [128, HC, N], F32, O_C)
        w2h = [at("w2h0", [128, HC, HALF], F32R, O_T + 12288), at("w2h1", [128, HC, HALF], F32R, O_X)]
        w2l = [at("w2l0", [128, HC, HALF], F32R, O_T + 30720), at("w2l1", [128, HC, HALF], F32R, O_X + 18432)]
        hth = [at("hth0", [128, HC, P], F32R, O_T + 49152), at("hth1", [128, HC, P], F32R, O_X + 36864)]
        htl = [at("htl0", [128, HC, P], F32R, O_T + 55168), at("htl1", [128, HC, P], F32R, O_X + 42880)]
        w2raw = at("w2raw", [128, 2, 3, HALF], F32, O_W)
        rtile2 = at("rtile2", [128, 2, HALF], F32, O_W + 9216)
        x1 = at("x1", [128, BLK, D], F32, O_T + 12288)
        xn2 = at("xn2", [128, 2, D], F32, O_T + 43008)
        r_x = Region(O_X + 49152, O_T)
        xn2T = r_x("xn2T", [128, 2, K, P], F32)
        stats2 = r_x("stats2", [128, BLK, 12], F32)
        mv2 = r_x("mv2", [128, BLK, 2], F32)
        sd2 = r_x("sd2", [128, BLK], F32)
        cmpk = r_x("cmpk", [128, BLK, 16], F32)
        cmpe = r_x("cmpe", [128, NE, BLK], F32)
        cmpb = r_x("cmpb", [1, SB, NE], F32)
        sume = r_x("sume", [128, BLK, NE], F32)
        onehot = r_x("onehot", [128, BLK, NE], F32)
        carry = r_x("carry", [128, BLK + 1, NE], F32)

        w12raw = [at("w12raw0", [128, K, 2 * FH], F32, O_X), None]
        w3raw = [at("w3raw0", [128, FC, D], F32, O_X + 12288), None]
        w12h = [at("w12h0", [128, K, 2 * FH], F32R, O_X + 18432), None]
        w12l = [at("w12l0", [128, K, 2 * FH], F32R, O_X + 30720), None]
        w3h = [at("w3h0", [128, FC, D], F32R, O_X + 43008), None]
        w3l = [at("w3l0", [128, FC, D], F32R, O_T), None]
        r_f = Region(O_T + 49152, ARENA)
        w12raw[1] = r_f("w12raw1", [128, K, 2 * FH], F32)
        w3raw[1] = r_f("w3raw1", [128, FC, D], F32)
        w12h[1] = r_f("w12h1", [128, K, 2 * FH], F32R)
        w12l[1] = r_f("w12l1", [128, K, 2 * FH], F32R)
        w3h[1] = r_f("w3h1", [128, FC, D], F32R)
        w3l[1] = r_f("w3l1", [128, FC, D], F32R)
        xg = r_f("xg", [128, 2, D], F32)
        xgh = r_f("xgh", [128, 2, K, 128], F32R)
        xgl = r_f("xgl", [128, 2, K, 128], F32R)
        gate = r_f("gate", [128, FH], F32)
        hid = r_f("hid", [128, FH], F32)
        hidh = r_f("hidh", [128, FC, 128], F32R)
        hidl = r_f("hidl", [128, FC, 128], F32R)
        yb = r_f("yb", [128, 2, D], BF16)
        yg = r_f("yg", [128, 2, D], BF16)

        PS = ctx.enter_context(nc.psum_tensor("PS", [128, 4096], F32))
        PA = PS[:, 0:1536]
        PB = PS[:, 1536:3072]

        def bank(i):
            return PS[:, 512 * i:512 * (i + 1)]

        xn_d = nc.dram_tensor("xn_scratch", (N, D), F32).ap()
        res_d = nc.dram_tensor("res_scratch", (N, D), F32).ap()

        def blocks(ap):
            return ap.rearrange("(b p) d -> p b d", p=P)

        x_b, xn_b, res_b = blocks(x), blocks(xn_d), blocks(res_d)

        tok_d = nc.dram_tensor("token_of_slot", (SLOTS, 1), I32).ap()
        xn2_d = nc.dram_tensor("xn2_scratch", (N, D), F32).ap()
        y_d = nc.dram_tensor("expert_out_scratch", (SLOTS, D), BF16).ap()

        def cols_by_k(w):
            return w.rearrange("(k p) n -> p k n", p=128)

        s_x = sems("s_x", PAIRS)
        s_cst = sem("s_cst")
        s_par = sem("s_par")
        s_pre = sem("s_pre")
        EDGE_COLS, BN_ROWS, EDGE_ROWS, LIMITS, PROJ_T, MAX_T, STAB = range(1, 8)
        s_prd = sem("s_prd")
        EDGE_F, EDGE_COL_D, EDGE_MM, EDGE_EL, BN_D, LIM_I, PROJ_D, GMAX_D, MROW_D, STAB_D = 1, 3, 5, 6, 7, 8, 9, 10, 11, 12
        s_var = sem("s_var")
        s_sd = sem("s_sd")
        s_xn = sem("s_xn")
        s_xt = sem("s_xt")
        s_xth = sem("s_xth")
        s_xtl = sem("s_xtl")
        s_res = sem("s_res")
        s_xst = sems("s_xst", 2)
        s_rst = sems("s_rst", 2)
        c_dve = sem("c_dve")
        c_pool = sem("c_pool")

        s_turn = sem("s_turn")
        s_wl = sem("s_wl")
        s_wsp = sem("s_wsp")
        s_w0h = sem("s_w0h")
        s_wok = sem("s_wok")
        s_kps = sem("s_kps")
        s_kh = sem("s_kh")
        s_kl = sem("s_kl")
        s_vps = sem("s_vps")
        s_vt = sem("s_vt")
        s_qps = sem("s_qps")
        s_qh = sem("s_qh")
        s_ql = sem("s_ql")
        s_kd = sem("s_kd")
        s_kdc = sem("s_kdc")
        s_kdg = sem("s_kdg")
        s_ksum = sem("s_ksum")
        s_kmT = sem("s_kmT")
        s_dg = sem("s_dg")
        s_stb = sem("s_stb")
        s_kb = sem("s_kb")
        s_ke = sem("s_ke")
        s_stc = sem("s_stc")
        s_kf = sem("s_kf")
        s_vtp = sem("s_vtp")
        s_v = sem("s_v")
        s_cx = sem("s_cx")
        s_cxs = sem("s_cxs")
        s_qdg = sem("s_qdg")
        s_qd = sem("s_qd")
        s_qb = sem("s_qb")
        s_qe = sem("s_qe")
        s_qt = sem("s_qt")
        s_qp = sem("s_qp")
        s_o = sem("s_o")
        s_at = sem("s_at")
        s_aT = sem("s_aT")
        s_as = sem("s_as")
        s_out = sem("s_out")
        s_pad = sem("s_pad")
        s_e = sem("s_e")
        s_bnv = sem("s_bnv")
        s_oh = sems("s_oh", 2)
        s_ohf = sems("s_ohf", 2)
        s_cn = sem("s_cn")
        s_cr = sem("s_cr")
        s_ct = sem("s_ct")
        s_cs = sem("s_cs")
        s_wor = sem("s_wor")
        s_woh = sem("s_woh")
        s_wol = sem("s_wol")
        s_ath = sem("s_ath")
        s_atl = sem("s_atl")
        s_ow = sem("s_ow")
        s_rl = sems("s_rl", 2)
        s_ro = sem("s_ro")
        s_rs = sems("s_rs", 2)
        s_ml = sems("s_ml", 2)
        s_ms = sem("s_ms")
        s_ex = sem("s_ex")
        s_eh = sem("s_eh")
        s_mm = sem("s_mm")
        s_mh = sem("s_mh")
        s_ep = sem("s_ep")
        s_sum = sem("s_sum")
        s_sumr = sem("s_sumr")
        s_ag = sem("s_ag")
        s_agh = sem("s_agh")
        s_agl = sem("s_agl")
        s_w1r = sems("s_w1r", 2)
        s_w1h = sem("s_w1h")
        s_w1l = sem("s_w1l")
        s_z = sem("s_z")
        s_h = sem("s_h")
        s_w2r = sems("s_w2r", 2)
        s_w2h = sem("s_w2h")
        s_w2l = sem("s_w2l")
        s_hth = sem("s_hth")
        s_htl = sem("s_htl")
        s_o2 = sem("s_o2")
        s_r2l = sems("s_r2l", 2)
        s_r2 = sem("s_r2")
        s_r2s = sems("s_r2s", 2)
        s_x1l = sem("s_x1l")
        s_v2 = sem("s_v2")
        s_sd2 = sem("s_sd2")
        s_xn2 = sem("s_xn2")
        s_xn2s = sems("s_xn2s", 2)
        s_x2t = sem("s_x2t")
        s_x2s = sem("s_x2s")
        s_rw = sem("s_rw")
        s_lg = sem("s_lg")
        s_lgs = sem("s_lgs")
        s_se = sem("s_se")
        s_route = sem("s_route")
        SHIFTED, ONE_HOT, EXPERTS, SLOTS_D = range(1, 5)
        s_rk = sem("s_rk")
        s_ts = sem("s_ts")
        s_tl = sem("s_tl")
        s_fr = sems("s_fr", 2)
        s_f3r = sems("s_f3r", 2)
        s_fh = sem("s_fh")
        s_fl = sem("s_fl")
        s_f3h = sem("s_f3h")
        s_f3 = sem("s_f3")
        s_g = sems("s_g", 2)
        s_gt = sem("s_gt")
        s_gh = sem("s_gh")
        s_gl = sem("s_gl")
        s_up = sem("s_up")
        s_sg = sem("s_sg")
        s_hd = sem("s_hd")
        s_ht = sem("s_ht")
        s_hh = sem("s_hh")
        s_hl = sem("s_hl")
        s_y = sem("s_y")
        s_yb = sem("s_yb")
        s_ys = sems("s_ys", 2)
        s_yg = sems("s_yg", 2)
        s_fin = sem("s_fin")

        def turn_limits(eng):
            return [0] + [eng.value_load(limi[0:1, BLK + b:BLK + b + 1], min_val=b + 1, max_val=(b + 1) * EG) for b in range(BLK)]

        block = ctx.enter_context(nc.Block())

        @block.sync
        def _(sp):
            for i in range(PAIRS):
                sp.dma_start(xin[0:112, 2 * i:2 * i + 2, :], x_b[0:112, 2 * i:2 * i + 2, :]).then_inc(s_x[i], 16)
                sp.dma_start(xin[112:P, 2 * i:2 * i + 2, :], x_b[112:P, 2 * i:2 * i + 2, :]).then_inc(s_x[i], 16)
            sp.wait_ge(s_pad, 1)
            for i, e in enumerate((dst, src)):
                full = E // 128 - 2 * ER
                sp.dma_start(edi[0:ER, i, 0:2], e[0:2 * ER * 128].rearrange("(g r e) -> r g e", g=2, r=ER)).then_inc(s_e, 16)
                sp.dma_start(edi[0:full, i, 2], e[2 * ER * 128:E // 128 * 128].rearrange("(r e) -> r e", e=128)).then_inc(s_e, 16)
                sp.dma_start(edi[full:full + 1, i, 2, 0:E % 128], e[E // 128 * 128:E].rearrange("(a e) -> a e", a=1)).then_inc(s_e, 16)

            def load_w2(i):
                if i >= 2:
                    sp.wait_ge(s_w2l, i - 1)
                sp.dma_start(w2raw[:, i % 2], cols_by_k(W2)[:, 3 * (i % 4):3 * (i % 4) + 3, HALF * (i // 4):HALF * (i // 4) + HALF])\
                    .then_inc(s_w2r[i % 2], 16)

            with sp.Fori(0, HP) as j:
                sp.wait_ge(s_wsp, j + 1)
                for n, w in enumerate((Wk, Wv, Wq)):
                    sp.dma_start(wraw[:, n], cols_by_k(w)[:, :, bass.ds(j * 128, 128)]).then_inc(s_wl, 16)
            sp.wait_ge(s_cst, 16)
            sp.dma_start(tok_d.rearrange("(p b) o -> p (b o)", b=SB), zeros[:, 0:2 * SB].bitcast(I32)).then_inc(s_rw, 16)
            sp.dma_start(rw[:], router_w.rearrange("(k p) e -> p k e", p=128)).then_inc(s_rw, 16)
            sp.dma_start(rb[:], router_b.rearrange("(a e) -> a e", a=1)).then_inc(s_rw, 16)
            for i in range(2):
                sp.wait_ge(s_rst[i], 32 * PAIRS)
            sp.wait_ge(s_qps, 3 * HP)
            sp.dma_start(woraw[:], cols_by_k(Wo)[:, :, 0:HALF]).then_inc(s_wor, 16)

            def residual(n, tile, landed, stored):
                if n < 2 * BLK:
                    h, b = n // BLK, n % BLK
                    if n >= 2:
                        sp.wait_ge(stored[n % 2], 16 * (n // 2))
                    sp.dma_start(tile[0:P, n % 2], res_b[:, b, HALF * h:HALF * h + HALF]).then_inc(landed[n % 2], 16)

            sp.wait_ge(s_as, HP * BLK)
            residual(0, rtile, s_rl, s_rs)
            for n in range(2 * BLK):
                h, b = n // BLK, n % BLK
                if n == 1:
                    sp.wait_ge(s_wol, 1)
                    sp.dma_start(woraw[:], cols_by_k(Wo)[:, :, HALF:D]).then_inc(s_wor, 16)
                residual(n + 1, rtile, s_rl, s_rs)
                sp.wait_ge(s_ro, n + 1)
                sp.dma_start(res_b[:, b, HALF * h:HALF * h + HALF], rtile[0:P, n % 2]).then_inc(s_rs[n % 2], 16)
            for i in range(2):
                sp.wait_ge(s_xst[i], 32 * PAIRS)
            sp.wait_ge(s_ow, 2 * BLK)
            for c in range(K):
                if c >= 2:
                    sp.wait_ge(s_ep, c - 1)
                sp.dma_start(msg[0:P, c % 2], xn_b[:, :, 128 * c:128 * c + 128]).then_inc(s_ml[c % 2], 16)
                if c < 2:
                    sp.dma_start(w1raw[:, c], cols_by_k(W1)[:, :, 128 * c:128 * c + 128]).then_inc(s_w1r[c], 16)
            for m in range(2, HC):
                sp.wait_ge(s_w1l, m - 1)
                sp.dma_start(w1raw[:, m % 2], cols_by_k(W1)[:, :, 128 * m:128 * m + 128]).then_inc(s_w1r[m % 2], 16)
                if m == 4:
                    for i in range(2):
                        load_w2(i)
                if 5 <= m < 7:
                    load_w2(m - 3)
            for i in range(2):
                sp.wait_ge(s_rs[i], 16 * BLK)
            for i in range(4, 6):
                load_w2(i)

            def store_norm2(b):
                sp.wait_ge(s_xn2, b + 1)
                sp.dma_start(blocks(xn2_d)[:, b], xn2[0:P, b % 2]).then_inc(s_xn2s[b % 2], 16)

            residual(0, rtile2, s_r2l, s_r2s)
            for n in range(2 * BLK):
                h, b = n // BLK, n % BLK
                if n in (1, 2):
                    load_w2(n + 5)
                if h == 0:
                    residual(n + 1, rtile2, s_r2l, s_r2s)
                elif n + 1 < 2 * BLK:
                    sp.wait_ge(s_r2, n)
                    sp.dma_start(rtile2[0:P, (n + 1) % 2], res_b[:, b + 1, HALF:D]).then_inc(s_r2l[(n + 1) % 2], 16)
                if n >= BLK + 3:
                    store_norm2(n - BLK - 3)
                if h == 0:
                    sp.wait_ge(s_r2, n + 1)
                    sp.dma_start(res_b[:, b, 0:HALF], rtile2[0:P, n % 2]).then_inc(s_r2s[n % 2], 16)
                if n == BLK:
                    for i in range(2):
                        sp.wait_ge(s_r2s[i], 16 * (BLK // 2))
                    sp.wait_ge(s_o2, BLK)
                    sp.dma_start(x1[0:P, :, 0:HALF], res_b[:, :, 0:HALF]).then_inc(s_x1l, 16)
            for b in range(BLK - 3, BLK):
                store_norm2(b)
            sp.wait_ge(s_route, EXPERTS)

            def load_expert(n, u, again=True):
                e = nc.sync.value_load(expi[0:1, bass.ds(n, 1)], min_val=0, max_val=NE - 1)
                if again:
                    sp.wait_ge(s_fl, n - 1)
                sp.dma_start(w12raw[u][:, :, 0:FH], w1[bass.ds(e, 1)].rearrange("a (k p) h -> p (a k) h", p=128)).then_inc(s_fr[u], 16)
                sp.dma_start(w12raw[u][:, :, FH:2 * FH], w2[bass.ds(e, 1)].rearrange("a (k p) h -> p (a k) h", p=128)).then_inc(s_fr[u], 16)
                if again:
                    sp.wait_ge(s_f3, n - 1)
                sp.dma_start(w3raw[u][:], w3[bass.ds(e, 1)].rearrange("a (k p) h -> p (a k) h", p=128)).then_inc(s_f3r[u], 16)

            for u in range(2):
                load_expert(u, u, again=False)
            with sp.Fori(1, SB // 2) as i:
                for u in range(2):
                    load_expert(i * 2 + u, u)
            load_expert(SB - 1, 0)
            for b in range(BLK):
                sp.wait_ge(s_fin, b + 1)
                sp.dma_start(blocks(out)[0:112, b], x1[0:112, b]).then_inc(s_out, 16)
                sp.dma_start(blocks(out)[112:P, b], x1[112:P, b]).then_inc(s_out, 16)
            sp.wait_ge(s_out, 32 * BLK)

        @block.gpsimd
        def _(pool):
            chain = Chain(pool, c_pool)
            nc.gpsimd.memset(ident[:], 0.0).then_inc(c_pool, 1)
            nc.gpsimd.memset(ones[:], 1.0).then_inc(c_pool, 1)
            nc.gpsimd.iota(iota[:], [[1, N]], base=0, channel_multiplier=0, allow_small_or_imprecise_dtypes=True).then_inc(s_cst, 1)
            nc.gpsimd.iota(gidx[:], [[1, EG], [0, GT]], base=0, channel_multiplier=0, allow_small_or_imprecise_dtypes=True).then_inc(s_cst, 1)
            nc.gpsimd.iota(blo[:], [[0, 1]], base=0, channel_multiplier=P, allow_small_or_imprecise_dtypes=True).then_inc(s_cst, 1)
            nc.gpsimd.memset(zeros[:], 0.0).then_inc(s_cst, 1)
            nc.gpsimd.iota(k128[:], [[128, SB]], base=0, channel_multiplier=0, allow_small_or_imprecise_dtypes=True).then_inc(s_cst, 1)
            nc.gpsimd.iota(upto[:], [[1, SB]], base=0, channel_multiplier=0, allow_small_or_imprecise_dtypes=True).then_inc(s_cst, 1)
            nc.gpsimd.iota(down[:], [[-1, NE]], base=NE, channel_multiplier=0, allow_small_or_imprecise_dtypes=True).then_inc(s_cst, 1)
            nc.gpsimd.iota(tokid[:], [[P, BLK]], base=0, channel_multiplier=1).then_inc(s_cst, 1)
            nc.gpsimd.memset(eps5[:], 1e-5).then_inc(s_cst, 1)
            nc.gpsimd.memset(vsum[:, :, DH:DH + 1], RATIO * EPS * BLK).then_inc(s_cst, 1)
            pool.wait_ge(c_pool, 2)
            nc.gpsimd.affine_select(out=ident[:], in_=ident[:], compare_op=ALU.not_equal, fill=1.0, base=0,
                                    pattern=[[-1, 128]], channel_multiplier=1).then_inc(s_cst, 1)
            nc.gpsimd.affine_select(out=tri[:], in_=ones[:], compare_op=ALU.is_gt, fill=0.0, base=0,
                                    pattern=[[1, 128]], channel_multiplier=-1).then_inc(s_cst, 1)
            pool.sem_inc(s_wsp, 1)
            pool.wait_ge(s_par, 144)
            chain.at(2)
            for b in range(BLK):
                pool.wait_ge(s_xn, b + 1)
                if b >= 2:
                    pool.wait_ge(s_rst[b % 2], 32 * (b // 2))
                chain(nc.gpsimd.tensor_tensor(res[0:P, b % 2], xin[0:P, b], xn[0:P, b % 2], ALU.add))
                nc.gpsimd.tensor_tensor(res[0:P, b % 2], res[0:P, b % 2], b2row[0:P, :], ALU.add).then_inc(s_res, 1)
            pool.wait_ge(s_wok, 1)
            pool.sem_inc(s_wsp, 1)
            with pool.Fori(1, HP) as j:
                pool.wait_ge(s_wl, 48 * j + 48)
                pool.wait_ge(s_qps, 3 * j)
                pool.sem_inc(s_turn, 1)
                chain.at(1 + BLK + j)
                chain(nc.gpsimd.tensor_copy(wh[:], wraw[:]))
                nc.gpsimd.tensor_tensor(wl[:], wraw[:], wh[:].bitcast(F32), ALU.subtract).then_inc(s_wok, 1)
                pool.wait_ge(s_wok, j + 1)
                pool.sem_inc(s_wsp, 1)
            pool.wait_ge(s_wor, 16)
            nc.gpsimd.tensor_copy(woh[:], woraw[:]).then_inc(s_woh, 1)
            pool.wait_ge(s_woh, 1)
            nc.gpsimd.tensor_tensor(wol[:], woraw[:], woh[:].bitcast(F32), ALU.subtract).then_inc(s_wol, 1)
            for c in range(K):
                u = c % 2
                pool.wait_ge(s_eh, c + 1)
                nc.gpsimd.tensor_tensor(parts[u][1][0:P], Ef[0:P], parts[u][0][0:P].bitcast(F32), ALU.subtract)
                pool.wait_ge(s_mh, c + 1)
                nc.gpsimd.tensor_tensor(parts[u][3][0:P], msg[0:P, u], parts[u][2][0:P].bitcast(F32), ALU.subtract).then_inc(s_ep, 1)
            pool.wait_ge(s_rw, 48)
            pool.wait_ge(s_route, SLOTS_D)
            for b in range(BLK):
                nc.gpsimd.indirect_dma_start(out=tok_d, out_offset=bass.IndirectOffsetOnAxis(ap=idxt[0:P, b:b + 1], axis=0),
                                             in_=tokid[0:P, b:b + 1], in_offset=None).then_inc(s_ts, 16)
            pool.wait_ge(s_ts, 16 * BLK)
            pool.dma_start(tok[:], tok_d.rearrange("(p b) o -> p (b o)", b=SB)).then_inc(s_tl, 16)
            for i in range(2):
                pool.wait_ge(s_xn2s[i], 16 * PAIRS)
            pool.wait_ge(s_tl, 16)

            def gather(n):
                if n < SB:
                    if n >= 2:
                        pool.wait_ge(s_gt, n - 1)
                    nc.gpsimd.indirect_dma_start(out=xg[:, n % 2, :], out_offset=None, in_=xn2_d,
                                                 in_offset=bass.IndirectOffsetOnAxis(ap=tok[:, n:n + 1], axis=0)).then_inc(s_g[n % 2], 16)

            gather(0)
            for n in range(SB):
                u = n % 2
                gather(n + 1)
                pool.wait_ge(s_f3h, n + 1)
                nc.gpsimd.tensor_tensor(w3l[u][:], w3raw[u][:], w3h[u][:].bitcast(F32), ALU.subtract).then_inc(s_f3, 1)
            for i in range(2):
                pool.wait_ge(s_ys[i], 16 * (SB // 2 + 2 - i))
            for b in range(BLK):
                if b >= 2:
                    pool.wait_ge(s_fin, b - 1)
                nc.gpsimd.indirect_dma_start(out=yg[0:P, b % 2, :], out_offset=None, in_=y_d,
                                             in_offset=bass.IndirectOffsetOnAxis(ap=idxy[0:P, b:b + 1], axis=0)).then_inc(s_yg[b % 2], 16)

        @block.scalar
        def _(act):
            act.dma_start(b2row[0:P, :], b2.rearrange("(a n) -> a n", a=1).to_broadcast([P, D])).then_inc(s_par, 16)
            for dup in range(2):
                act.dma_start(praw[:, :, 64 * dup:64 * dup + 64], proj.rearrange("(c p) d -> p c d", p=128)).then_inc(s_par, 16)
            for i, row in enumerate((gamma, beta, mean, var, b1)):
                act.dma_start(bnr[HC * i:HC * i + HC, :], row.rearrange("(a n) -> a n", n=128)).then_inc(s_par, 16)
            act.dma_start(tb[:], t.rearrange("(a n) -> a n", a=1).to_broadcast([128, 1])).then_inc(s_par, 16)
            act.wait_ge(s_cst, 16)

            def deviation(h):
                act.wait_ge(s_var, PAIRS * (h + 1))
                nc.scalar.activation(stdev[0:P, PAIRS * h:PAIRS * (h + 1)], meanvar[0:P, PAIRS * h:PAIRS * (h + 1), 1],
                                     ACT.Sqrt, bias=eps5[0:P, :]).then_inc(s_sd, 1)

            def store(b):
                act.wait_ge(s_xn, b + 1)
                act.dma_start(xn_b[0:112, b], xn[0:112, b % 2]).then_inc(s_xst[b % 2], 16)
                act.dma_start(xn_b[112:P, b], xn[112:P, b % 2]).then_inc(s_xst[b % 2], 16)

            def store_res(b):
                act.wait_ge(s_res, b + 1)
                act.dma_start(res_b[0:112, b], res[0:112, b % 2]).then_inc(s_rst[b % 2], 16)
                act.dma_start(res_b[112:P, b], res[112:P, b % 2]).then_inc(s_rst[b % 2], 16)

            deviation(0)
            for b in range(BLK):
                if b == PAIRS:
                    deviation(1)
                    act.wait_ge(s_pre, BN_ROWS)
                    nc.scalar.activation(bns[:, 0, :], bank(7)[:, 3 * HC:4 * HC], ACT.Sqrt, bias=eps5[:]).then_inc(s_bnv, 1)
                store(b)
                for i in range(2):
                    act.wait_ge(s_xt, 2 * b + i + 1)
                    nc.scalar.activation(XTh[:, 3 * i:3 * i + 3, P * b:P * b + P],
                                         bank(2 * (b % 2) + i)[:, 0:375].rearrange("p (k n) -> p k n", k=3),
                                         ACT.Copy).then_inc(s_xth, 1)
                if b >= 1:
                    store_res(b - 1)
                if b == 6:
                    act.wait_ge(s_wl, 48)
                    nc.scalar.activation(wh[:], wraw[:], ACT.Copy).then_inc(s_w0h, 1)
            store_res(BLK - 1)
            for i in range(2):
                act.wait_ge(s_xst[i], 32 * PAIRS)
                act.wait_ge(s_rst[i], 32 * PAIRS)

            def norm2(b):
                act.wait_ge(s_v2, b + 1)
                nc.scalar.activation(sd2[0:P, b:b + 1], mv2[0:P, b, 1:2], ACT.Sqrt, bias=eps5[0:P, :]).then_inc(s_sd2, 1)

            def put_norm2(b):
                act.wait_ge(s_x2t, b + 1)
                if b >= 2:
                    act.wait_ge(s_lg, b - 1)
                for c in range(2):
                    ins = nc.scalar.activation(xn2T[:, b % 2, 3 * c:3 * c + 3], bank(2 + c)[:, 0:375].rearrange("p (k n) -> p k n", k=3),
                                               ACT.Copy)
                ins.then_inc(s_x2s, 1)

            with act.Fori(0, HP) as j:
                act.wait_ge(s_vps, 3 * j + 3)
                nc.scalar.activation(VT[:], PA[:, 0:N], ACT.Copy).then_inc(s_vt, 1)
                for n, (c0, c1) in enumerate(BANKS):
                    act.wait_ge(s_kps, 3 * j + n + 1)
                    nc.scalar.activation(KTh[:, c0:c1], PB[:, c0:c1], ACT.Copy)
                    nc.scalar.activation(sq[:, c0:c1], PB[:, c0:c1], ACT.Square).then_inc(s_kh, 1)
                for b in range(BLK):
                    act.wait_ge(s_kb, BLK * j + b + 1)
                    for a in range(2):
                        ins = nc.scalar.activation(kp[0:P, a, b, :], bank(6 + b % 2)[0:P, M * a:M * a + M], ACT.Exp,
                                                   bias=kneg[0:P, b, a:a + 1])
                    ins.then_inc(s_ke, 1)
                act.wait_ge(s_kdg, j + 1)
                for n, (c0, c1) in enumerate(BANKS):
                    act.wait_ge(s_qps, 3 * j + n + 1)
                    nc.scalar.activation(QTh[:, c0:c1], PB[:, c0:c1], ACT.Copy)
                    nc.scalar.activation(sq[:, c0:c1], PB[:, c0:c1], ACT.Square).then_inc(s_qh, 1)
                    if n == 1:
                        act.wait_ge(s_stc, j + 1)
                        for a in range(2):
                            ins = nc.scalar.activation(kfac[0:P, :, a], kexp[0:P, :, a], ACT.Exp, bias=nstab[0:P, a:a + 1])
                        ins.then_inc(s_kf, 1)

                def put_attT(b):
                    act.wait_ge(s_aT, BLK * j + b + 1)
                    nc.scalar.activation(attT[:, bass.ds(j, 1), P * b:P * b + P],
                                         bank(4 + b % 2)[:, 0:P].rearrange("p (a n) -> p a n", a=1),
                                         ACT.Copy).then_inc(s_as, 1)

                for u in range(BLK):
                    act.wait_ge(s_qb, BLK * j + u + 1)
                    if u >= 2:
                        act.wait_ge(s_qt, BLK * j + u - 1)
                    for a in range(2):
                        ins = nc.scalar.activation(qe[0:P, u % 2, a, :], bank(6 + u % 2)[0:P, M * a:M * a + M],
                                                   ACT.Exp, bias=qbias[0:P, u % 2, a:a + 1])
                    ins.then_inc(s_qe, 1)
                    if u == 1:
                        act.wait_ge(s_cx, j + 1)
                        nc.scalar.activation(ctxs[:], bank(3)[:, 0:260].rearrange("p (a c d) -> p a c d", a=2, c=2),
                                             ACT.Copy).then_inc(s_cxs, 1)
                    if u >= 6:
                        put_attT(u - 6)
                for b in range(BLK - 6, BLK):
                    put_attT(b)

            def put_counts(b):
                for i in range(3):
                    n = min(4, BLK - 4 * i)
                    act.wait_ge(s_ct, 3 * b + i + 1)
                    nc.scalar.activation(CT[0:P, 4 * i:4 * i + n, P * b:P * b + P],
                                         bank(6 + (3 * b + i) % 2)[0:P, 0:P * n].rearrange("p (s n) -> p s n", s=n),
                                         ACT.Copy).then_inc(s_cs, 1)

            for n in range(2 * BLK):
                b = n % BLK
                if n == BLK:
                    act.wait_ge(s_wor, 32)
                    act.wait_ge(s_ow, BLK)
                    nc.scalar.activation(woh[:], woraw[:], ACT.Copy).then_inc(s_woh, 1)
                if n >= 2:
                    act.wait_ge(s_ow, n - 1)
                nc.scalar.activation(atth[:, n % 2], attT[:, :, P * b:P * b + P], ACT.Copy).then_inc(s_ath, 1)

            def exponentials(c):
                if c >= K:
                    return
                u = c % 2
                act.wait_ge(s_ms, c + 1)
                if c >= 1:
                    act.wait_ge(s_ep, c)
                nc.scalar.activation(Ef[0:P], msg[0:P, u], ACT.Exp, bias=mbias[0:P, :], scale=tb[0:P, :]).then_inc(s_ex, 1)
                if c >= 2:
                    act.wait_ge(s_sum, 2 * (c - 1))
                act.wait_ge(s_ex, c + 1)
                nc.scalar.activation(parts[u][0][0:P], Ef[0:P], ACT.Copy).then_inc(s_eh, 1)
                act.wait_ge(s_mm, c + 1)
                nc.scalar.activation(parts[u][2][0:P], msg[0:P, u], ACT.Copy).then_inc(s_mh, 1)

            act.wait_ge(s_prd, STAB_D)
            act.wait_ge(s_ow, 2 * BLK)
            exponentials(0)
            exponentials(1)
            for b in range(BLK):
                act.wait_ge(s_cn, b + 1)
                if b >= 2:
                    act.wait_ge(s_ct, 3 * (b - 1))
                nc.scalar.activation(crow[0:P, b % 2, :], PS[0:P, 1536 * (b % 2):1536 * (b % 2) + N], ACT.Copy).then_inc(s_cr, 1)
                if b >= 1:
                    put_counts(b - 1)
            put_counts(BLK - 1)
            for c in range(K):
                if c >= 1:
                    exponentials(c + 1)
                act.wait_ge(s_ag, c + 1)
                nc.scalar.activation(XTh[:, c, :], agg[:], ACT.Copy).then_inc(s_agh, 1)

            def w1_parts(m):
                if m < HC:
                    act.wait_ge(s_w1r[m % 2], 16 * (m // 2 + 1))
                    if m < 2:
                        act.wait_ge(s_sum, 2 * (K - 1))
                    else:
                        act.wait_ge(s_z, m - 1)
                    nc.scalar.activation(w1h[:, m % 2], w1raw[:, m % 2], ACT.Copy).then_inc(s_w1h, 1)

            def w2_parts(i):
                act.wait_ge(s_w2r[i % 2], 16 * (i // 2 + 1))
                nc.scalar.activation(w2h[i // 4][:, 3 * (i % 4):3 * (i % 4) + 3, :], w2raw[:, i % 2], ACT.Copy).then_inc(s_w2h, 1)

            w1_parts(0)
            for m in range(HC):
                w1_parts(m + 1)
                act.wait_ge(s_z, m + 1)
                nc.scalar.activation(HT[:, m, :], PS[:, 1536 * (m % 2):1536 * (m % 2) + N], ACT.Relu,
                                     bias=bns[:, 2, m:m + 1], scale=bns[:, 1, m:m + 1]).then_inc(s_h, 1)
                if 4 <= m < 8:
                    w2_parts(m - 4)

            def hidden_parts(n):
                if n < 2 * BLK:
                    b = n % BLK
                    if n >= 2:
                        act.wait_ge(s_o2, n - 1)
                    nc.scalar.activation(hth[n % 2][:], HT[:, :, P * b:P * b + P], ACT.Copy).then_inc(s_hth, 1)

            act.wait_ge(s_h, HC)
            hidden_parts(0)
            hidden_parts(1)
            for i in range(4, 8):
                w2_parts(i)
                hidden_parts(i - 2)
            for n in range(6, 2 * BLK):
                hidden_parts(n)
                if n >= BLK + 2:
                    norm2(n - BLK - 2)
                if n >= BLK + 5:
                    put_norm2(n - BLK - 5)
            norm2(BLK - 2)
            norm2(BLK - 1)
            for b in range(BLK - 5, BLK):
                put_norm2(b)
            act.wait_ge(s_route, SHIFTED)
            nc.scalar.activation(sume[0:P], sume[0:P], ACT.Exp).then_inc(s_se, 1)

            def expert_parts(n, u, i):
                act.wait_ge(s_fr[u], i * 32 + 32)
                act.wait_ge(s_up, n + 1)
                nc.scalar.activation(w12h[u][:], w12raw[u][:], ACT.Copy).then_inc(s_fh, 1)

            def expert_down_parts(n, u, i):
                act.wait_ge(s_f3r[u], i * 16 + 16)
                act.wait_ge(s_y, n + 1)
                nc.scalar.activation(w3h[u][:], w3raw[u][:], ACT.Copy).then_inc(s_f3h, 1)

            def rows_parts(n, u):
                act.wait_ge(s_gt, n + 1)
                act.wait_ge(s_up, n + 1)
                for c in range(2):
                    ins = nc.scalar.activation(xgh[:, u, 3 * c:3 * c + 3], bank(c)[:, 0:384].rearrange("p (k n) -> p k n", k=3), ACT.Copy)
                ins.then_inc(s_gh, 1)

            def expert(n, u):
                act.wait_ge(s_up, n + 3)
                nc.scalar.activation(gate[:], bank(2)[:, 0:FH], ACT.Silu).then_inc(s_sg, 1)

            def expert_hidden(n, u):
                act.wait_ge(s_ht, n + 1)
                act.wait_ge(s_y, n + 2)
                nc.scalar.activation(hidh[:], bank(3)[:, 0:FH].rearrange("p (k n) -> p k n", k=FC), ACT.Copy).then_inc(s_hh, 1)

            def expert_out(n, u, i):
                act.wait_ge(s_y, n + 3)
                act.wait_ge(s_ys[u], i * 16 + 16)
                for c in range(2):
                    ins = nc.scalar.activation(yb[:, u, HALF * c:HALF * c + HALF], bank(4 + c)[:, 0:HALF], ACT.Copy)
                ins.then_inc(s_yb, 1)
                act.wait_ge(s_yb, n + 1)
                act.dma_start(y_d.rearrange("(b p) d -> p b d", p=128)[:, bass.ds(n, 1), :], yb[:, u:u + 1, :]).then_inc(s_ys[u], 16)

            for i in range(2):
                act.sem_inc(s_ys[i], 16)

            def expert_turn(n, u, i, last=False):
                if not last:
                    expert_parts(n + 1, 1 - u, i + 1 if u else i)
                expert(n, u)
                if not last:
                    rows_parts(n + 1, 1 - u)
                expert_out(n - 1, 1 - u, i if u else i - 1)
                expert_hidden(n, u)
                if not last:
                    expert_down_parts(n + 1, 1 - u, i + 1 if u else i)

            expert_parts(0, 0, 0)
            expert_down_parts(0, 0, 0)
            rows_parts(0, 0)
            expert_parts(1, 1, 0)
            expert(0, 0)
            rows_parts(1, 1)
            expert_hidden(0, 0)
            expert_down_parts(1, 1, 0)
            expert_turn(1, 1, 0)
            with act.Fori(1, SB // 2) as i:
                for u in range(2):
                    expert_turn(i * 2 + u, u, i)
            expert_turn(SB - 1, 0, SB // 2, last=True)
            expert_out(SB - 1, 0, SB // 2)

        @block.vector
        def _(dve):
            chain = Chain(dve, c_dve)
            for a in range(2):
                for c in range(2):
                    nc.vector.memset(ind[64 * a:64 * a + 64, c:c + 1], 0.5 * NORM * NORM if a == c else 0.0).then_inc(s_cst, 1)

            nc.vector.memset(edi[:], PADV).then_inc(s_pad, 1)

            def edges_to_float():
                dve.wait_ge(s_e, 96)
                nc.vector.tensor_copy(edf[0:ER], edi[0:ER]).then_inc(s_prd, 1)

            def edge_columns():
                dve.wait_ge(s_pre, EDGE_COLS)
                for i in range(2):
                    nc.vector.tensor_copy((dcol, scol)[i][:], bank(4 + i)[:, 0:ET]).then_inc(s_prd, 1)
                nc.vector.tensor_reduce(tmm[0:ER, 0, :], edf[0:ER, 0], X_AXIS, ALU.min).then_inc(s_prd, 1)
                nc.vector.tensor_reduce(tmm[0:ER, 1, :], edf[0:ER, 0], X_AXIS, ALU.max).then_inc(s_prd, 1)

            def edge_ranges():
                dve.wait_ge(s_pre, EDGE_ROWS)
                chain(nc.vector.tensor_scalar(emask[0:BLK, 0], bank(5)[0:BLK, 0:ET], blo[0:BLK], None, ALU.is_ge))
                chain(nc.vector.tensor_scalar(emask[0:BLK, 1], bank(4)[0:BLK, 0:ET], blo[0:BLK], float(P), ALU.subtract, ALU.is_lt))
                chain(nc.vector.tensor_tensor(emask[0:BLK, 0], emask[0:BLK, 0], emask[0:BLK, 1], ALU.mult))
                g = gidx[0:BLK].rearrange("p g t -> p (g t)")
                chain(nc.vector.scalar_tensor_tensor(out=emask[0:BLK, 1], in0=g, scalar=1.0, in1=emask[0:BLK, 0],
                                                     op0=ALU.add, op1=ALU.mult))
                chain(nc.vector.reduce_max(emax[0:BLK, 0:1], emask[0:BLK, 1], X_AXIS))
                chain(nc.vector.tensor_scalar(emask[0:BLK, 1], g, -1.0, float(EG), ALU.mult, ALU.add))
                chain(nc.vector.tensor_tensor(emask[0:BLK, 1], emask[0:BLK, 1], emask[0:BLK, 0], ALU.mult))
                chain(nc.vector.reduce_max(emax[0:BLK, 1:2], emask[0:BLK, 1], X_AXIS))
                chain(nc.vector.tensor_scalar(elim[0:BLK, 1:2], emax[0:BLK, 0:1], 1.0, None, ALU.max))
                chain(nc.vector.tensor_scalar(elim[0:BLK, 0:1], emax[0:BLK, 1:2], -1.0, float(EG), ALU.mult, ALU.add))
                chain(nc.vector.tensor_scalar(elim[0:BLK, 2:3], elim[0:BLK, 1:2], -1.0, None, ALU.add))
                chain(nc.vector.tensor_tensor(elim[0:BLK, 0:1], elim[0:BLK, 0:1], elim[0:BLK, 2:3], ALU.min))
                nc.vector.tensor_tensor(elim[0:BLK, 2:3], elim[0:BLK, 1:2], elim[0:BLK, 0:1], ALU.subtract).then_inc(s_prd, 1)

            def edge_limits():
                dve.wait_ge(s_pre, LIMITS)
                chain(nc.vector.tensor_copy(limf[0:1, 0:30], bank(7)[0:1, 64:94]))
                chain(nc.vector.tensor_tensor(limf[0:1, 20:30], limf[0:1, 20:30], limf[0:1, 0:10], ALU.subtract))
                nc.vector.tensor_copy(limi[0:1, 0:30], limf[0:1, 0:30]).then_inc(s_prd, 1)

            def batch_norm():
                dve.wait_ge(s_bnv, 1)
                chain(nc.vector.tensor_copy(bnc[:], bank(7)[:, 0:5 * HC].rearrange("p (a c) -> p a c", a=5)))
                chain(nc.vector.reciprocal(bns[:, 0, :], bns[:, 0, :]))
                chain(nc.vector.tensor_tensor(bns[:, 1, :], bns[:, 0, :], bnc[:, 0, :], ALU.mult))
                chain(nc.vector.tensor_tensor(bnc[:, 4, :], bnc[:, 4, :], bnc[:, 2, :], ALU.subtract))
                chain(nc.vector.tensor_tensor(bnc[:, 4, :], bnc[:, 4, :], bns[:, 1, :], ALU.mult))
                nc.vector.tensor_tensor(bns[:, 2, :], bnc[:, 4, :], bnc[:, 1, :], ALU.add).then_inc(s_prd, 1)

            def normalise(b):
                if b >= 2:
                    dve.wait_ge(s_xst[b % 2], 32 * (b // 2))
                    dve.wait_ge(s_res, b - 1)
                    dve.wait_ge(s_xt, 2 * (b - 1))
                nc.vector.tensor_scalar(xn[0:P, b % 2], xin[0:P, b], meanvar[0:P, b, 0:1], rstd[0:P, b:b + 1],
                                        ALU.subtract, ALU.mult).then_inc(s_xn, 1)

            def low_parts(b):
                for i in range(2):
                    dve.wait_ge(s_xth, 2 * b + i + 1)
                    nc.vector.tensor_tensor(XTl[:, 3 * i:3 * i + 3, P * b:P * b + P],
                                            bank(2 * (b % 2) + i)[:, 0:375].rearrange("p (k n) -> p k n", k=3),
                                            XTh[:, 3 * i:3 * i + 3, P * b:P * b + P].bitcast(F32),
                                            ALU.subtract).then_inc(s_xtl, 1)

            for h in range(2):
                for b in range(PAIRS * h, PAIRS * (h + 1)):
                    dve.wait_ge(s_x[b // 2], 32)
                    for i in range(2):
                        chain(nc.vector.bn_stats(stats[0:P, b, 6 * i:6 * i + 6], xin[0:P, b, 384 * i:384 * i + 384]))
                    nc.vector.bn_aggr(meanvar[0:P, b, :], stats[0:P, b, :]).then_inc(s_var, 1)
                dve.wait_ge(s_sd, h + 1)
                chain(nc.vector.reciprocal(rstd[0:P, PAIRS * h:PAIRS * (h + 1)], stdev[0:P, PAIRS * h:PAIRS * (h + 1)]))
                for b in range(PAIRS * h, PAIRS * (h + 1)):
                    normalise(b)
                    if b >= 1:
                        low_parts(b - 1)
                    {0: edges_to_float, 2: edge_columns, 4: edge_ranges, 6: batch_norm, 7: edge_limits}.get(b, lambda: None)()
            low_parts(BLK - 1)
            dve.wait_ge(s_w0h, 1)
            nc.vector.tensor_tensor(wl[:], wraw[:], wh[:].bitcast(F32), ALU.subtract).then_inc(s_wok, 1)
            dve.wait_ge(s_pre, PROJ_T)
            chain(nc.vector.memset(pscaled[:], 0.0))
            for a in range(2):
                chain(nc.vector.tensor_scalar(pscaled[64 * a:64 * a + 64, M * a:M * a + M], bank(6)[64 * a:64 * a + 64, 0:M],
                                              NORM, None, ALU.mult))
            chain(nc.vector.tensor_copy(projh[:], pscaled[:]))
            nc.vector.tensor_tensor(projl[:], pscaled[:], projh[:].bitcast(F32), ALU.subtract).then_inc(s_prd, 1)
            dve.wait_ge(s_prd, PROJ_D)
            nc.vector.reduce_max(gmax[:], XTh[:].bitcast(F32).rearrange("p k n -> p (k n)"), X_AXIS).then_inc(s_prd, 1)

            def route():
                grid = [P, BLK, NE]
                dve.wait_ge(s_lgs, 1)
                chain(nc.vector.reduce_max(best[0:P], logit[0:P], X_AXIS))
                chain(nc.vector.tensor_tensor(logit[0:P], logit[0:P], best[0:P].unsqueeze(2).to_broadcast(grid), ALU.subtract))
                nc.vector.tensor_copy(sume[0:P], logit[0:P]).then_inc(s_route, 1)
                chain(nc.vector.tensor_scalar(logit[0:P], logit[0:P], 0.0, None, ALU.is_equal))
                chain(nc.vector.tensor_tensor(logit[0:P], logit[0:P], down[0:P].unsqueeze(1).to_broadcast(grid), ALU.mult))
                chain(nc.vector.reduce_max(best[0:P], logit[0:P], X_AXIS))
                nc.vector.tensor_tensor(onehot[0:P], logit[0:P], best[0:P].unsqueeze(2).to_broadcast(grid), ALU.is_equal).then_inc(s_route, 1)
                dve.wait_ge(s_se, 1)
                chain(nc.vector.reduce_sum(prob[0:P], sume[0:P], X_AXIS))
                chain(nc.vector.reciprocal(prob[0:P], prob[0:P]))
                dve.wait_ge(s_rk, 1)
                chain(nc.vector.memset(carry[0:P, 0], 0.0))
                for b in range(BLK):
                    chain(nc.vector.tensor_tensor(carry[0:P, b + 1], carry[0:P, b], bank(6)[0:P, NE * b:NE * b + NE], ALU.add))
                chain(nc.vector.tensor_tensor(cmpe[0:P], carry[0:P, BLK].unsqueeze(2).to_broadcast([P, NE, BLK]),
                                              k128[0:P, 0:BLK].unsqueeze(1).to_broadcast([P, NE, BLK]), ALU.is_gt))
                chain(nc.vector.reduce_sum(nblk[0:P], cmpe[0:P], X_AXIS))
                chain(nc.vector.tensor_copy(endb[0:P, 0:1], nblk[0:P, 0:1]))
                for e in range(1, NE):
                    chain(nc.vector.tensor_tensor(endb[0:P, e:e + 1], endb[0:P, e - 1:e], nblk[0:P, e:e + 1], ALU.add))
                chain(nc.vector.tensor_tensor(cmpb[:], upto[0:1].unsqueeze(2).to_broadcast([1, SB, NE]),
                                              endb[0:1].unsqueeze(1).to_broadcast([1, SB, NE]), ALU.is_ge))
                chain(nc.vector.reduce_sum(expf[:], cmpb[:], X_AXIS))
                chain(nc.vector.tensor_scalar(expf[:], expf[:], float(NE - 1), None, ALU.min))
                nc.vector.tensor_copy(expi[:], expf[:]).then_inc(s_route, 1)
                chain(nc.vector.tensor_tensor(nblk[0:P], endb[0:P], nblk[0:P], ALU.subtract))
                chain(nc.vector.tensor_scalar(nblk[0:P], nblk[0:P], 128.0, None, ALU.mult))
                chain(nc.vector.tensor_tensor(sume[0:P], bank(5)[0:P, 0:BLK * NE].rearrange("p (b e) -> p b e", b=BLK), carry[0:P, 0:BLK], ALU.add))
                chain(nc.vector.tensor_tensor(sume[0:P], sume[0:P], nblk[0:P].unsqueeze(1).to_broadcast(grid), ALU.add))
                chain(nc.vector.tensor_tensor(sume[0:P], sume[0:P], onehot[0:P], ALU.mult))
                chain(nc.vector.reduce_sum(pos[0:P], sume[0:P], X_AXIS))
                chain(nc.vector.tensor_copy(idxy[0:P], pos[0:P]))
                chain(nc.vector.tensor_tensor(cmpk[0:P], pos[0:P].unsqueeze(2).to_broadcast([P, BLK, SB - 1]),
                                              k128[0:P, 1:SB].unsqueeze(1).to_broadcast([P, BLK, SB - 1]), ALU.is_ge))
                chain(nc.vector.reduce_sum(quo[0:P], cmpk[0:P], X_AXIS))
                chain(nc.vector.tensor_scalar(quo[0:P], quo[0:P], 1.0 - 128.0 * SB, None, ALU.mult))
                chain(nc.vector.scalar_tensor_tensor(out=pos[0:P], in0=pos[0:P], scalar=float(SB), in1=quo[0:P], op0=ALU.mult, op1=ALU.add))
                nc.vector.tensor_copy(idxt[0:P], pos[0:P]).then_inc(s_route, 1)

            def stabiliser():
                dve.wait_ge(s_pre, MAX_T)
                chain(nc.vector.reduce_max(mrow[0:1, 0:1], bank(7)[0:1, 0:128], X_AXIS))
                chain(nc.vector.tensor_scalar(mrow[0:1, 1:2], mrow[0:1, 0:1], 0.0, 1e-7, ALU.max, ALU.add))
                chain(nc.vector.tensor_tensor(mrow[0:1, 2:3], mrow[0:1, 1:2], tb[0:1, :], ALU.mult))
                chain(nc.vector.scalar_tensor_tensor(out=mrow[0:1, 3:4], in0=tb[0:1, :], scalar=1e-7, in1=mrow[0:1, 2:3],
                                                     op0=ALU.mult, op1=ALU.max))
                nc.vector.tensor_scalar(mrow[0:1, 4:5], mrow[0:1, 3:4], -1.0, SHIFT, ALU.mult, ALU.add).then_inc(s_prd, 1)

            first = chain.n
            PER = 6 + 3 * BLK

            with dve.Fori(0, HP) as j:
                chain.at(j * PER + first)

                def low_bank(low, high, ready, done, n):
                    c0, c1 = BANKS[n]
                    dve.wait_ge(ready, 3 * j + n + 1)
                    nc.vector.tensor_tensor(low[:, c0:c1], PB[:, c0:c1], high[:, c0:c1].bitcast(F32), ALU.subtract).then_inc(done, 1)

                for n in range(3):
                    low_bank(KTl, KTh, s_kh, s_kl, n)
                for u in range(BLK):
                    dve.wait_ge(s_kd, BLK * j + u + 1)
                    chain(nc.vector.reduce_max(kmax[0:P, u], bank(6 + u % 2)[0:P, :].rearrange("p (a m) -> p a m", a=2), X_AXIS))
                    nc.vector.tensor_scalar(kneg[0:P, u], kmax[0:P, u], -1.0, None, ALU.mult).then_inc(s_kb, 1)
                chain(nc.vector.reduce_max(km[0:P], kmax[0:P].rearrange("p b a -> p a b"), X_AXIS))
                nc.vector.sem_inc(s_ksum, 1)
                dve.wait_ge(s_kdg, j + 1)
                nc.vector.tensor_copy(kdiag[0:P], bank(5)[0:P, 256:276].rearrange("p (b a) -> p b a", a=2)).then_inc(s_kdc, 1)
                dve.wait_ge(s_kdc, j + 1)
                chain(nc.vector.tensor_tensor(kexp[0:P], kmax[0:P], kdiag[0:P], ALU.subtract))
                dve.wait_ge(s_vtp, j + 1)
                chain(nc.vector.reduce_sum(vsum[0:P, :, 0:DH], PA[0:P, 0:1280].rearrange("p (b a d) -> p a d b", b=BLK, a=2), X_AXIS))
                chain(nc.vector.tensor_scalar(vsum[0:P, :, 0:DH], vsum[0:P, :, 0:DH], RATIO * EPS, None, ALU.mult))
                low_bank(QTl, QTh, s_qh, s_ql, 0)
                dve.wait_ge(s_kmT, j + 1)
                chain(nc.vector.reduce_max(gmx[0:2, :], bank(6)[0:2, 0:P], X_AXIS))
                nc.vector.tensor_scalar(dg[0:2, :], ident[0:2, 0:2], gmx[0:2, :], None, ALU.mult).then_inc(s_dg, 1)
                low_bank(QTl, QTh, s_qh, s_ql, 1)
                dve.wait_ge(s_stb, j + 1)
                nc.vector.tensor_scalar(nstab[0:P, :], bank(7)[0:P, 0:2], -1.0, None, ALU.mult).then_inc(s_stc, 1)
                dve.wait_ge(s_kf, j + 1)
                for b0, b1 in ((0, 8), (8, BLK)):
                    nc.vector.scalar_tensor_tensor(out=V[0:P, b0:b1, :, 0:DH],
                                                   in0=PA[0:P, 128 * b0:128 * b1].rearrange("p (b a d) -> p b a d", b=b1 - b0, a=2),
                                                   scalar=RATIO, in1=kfac[0:P, b0:b1].unsqueeze(3).to_broadcast([P, b1 - b0, 2, DH]),
                                                   op0=ALU.mult, op1=ALU.mult)
                nc.vector.tensor_scalar(V[0:P, :, :, DH], kfac[0:P], RATIO, None, ALU.mult).then_inc(s_v, 1)
                low_bank(QTl, QTh, s_qh, s_ql, 2)
                dve.wait_ge(s_qdg, j + 1)
                chain(nc.vector.tensor_copy(qdiag[0:P], bank(5)[0:P, 256:276].rearrange("p (b a) -> p b a", a=2)))

                def bias(u):
                    dve.wait_ge(s_qd, BLK * j + u + 1)
                    chain(nc.vector.reduce_max(qmx[0:P, u % 2], bank(6 + u % 2)[0:P, :].rearrange("p (a m) -> p a m", a=2), X_AXIS))
                    nc.vector.scalar_tensor_tensor(out=qbias[0:P, u % 2, :], in0=qmx[0:P, u % 2], scalar=-1.0,
                                                   in1=qdiag[0:P, u, :], op0=ALU.mult,
                                                   op1=ALU.subtract).then_inc(s_qb, 1)

                def features(u):
                    dve.wait_ge(s_qt, BLK * j + u + 1)
                    if u >= 2:
                        dve.wait_ge(s_o, BLK * j + u - 1)
                    nc.vector.tensor_scalar(qpT[:, u % 2], bank(1 + u % 2)[:, 0:4 * P].rearrange("p (a c n) -> p a c n", a=2, c=2),
                                            EPS, RATIO, ALU.add, ALU.mult).then_inc(s_qp, 1)

                def normal(u):
                    o = bank(3 * (u % 2))[0:P, 0:130].rearrange("p (a d) -> p a d", a=2)
                    dve.wait_ge(s_o, BLK * j + u + 1)
                    chain(nc.vector.reciprocal(rden[0:P, u % 2], o[:, :, DH]))
                    nc.vector.tensor_tensor(att[0:P, u, :].rearrange("p (a d) -> p a d", a=2), o[:, :, 0:DH],
                                            rden[0:P, u % 2].unsqueeze(2).to_broadcast([P, 2, DH]), ALU.mult).then_inc(s_at, 1)

                for u in range(BLK + 4):
                    if u < BLK:
                        bias(u)
                    if 2 <= u < BLK + 2:
                        features(u - 2)
                    if u >= 4:
                        normal(u - 4)
                assert chain.n == PER, (chain.n, PER)
            chain.at(first + HP * PER)
            stabiliser()

            for n in range(2 * BLK + 2):
                if n == 4:
                    dve.wait_ge(s_pre, STAB)
                    nc.vector.tensor_copy(mbias[:], bank(7)[:, 0:1]).then_inc(s_prd, 1)
                if n == BLK:
                    dve.wait_ge(s_woh, 2)
                    nc.vector.tensor_tensor(wol[:], woraw[:], woh[:].bitcast(F32), ALU.subtract).then_inc(s_wol, 1)
                if n < 2 * BLK:
                    b = n % BLK
                    dve.wait_ge(s_ath, n + 1)
                    nc.vector.tensor_tensor(attl[:, n % 2], attT[:, :, P * b:P * b + P], atth[:, n % 2].bitcast(F32),
                                            ALU.subtract).then_inc(s_atl, 1)
                if n >= 2:
                    o = n - 2
                    dve.wait_ge(s_ow, o + 1)
                    dve.wait_ge(s_rl[o % 2], 16 * (o // 2 + 1))
                    nc.vector.tensor_tensor(rtile[0:P, o % 2], rtile[0:P, o % 2], bank(o % 2)[0:P, 0:HALF], ALU.add).then_inc(s_ro, 1)

            def exponentials(c):
                if c >= K:
                    return
                u = c % 2
                if c == 0:
                    dve.wait_ge(s_ow, 2 * BLK)
                dve.wait_ge(s_ml[u], 16 * (c // 2 + 1))
                nc.vector.tensor_scalar(msg[0:P, u], msg[0:P, u], 0.0, 1e-7, ALU.max, ALU.add).then_inc(s_ms, 1)
                dve.wait_ge(s_ex, c + 1)
                nc.vector.tensor_tensor(msg[0:P, u], Ef[0:P], msg[0:P, u], ALU.mult).then_inc(s_mm, 1)

            exponentials(0)
            exponentials(1)
            for i in range(2):
                dve.wait_ge(s_rs[i], 16 * BLK)
            turns = turn_limits(nc.vector)
            offsets = [nc.vector.value_load(limi[0:1, 2 * BLK + b:2 * BLK + b + 1], min_val=-b * EG, max_val=EG) for b in range(BLK)]
            for b in range(BLK):
                with dve.Fori(turns[b], turns[b + 1]) as n:
                    g = nc.s_assert_within(n + offsets[b], 0, EG - 1, skip_runtime_bounds_check_because="turns map to groups first .. end - 1 of the block, all within the list")
                    for h in range(2):
                        dve.wait_ge(s_ohf[h], n + 1)
                        for u in range(GT // 2 * h, GT // 2 * (h + 1)):
                            nc.vector.tensor_scalar(ohd[:, u, 0:P], iota[:, P * b:P * b + P], dcol[:, bass.ds(g * GT + u, 1)], None, ALU.is_equal)
                            ins = nc.vector.tensor_scalar(ohs[:, u, :], iota[:], scol[:, bass.ds(g * GT + u, 1)], None, ALU.is_equal)
                        ins.then_inc(s_oh[h], 1)

            for c in range(K):
                if c >= 1:
                    exponentials(c + 1)
                dve.wait_ge(s_sum, 2 * c + 1)
                chain(nc.vector.tensor_scalar(rec[:], PS[:, 0:N], 1e-37, None, ALU.max))
                nc.vector.sem_inc(s_sumr, 1)
                chain(nc.vector.reciprocal(rec[:], rec[:]))
                dve.wait_ge(s_sum, 2 * c + 2)
                chain(nc.vector.tensor_tensor(agg[:], PS[:, 1536:1536 + N], rec[:], ALU.mult))
                nc.vector.sem_inc(s_sumr, 1)
                chain(nc.vector.tensor_tensor(agg[:], agg[:], XTh[:, c, :].bitcast(F32), ALU.add))
                nc.vector.tensor_tensor(agg[:], agg[:], XTl[:, c, :].bitcast(F32), ALU.add).then_inc(s_ag, 1)
                dve.wait_ge(s_agh, c + 1)
                nc.vector.tensor_tensor(XTl[:, c, :], agg[:], XTh[:, c, :].bitcast(F32), ALU.subtract).then_inc(s_agl, 1)
                dve.wait_ge(s_agl, c + 1)

            def w1_parts(m):
                if m < HC:
                    dve.wait_ge(s_w1h, m + 1)
                    nc.vector.tensor_tensor(w1l[:, m % 2], w1raw[:, m % 2], w1h[:, m % 2].bitcast(F32), ALU.subtract).then_inc(s_w1l, 1)

            def w2_parts(i):
                k = 3 * (i % 4)
                dve.wait_ge(s_w2h, i + 1)
                nc.vector.tensor_tensor(w2l[i // 4][:, k:k + 3, :], w2raw[:, i % 2], w2h[i // 4][:, k:k + 3, :].bitcast(F32),
                                        ALU.subtract).then_inc(s_w2l, 1)

            for m in range(HC):
                w1_parts(m)
                if 5 <= m < 9:
                    w2_parts(m - 5)

            def hidden_parts(n):
                if n < 2 * BLK:
                    b = n % BLK
                    dve.wait_ge(s_hth, n + 1)
                    nc.vector.tensor_tensor(htl[n % 2][:], HT[:, :, P * b:P * b + P], hth[n % 2][:].bitcast(F32), ALU.subtract).then_inc(s_htl, 1)

            def second_layer(n):
                h, b = n // BLK, n % BLK
                dve.wait_ge(s_o2, n + 1)
                dve.wait_ge(s_r2l[n % 2], 16 * (n // 2 + 1))
                where = rtile2[0:P, n % 2] if h == 0 else x1[0:P, b, HALF:D]
                nc.vector.tensor_tensor(where, rtile2[0:P, n % 2], bank(n % 2)[0:P, 0:HALF], ALU.add).then_inc(s_r2, 1)

            def norm2(b):
                if b == 0:
                    dve.wait_ge(s_x1l, 16)
                dve.wait_ge(s_r2, BLK + b + 1)
                for i in range(2):
                    chain(nc.vector.bn_stats(stats2[0:P, b, 6 * i:6 * i + 6], x1[0:P, b, HALF * i:HALF * i + HALF]))
                nc.vector.bn_aggr(mv2[0:P, b, :], stats2[0:P, b, :]).then_inc(s_v2, 1)

            def apply_norm2(b):
                dve.wait_ge(s_sd2, b + 1)
                chain(nc.vector.reciprocal(sd2[0:P, b:b + 1], sd2[0:P, b:b + 1]))
                if b >= 2:
                    dve.wait_ge(s_xn2s[b % 2], 16 * (b // 2))
                    dve.wait_ge(s_x2t, b - 1)
                nc.vector.tensor_scalar(xn2[0:P, b % 2], x1[0:P, b], mv2[0:P, b, 0:1], sd2[0:P, b:b + 1],
                                        ALU.subtract, ALU.mult).then_inc(s_xn2, 1)

            hidden_parts(0)
            hidden_parts(1)
            for i in range(4, 8):
                w2_parts(i)
                second_layer(i - 4)
                hidden_parts(i - 2)
            for n in range(6, 2 * BLK + 2):
                hidden_parts(n)
                second_layer(n - 2)
                if n >= BLK + 2:
                    norm2(n - BLK - 2)
                if n >= BLK + 3:
                    apply_norm2(n - BLK - 3)
            apply_norm2(BLK - 1)
            dve.wait_ge(s_lg, BLK)
            nc.vector.tensor_copy(logit[0:P], bank(4)[0:P, 0:NE * BLK].rearrange("p (b e) -> p b e", b=BLK)).then_inc(s_lgs, 1)
            route()

            def expert_parts(n, u):
                dve.wait_ge(s_fh, n + 1)
                nc.vector.tensor_tensor(w12l[u][:], w12raw[u][:], w12h[u][:].bitcast(F32), ALU.subtract).then_inc(s_fl, 1)

            def rows_parts(n, u):
                dve.wait_ge(s_gh, n + 1)
                for c in range(2):
                    ins = nc.vector.tensor_tensor(xgl[:, u, 3 * c:3 * c + 3], bank(c)[:, 0:384].rearrange("p (k n) -> p k n", k=3),
                                                  xgh[:, u, 3 * c:3 * c + 3].bitcast(F32), ALU.subtract)
                ins.then_inc(s_gl, 1)

            def expert_gate(n):
                dve.wait_ge(s_sg, n + 1)
                nc.vector.tensor_tensor(hid[:], gate[:], bank(2)[:, FH:2 * FH], ALU.mult).then_inc(s_hd, 1)

            def expert_hidden(n):
                dve.wait_ge(s_hh, n + 1)
                nc.vector.tensor_tensor(hidl[:], bank(3)[:, 0:FH].rearrange("p (k n) -> p k n", k=FC), hidh[:].bitcast(F32),
                                        ALU.subtract).then_inc(s_hl, 1)

            def expert_turn(n, u, i, last=False):
                if not last:
                    expert_parts(n + 1, 1 - u)
                expert_gate(n)
                if not last:
                    rows_parts(n + 1, 1 - u)
                expert_hidden(n)

            expert_parts(0, 0)
            rows_parts(0, 0)
            with dve.Fori(0, SB // 2) as i:
                for u in range(2):
                    expert_turn(i * 2 + u, u, i)
            expert_turn(SB - 1, 0, SB // 2, last=True)
            for b in range(BLK):
                dve.wait_ge(s_yg[b % 2], 16 * (b // 2 + 1))
                nc.vector.scalar_tensor_tensor(out=x1[0:P, b], in0=yg[0:P, b % 2], scalar=prob[0:P, b:b + 1], in1=x1[0:P, b],
                                               op0=ALU.mult, op1=ALU.add).then_inc(s_fin, 1)

        @block.tensor
        def _(pe):
            pe.wait_ge(s_cst, 16)
            for b in range(BLK):
                pe.wait_ge(s_xn, b + 1)
                for i in range(2):
                    if b >= 2:
                        pe.wait_ge(s_xtl, 2 * (b - 2) + i + 1)
                    for c in range(3):
                        ins = nc.tensor.transpose(bank(2 * (b % 2) + i)[:, P * c:P * c + P],
                                                  xn[0:P, b % 2, 384 * i + 128 * c:384 * i + 128 * c + 128], ident[0:P, 0:P])
                    ins.then_inc(s_xt, 1)
                if b == 1:
                    pe.wait_ge(s_prd, EDGE_F)
                    for i in range(2):
                        for g in range(3):
                            ins = nc.tensor.transpose(bank(4 + i)[:, ER * g:ER * g + ER], edf[0:ER, i, g, :], ident[0:ER, 0:ER])
                    ins.then_inc(s_pre, 1)
                    pe.wait_ge(s_par, 144)
                    nc.tensor.transpose(bank(7)[:, 0:5 * HC], bnr[0:5 * HC, :], ident[0:5 * HC, 0:5 * HC]).then_inc(s_pre, 1)
                if b == 3:
                    pe.wait_ge(s_prd, EDGE_MM)
                    for i in range(2):
                        for g in range(3):
                            ins = nc.tensor.matmul(bank(4 + i)[0:BLK, ER * g:ER * g + ER], tmm[0:ER, i, g:g + 1].to_broadcast([ER, BLK]),
                                                   ident[0:ER, 0:ER], start=True, stop=True)
                    ins.then_inc(s_pre, 1)
                if b == 6:
                    pe.wait_ge(s_prd, EDGE_EL)
                    pe.wait_ge(s_prd, BN_D)
                    nc.tensor.matmul(bank(7)[0:1, 64:64 + BLK], elim[0:BLK, 2:3], tri[0:BLK, 0:BLK], start=True, stop=True)
                    nc.tensor.matmul(bank(7)[0:1, 64 + BLK:64 + 2 * BLK], elim[0:BLK, 2:3], tri[0:BLK, 0:BLK], start=True, stop=False)
                    nc.tensor.matmul(bank(7)[0:1, 64 + BLK:64 + 2 * BLK], elim[0:BLK, 2:3], ident[0:BLK, 0:BLK], start=False, stop=True)
                    ins = nc.tensor.matmul(bank(7)[0:1, 64 + 2 * BLK:64 + 3 * BLK], elim[0:BLK, 0:1], ident[0:BLK, 0:BLK], start=True, stop=True)
                    ins.then_inc(s_pre, 1)
            pe.wait_ge(s_par, 144)
            for c in range(2):
                ins = nc.tensor.transpose(bank(6)[:, 128 * c:128 * c + 128], praw[:, c, :], ident[:])
            ins.then_inc(s_pre, 1)
            pe.wait_ge(s_xtl, 2 * BLK)
            pe.wait_ge(s_prd, PROJ_D)

            def project(j, n, where, done, i):
                c0, c1 = BANKS[i]
                for k in range(K):
                    for w, xt in ((wh, XTh), (wh, XTl), (wl, XTh)):
                        ins = nc.tensor.matmul(where[:, c0:c1], w[:, n, k, :], xt[:, k, c0:c1],
                                               start=(k == 0 and w is wh and xt is XTh), stop=(k == K - 1 and w is wl))
                ins.then_inc(done, 1)

            def head_pair(j, last):
                def dash(u, th, tl):
                    for q, w in ((th, projh), (th, projl), (tl, projh)):
                        ins = nc.tensor.matmul(bank(6 + u % 2)[0:P, :], q[:, P * u:P * u + P], w[:],
                                               start=(q is th and w is projh), stop=(q is tl))
                    return ins

                def diag():
                    for b in range(BLK):
                        ins = nc.tensor.matmul(bank(5)[0:P, 256 + 2 * b:258 + 2 * b], sq[:, P * b:P * b + P], ind[:], start=True, stop=True)
                    return ins

                def context(a):
                    for c in range(2):
                        g = 2 * a + c
                        for b in range(BLK):
                            nc.tensor.matmul(bank(3)[:, 65 * g:65 * g + 65], kp[0:P, a, b, 128 * c:128 * c + 128], V[0:P, b, a, :],
                                             start=(b == 0), stop=False)
                        ins = nc.tensor.matmul(bank(3)[:, 65 * g:65 * g + 65], ones[0:P, :], vsum[0:P, a, :], start=False, stop=True)
                    return ins

                def turn(u):
                    pe.wait_ge(s_qe, BLK * j + u + 1)
                    for a in range(2):
                        for c in range(2):
                            g = 2 * a + c
                            ins = nc.tensor.transpose(bank(1 + u % 2)[:, P * g:P * g + P], qe[0:P, u % 2, a, 128 * c:128 * c + 128], ident[0:P, 0:P])
                    ins.then_inc(s_qt, 1)

                def attend(u):
                    pe.wait_ge(s_qp, BLK * j + u + 1)
                    if u >= 2:
                        pe.wait_ge(s_at, BLK * j + u - 1)
                    if u == 0:
                        pe.wait_ge(s_cxs, j + 1)
                    for a in range(2):
                        for c in range(2):
                            ins = nc.tensor.matmul(bank(3 * (u % 2))[0:P, 65 * a:65 * a + 65], qpT[:, u % 2, a, c, :], ctxs[:, a, c, :], start=(c == 0), stop=(c == 1))
                    ins.then_inc(s_o, 1)

                def turn_att(b):
                    pe.wait_ge(s_at, BLK * j + b + 1)
                    if b == 1:
                        pe.wait_ge(s_qb, BLK * j + 1)
                    if b >= 2:
                        pe.wait_ge(s_as, BLK * j + b - 1)
                    nc.tensor.transpose(bank(4 + b % 2)[:, 0:P], att[0:P, b, :], ident[0:P, 0:P]).then_inc(s_aT, 1)

                def step(u):
                    if u < BLK:
                        pe.wait_ge(s_qe, BLK * j + u - 1)
                        dash(u, QTh, QTl).then_inc(s_qd, 1)
                    if u - 2 < BLK:
                        turn(u - 2)
                    if 0 <= u - 3 < BLK:
                        attend(u - 3)
                    if u >= 5:
                        turn_att(u - 5)

                for i in range(3):
                    project(j, 0, PB, s_kps, i)
                pe.wait_ge(s_vt, j + 1)
                for b in range(BLK):
                    ins = nc.tensor.transpose(PA[0:P, 128 * b:128 * b + 128], VT[:, P * b:P * b + P], ident[:])
                ins.then_inc(s_vtp, 1)
                for u in range(BLK):
                    if u % 4 == 0:
                        pe.wait_ge(s_kl, 3 * j + u // 4 + 1)
                    if u >= 2:
                        pe.wait_ge(s_ke, BLK * j + u - 1)
                    dash(u, KTh, KTl).then_inc(s_kd, 1)
                diag().then_inc(s_kdg, 1)
                project(j, 2, PB, s_qps, 0)
                pe.wait_ge(s_ksum, j + 1)
                pe.wait_ge(s_ke, BLK * j + BLK)
                nc.tensor.transpose(bank(6)[0:2, 0:P], km[0:P, :], ident[0:P, 0:P]).then_inc(s_kmT, 1)
                project(j, 2, PB, s_qps, 1)
                pe.wait_ge(s_dg, j + 1)
                nc.tensor.matmul(bank(7)[0:P, 0:2], ones[0:2, 0:P], dg[0:2, :], start=True, stop=True).then_inc(s_stb, 1)
                pe.wait_ge(s_kdc, j + 1)
                project(j, 2, PB, s_qps, 2)
                pe.wait_ge(s_stc, j + 1)
                pe.wait_ge(s_ql, 3 * j + 1)
                dash(0, QTh, QTl).then_inc(s_qd, 1)
                dash(1, QTh, QTl).then_inc(s_qd, 1)
                pe.wait_ge(s_v, j + 1)
                context(0)
                pe.wait_ge(s_ql, 3 * j + 3)
                diag().then_inc(s_qdg, 1)
                context(1).then_inc(s_cx, 1)
                for u in range(2, BLK + 3):
                    step(u)
                if not last:
                    pe.wait_ge(s_wok, j + 2)
                    project(j + 1, 1, PA, s_vps, 1)
                turn_att(BLK - 2)
                if not last:
                    project(j + 1, 1, PA, s_vps, 2)
                turn_att(BLK - 1)
                if not last:
                    project(j + 1, 1, PA, s_vps, 0)
                pe.wait_ge(s_as, BLK * j + BLK)

            pe.wait_ge(s_wok, 1)
            for i in range(3):
                project(0, 1, PA, s_vps, i)
            with pe.Fori(0, HP - 1) as j:
                head_pair(j, last=False)
            head_pair(HP - 1, last=True)

            pe.wait_ge(s_prd, GMAX_D)
            nc.tensor.transpose(bank(7)[0:1, 0:128], gmax[:], ident[:]).then_inc(s_pre, 1)
            for n in range(2 * BLK):
                if n == 2:
                    pe.wait_ge(s_prd, MROW_D)
                    nc.tensor.matmul(bank(7)[:, 0:1], ones[0:1, :], mrow[0:1, 4:5], start=True, stop=True).then_inc(s_pre, 1)
                if n % BLK == 0:
                    pe.wait_ge(s_wol, n // BLK + 1)
                pe.wait_ge(s_atl, n + 1)
                if n >= 2:
                    pe.wait_ge(s_ro, n - 1)
                for k in range(K):
                    for q, w in ((atth, woh), (atth, wol), (attl, woh)):
                        ins = nc.tensor.matmul(bank(n % 2)[0:P, 0:HALF], q[:, n % 2, k, :], w[:, k, :],
                                               start=(k == 0 and q is atth and w is woh), stop=(k == K - 1 and q is attl))
                ins.then_inc(s_ow, 1)

            pe.wait_ge(s_ro, 2 * BLK)
            turns = turn_limits(nc.tensor)
            pe.wait_ge(s_prd, STAB_D)
            for u in range(2):
                pe.sem_inc(s_ohf[u], 1)

            def turn_counts(b):
                pe.wait_ge(s_cr, b + 1)
                for i in range(3):
                    if 3 * b + i >= 2:
                        pe.wait_ge(s_cs, 3 * b + i - 1)
                    for c in range(min(4, BLK - 4 * i)):
                        ins = nc.tensor.transpose(bank(6 + (3 * b + i) % 2)[0:P, P * c:P * c + P],
                                                  crow[0:P, b % 2, P * (4 * i + c):P * (4 * i + c) + P], ident[0:P, 0:P])
                    ins.then_inc(s_ct, 1)

            for b in range(BLK):
                if b >= 2:
                    pe.wait_ge(s_cr, b - 1)
                counts = PS[0:P, 1536 * (b % 2):1536 * (b % 2) + 1536]
                for c in range(3):
                    nc.tensor.matmul(counts[:, 512 * c:512 * c + 512], zeros[:, 0:P], zeros[:], start=True, stop=False, skip_group_check=True)
                with pe.Fori(turns[b], turns[b + 1]) as n:
                    for h in range(2):
                        pe.wait_ge(s_oh[h], n + 1)
                        for u in range(GT // 2 * h, GT // 2 * (h + 1)):
                            for c0, c1 in BANKS:
                                ins = nc.tensor.matmul(counts[:, c0:c1], ohd[:, u, 0:P], ohs[:, u, c0:c1], start=False, stop=False,
                                                       skip_group_check=True)
                        ins.then_inc(s_ohf[h], 1)
                for c in range(3):
                    ins = nc.tensor.matmul(counts[:, 512 * c:512 * c + 2], zeros[:, 0:P], zeros[:, 0:2], start=False, stop=True,
                                           skip_group_check=True)
                ins.then_inc(s_cn, 1)
                if b >= 1:
                    turn_counts(b - 1)
            turn_counts(BLK - 1)

            pe.wait_ge(s_cs, 3 * BLK)
            pe.wait_ge(s_ro, 2 * BLK)
            for c in range(K):
                pe.wait_ge(s_ep, c + 1)
                for n, (pa, pb_) in enumerate(((0, 1), (2, 3))):
                    if c >= 1:
                        pe.wait_ge(s_sumr, 2 * c - 1 + n)
                    for s in range(BLK):
                        for q in (pa, pb_):
                            for c0, c1 in BANKS:
                                ins = nc.tensor.matmul(PS[:, 1536 * n + c0:1536 * n + c1], parts[c % 2][q][0:P, s, :], CT[0:P, s, c0:c1],
                                                       start=(s == 0 and q == pa), stop=(s == BLK - 1 and q == pb_))
                    ins.then_inc(s_sum, 1)

            for m in range(HC):
                pe.wait_ge(s_w1l, m + 1)
                if m >= 2:
                    pe.wait_ge(s_h, m - 1)
                else:
                    pe.wait_ge(s_sumr, 2 * K - 1 + m)
                for k in range(K):
                    if m == 0:
                        pe.wait_ge(s_agl, k + 1)
                    for w, q in ((w1h, XTh), (w1h, XTl), (w1l, XTh)):
                        for c0, c1 in BANKS:
                            ins = nc.tensor.matmul(PS[:, 1536 * (m % 2) + c0:1536 * (m % 2) + c1], w[:, m % 2, k, :], q[:, k, c0:c1],
                                                   start=(k == 0 and w is w1h and q is XTh), stop=(k == K - 1 and w is w1l))
                ins.then_inc(s_z, 1)

            def second_layer(n):
                h = n // BLK
                if n % BLK == 0:
                    pe.wait_ge(s_w2l, 4 * h + 4)
                pe.wait_ge(s_htl, n + 1)
                if n >= 2:
                    pe.wait_ge(s_r2, n - 1)
                for k in range(HC):
                    for i, (q, w) in enumerate(((hth, w2h), (hth, w2l), (htl, w2h))):
                        ins = nc.tensor.matmul(bank(n % 2)[0:P, 0:HALF], q[n % 2][:, k, :], w[h][:, k, :],
                                               start=(k == 0 and i == 0), stop=(k == HC - 1 and i == 2))
                ins.then_inc(s_o2, 1)

            def turn_norm2(b):
                pe.wait_ge(s_xn2, b + 1)
                if b >= 1:
                    pe.wait_ge(s_x2s, b)
                for k in range(K):
                    ins = nc.tensor.transpose(bank(2 + k // 3)[:, P * (k % 3):P * (k % 3) + P], xn2[0:P, b % 2, 128 * k:128 * k + 128], ident[0:P, 0:P])
                ins.then_inc(s_x2t, 1)

            def router(b):
                pe.wait_ge(s_x2s, b + 1)
                where = bank(4)[0:P, NE * b:NE * b + NE]
                for k in range(K):
                    nc.tensor.matmul(where, xn2T[:, b % 2, k, :], rw[:, k, :], start=(k == 0), stop=False)
                nc.tensor.matmul(where, ones[0:1, 0:P], rb[:], start=False, stop=True).then_inc(s_lg, 1)

            pe.wait_ge(s_h, HC)
            pe.wait_ge(s_rw, 48)
            for n in range(2 * BLK):
                if n >= BLK + 4:
                    turn_norm2(n - BLK - 4)
                if n >= BLK + 5:
                    router(n - BLK - 5)
                second_layer(n)
            for b in range(BLK - 4, BLK):
                turn_norm2(b)
                router(b - 1)
            router(BLK - 1)
            pe.wait_ge(s_route, ONE_HOT)
            hot = onehot[0:P].rearrange("p b e -> p (b e)")
            nc.tensor.matmul(bank(5)[0:P, 0:BLK * NE], tri[0:P, 0:P], hot, start=True, stop=True)
            nc.tensor.matmul(bank(6)[0:P, 0:BLK * NE], ones[0:P, 0:P], hot, start=True, stop=True).then_inc(s_rk, 1)

            def turn_rows(n, u, i):
                pe.wait_ge(s_g[u], i * 16 + 16)
                pe.wait_ge(s_gl, n + 1)
                for k in range(K):
                    ins = nc.tensor.transpose(bank(k // 3)[:, 128 * (k % 3):128 * (k % 3) + 128], xg[:, u, 128 * k:128 * k + 128], ident[:])
                ins.then_inc(s_gt, 1)

            def up(n, u):
                pe.wait_ge(s_gl, n + 2)
                pe.wait_ge(s_fl, n + 1)
                for k in range(K):
                    for i, (q, w) in enumerate(((xgh, w12h), (xgh, w12l), (xgl, w12h))):
                        ins = nc.tensor.matmul(bank(2)[:, :], q[:, u, k, :], w[u][:, k, :], start=(k == 0 and i == 0), stop=(k == K - 1 and i == 2))
                ins.then_inc(s_up, 1)

            def turn_hidden(n):
                pe.wait_ge(s_hd, n + 1)
                for k in range(FC):
                    ins = nc.tensor.transpose(bank(3)[:, 128 * k:128 * k + 128], hid[:, 128 * k:128 * k + 128], ident[:])
                ins.then_inc(s_ht, 1)

            def down_projection(n, u):
                pe.wait_ge(s_hl, n + 1)
                pe.wait_ge(s_f3, n + 1)
                if isinstance(n, int) and n >= 1:
                    pe.wait_ge(s_yb, n)
                for c in range(2):
                    for k in range(FC):
                        for i, (q, w) in enumerate(((hidh, w3h), (hidh, w3l), (hidl, w3h))):
                            ins = nc.tensor.matmul(bank(4 + c)[:, 0:HALF], q[:, k, :], w[u][:, k, HALF * c:HALF * c + HALF],
                                                   start=(k == 0 and i == 0), stop=(k == FC - 1 and i == 2))
                ins.then_inc(s_y, 1)

            pe.sem_inc(s_gl, 1)
            pe.sem_inc(s_up, 2)
            pe.sem_inc(s_y, 2)
            turn_rows(0, 0, 0)
            up(0, 0)
            turn_rows(1, 1, 0)
            turn_hidden(0)
            up(1, 1)
            turn_rows(2, 0, 1)
            down_projection(0, 0)
            turn_hidden(1)
            with pe.Fori(1, SB // 2) as i:
                for u in range(2):
                    n = i * 2 + u
                    up(n, u)
                    turn_rows(n + 1, 1 - u, i + u)
                    pe.wait_ge(s_yb, n - 1)
                    down_projection(n - 1, 1 - u)
                    turn_hidden(n)
            up(SB - 1, 0)
            down_projection(SB - 2, 1)
            turn_hidden(SB - 1)
            down_projection(SB - 1, 0)


_INS = ['x', 'src', 'dst', 'L0_gnn_t', 'L0_gnn_W1', 'L0_gnn_b1', 'L0_gnn_bn_gamma', 'L0_gnn_bn_beta', 'L0_gnn_bn_mean',
        'L0_gnn_bn_var', 'L0_gnn_W2', 'L0_gnn_b2', 'L0_mix_Wq', 'L0_mix_Wk', 'L0_mix_Wv', 'L0_mix_Wo', 'L0_mix_proj',
        'L0_ffn_router_w', 'L0_ffn_router_b', 'L0_ffn_w1', 'L0_ffn_w2', 'L0_ffn_w3']


def kernel(**inputs):
    import numpy as _np
    import concourse.bacc as _bacc
    from concourse import mybir as _mybir
    from concourse.bass_utils import run_bass_kernel_spmd as _run

    nc = _bacc.Bacc("TRN2", target_bir_lowering=False, num_devices=1)
    arrays, args = {}, []
    for name in _INS:
        a = _np.ascontiguousarray(inputs[name])
        if a.ndim == 0:
            a = a.reshape(1)
        arrays[f"in_{name}_dram"] = a
        args.append(nc.dram_tensor(f"in_{name}_dram", a.shape, _mybir.dt.from_np(a.dtype), kind="ExternalInput").ap())
    out = nc.dram_tensor("out_0_dram", (1250, 768), _mybir.dt.float32, kind="ExternalOutput").ap()
    build(nc, *args, out)
    r = _run(nc, [arrays], core_ids=[0])
    return r.results[0]["out_0_dram"]
```

```python
import concourse.bass as bass
from concourse import mybir
from contextlib import ExitStack

F32, F32R = mybir.dt.float32, mybir.dt.float32r
BF16, FP16, I32 = mybir.dt.bfloat16, mybir.dt.float16, mybir.dt.int32
ALU = mybir.AluOpType
ACT = mybir.ActivationFunctionType
X_AXIS = mybir.AxisListType.X


class Chain:

    def __init__(self, eng, sem):
        self.eng, self.sem, self.start, self.n = eng, sem, 0, 0

    def at(self, start):
        self.start, self.n = start, 0

    def __call__(self, ins):
        self.n += 1
        ins.then_inc(self.sem, 1)
        self.eng.wait_ge(self.sem, self.start + self.n)


def build(nc, x, src, dst, t, W1, b1, gamma, beta, mean, var, W2, b2, Wq, Wk, Wv, Wo, proj,
          router_w, router_b, w1, w2, w3, out):
    N, D = x.shape
    P = 125
    BLK = N // P
    PAIRS = BLK // 2
    K = D // 128
    M, DH = proj.shape
    HEADS = D // DH
    HP = HEADS // 2
    RATIO = M ** -0.5
    NORM = DH ** -0.25
    EPS = 1e-4
    BANKS = [(0, 512), (512, 1024), (1024, N)]
    E = src.shape[0]
    ET = 324
    GT = 4
    EG = ET // GT
    ER, PADV = ET // 3, 5000
    HID = W1.shape[1]
    HC = HID // 128
    HALF = D // 2
    NE, _, FH = w1.shape
    FC = FH // 128
    SB = 17
    SLOTS = SB * 128
    SHIFT = 60.0
    assert ET * 128 >= E and SB == (N + NE * 127) // 128 and PADV > N
    assert N == P * BLK and BLK == 2 * PAIRS and D == 128 * K and M == 256 and DH == 64 and HEADS == 2 * K

    ctx = ExitStack()
    with ctx:
        def sem(name):
            return ctx.enter_context(nc.semaphore(name))

        def sems(name, n):
            return [sem(f"{name}{i}") for i in range(n)]

        ARENA = 212800
        arena = ctx.enter_context(nc.sbuf_tensor("arena", [128, ARENA], mybir.dt.uint8))
        base_off = nc.sbuf_base - ARENA

        def at(name, shape, dt, off):
            size = 2 if dt in (BF16, FP16) else 4
            for n in shape[1:]:
                size *= n
            assert off % 32 == 0 and off + size <= ARENA, (name, off, size)
            return nc.alloc_sbuf_tensor_at(name, shape, dt, offset=base_off + off)

        class Region:

            def __init__(self, start, end):
                self.at, self.end = start, end

            def __call__(self, name, shape, dt):
                size = 2 if dt in (BF16, FP16) else 4
                for n in shape[1:]:
                    size *= n
                place = at(name, shape, dt, self.at)
                self.at += -(-size // 32) * 32
                assert self.at <= self.end, (name, self.at, self.end)
                return place

        O_X = 15360
        O_T = O_X + 60032
        O_V = O_T + 30720
        O_C = O_V + 33024
        O_W = O_C + 60064
        const = Region(0, O_X)
        ident = const("ident", [128, 128], F32)
        ones = const("ones", [128, 128], F32)
        eps5 = const("eps5", [128, 1], F32)
        ind = const("ind", [128, 2], F32)
        stats = const("stats", [128, BLK, 12], F32)
        meanvar = const("meanvar", [128, BLK, 2], F32)
        stdev = const("stdev", [128, BLK], F32)
        rstd = const("rstd", [128, BLK], F32)
        shift = const("shift", [128, BLK], F32)
        twice = const("twice", [128, BLK], F32)
        kdiag = const("kdiag", [128, BLK, 2], F32)
        nstab = const("nstab", [128, 2], F32)
        kmax = const("kmax", [128, BLK, 2], F32)
        kneg = const("kneg", [128, BLK, 2], F32)
        kexp = const("kexp", [128, BLK, 2], F32)
        kfac = const("kfac", [128, BLK, 2], F32)
        vsum = const("vsum", [128, 2, DH + 1], F32)
        km = const("km", [128, 2], F32)
        gmx = const("gmx", [128, 1], F32)
        dg = const("dg", [128, 2], F32)
        qmx = const("qmx", [128, 2, 2], F32)
        qbias = const("qbias", [128, 2, 2], F32)
        rden = const("rden", [128, 2, 2], F32)
        qdiag = const("qdiag", [128, BLK, 2], F32)
        tri = const("tri", [128, 128], F32)
        dneg = const("dneg", [128, ET], F32)
        sneg = const("sneg", [128, ET], F32)
        minus = const("minus", [128, N], FP16)
        zeros = const("zeros", [128, 512], BF16)
        gidx = const("gidx", [16, EG, GT], F32)
        blo = const("blo", [16, 1], F32)
        tmm = const("tmm", [128, 2, 3], F32)
        emax = const("emax", [16, 2], F32)
        elim = const("elim", [16, 3], F32)
        limf = const("limf", [1, 32], F32)
        limi = const("limi", [1, 32], I32)
        bnr = const("bnr", [128, 128], F32)
        bnc = const("bnc", [128, 5, HC], F32)
        bns = const("bns", [128, 3, HC], F32)
        tb = const("tb", [128, 1], F32)
        gmax = const("gmax", [128, 1], F32)
        mrow = const("mrow", [1, 8], F32)
        mbias = const("mbias", [128, 1], F32)

        rw = const("rw", [128, K, NE], F32)
        rb = const("rb", [1, NE], F32)
        logit = const("logit", [128, BLK, NE], F32)
        prob = const("prob", [128, BLK], F32)
        best = const("best", [128, BLK], F32)
        pos = const("pos", [128, BLK], F32)
        quo = const("quo", [128, BLK], F32)
        k128 = const("k128", [128, SB], F32)
        upto = const("upto", [128, SB], F32)
        down = const("down", [128, NE], F32)
        nblk = const("nblk", [128, NE], F32)
        endb = const("endb", [128, NE], F32)
        tokid = const("tokid", [128, BLK], F32)
        idxy = const("idxy", [128, BLK], I32)
        tok = const("tok", [128, SB], I32)
        expf = const("expf", [1, SB], F32)
        expi = const("expi", [1, SB], I32)

        r_x = Region(O_X, O_T)
        XTh = r_x("XTh", [128, K, N], F32R)
        XTl = r_x("XTl", [128, K, N], F32R)
        attT = at("attT", [128, K, N], F32, O_T)
        r_c = Region(O_C, O_W)
        xin = r_c("xin", [128, BLK, D], F32)
        xn = at("xn", [128, BLK, D], F32, O_T)
        praw = r_c("praw", [128, 2, 128], F32)
        pscaled = r_c("pscaled", [128, 2 * M], F32)
        edi = r_c("edi", [128, 2, 3, 128], I32)
        edf = r_c("edf", [128, 2, 3, 128], F32)
        emask = r_c("emask", [16, 2, ET], F32)
        r_v = Region(O_V, O_C)
        wraw = r_v("wraw", [128, 3, K, 128], F32)
        wh = r_v("wh", [128, 3, K, 128], F32R)
        wl = r_v("wl", [128, 3, K, 128], F32R)
        V = r_v("V", [128, BLK, 2, DH + 1], F32)
        r_c = Region(O_C, O_W)
        KTh = r_c("KTh", [128, N], F32R)
        KTl = r_c("KTl", [128, N], F32R)
        QTh = r_c("QTh", [128, N], F32R)
        QTl = r_c("QTl", [128, N], F32R)
        VT = r_c("VT", [128, N], F32)
        sq = r_c("sq", [128, N], F32)
        kp = r_c("kp", [128, 2, BLK, M], F32)
        ctxT = r_c("ctxT", [128, 2 * M], F32)
        att = r_c("att", [128, BLK, 128], F32)
        r_w = Region(O_W, ARENA)
        qe = r_w("qe", [128, 2, 2, M], F32)
        qpT = r_w("qpT", [128, 2, 2, 2, P], F32)
        ctxs = r_w("ctxs", [128, 2, 2, DH + 1], F32)
        projh = r_w("projh", [128, 2 * M], F32R)
        projl = r_w("projl", [128, 2 * M], F32R)

        CT = at("CT", [128, BLK, N], F32R, O_C)
        crow = at("crow", [128, 2, N], F32, O_C + 50016)
        r_w = Region(O_W, ARENA)
        ohs = r_w("ohs", [128, GT, N], BF16)
        ohd = r_w("ohd", [128, GT, P], BF16)
        dist = r_w("dist", [128, GT, P], BF16)
        r_v = Region(O_V, O_V + 3 * 9216)
        r_c = Region(O_C, O_C + 50016)
        woh = [r_v("woh0", [128, K, HALF], F32R), r_c("woh1", [128, K, HALF], F32R)]
        wol = [r_v("wol0", [128, K, HALF], F32R), r_c("wol1", [128, K, HALF], F32R)]
        woraw = r_v("woraw", [128, K, HALF], F32)
        atth = r_c("atth", [128, 2, K, P], F32R)
        attl = r_c("attl", [128, 2, K, P], F32R)
        rtile = r_c("rtile", [128, 2, HALF], F32)
        b2row = r_c("b2row", [128, D], F32)

        r_t = Region(O_T, O_C)
        parts = [[r_t(f"{n}{u}", [128, BLK, 128], F32R) for n in ("Eh", "El", "Mh", "Ml")] for u in range(2)]
        Ef = r_t("Ef", [128, BLK, 128], F32)
        msg = r_t("msg", [128, 2, BLK, 128], F32)
        w1raw = r_t("w1raw", [128, 2, K, 128], F32)
        r_w = Region(O_W, ARENA)
        rec = r_w("rec", [128, N], F32)
        agg = r_w("agg", [128, N], F32)

        r_t = Region(O_T, O_T + 12288)
        w1h = r_t("w1h", [128, 2, K, 128], F32R)
        w1l = r_t("w1l", [128, 2, K, 128], F32R)
        HT = at("HT", [128, HC, N], F32, O_C)
        w2h = [at("w2h0", [128, HC, HALF], F32R, O_T + 12288), at("w2h1", [128, HC, HALF], F32R, O_X)]
        w2l = [at("w2l0", [128, HC, HALF], F32R, O_T + 30720), at("w2l1", [128, HC, HALF], F32R, O_X + 18432)]
        hth = [at("hth0", [128, HC, P], F32R, O_T + 49152), at("hth1", [128, HC, P], F32R, O_X + 36864)]
        htl = [at("htl0", [128, HC, P], F32R, O_T + 55168), at("htl1", [128, HC, P], F32R, O_X + 42880)]
        w2raw = at("w2raw", [128, 2, 3, HALF], F32, O_W)
        rtile2 = at("rtile2", [128, 2, HALF], F32, O_W + 9216)
        x1 = at("x1", [128, BLK, D], F32, O_T + 12288)
        xn2 = at("xn2", [128, 2, D], F32, O_T + 43008)
        r_x = Region(O_X + 49152, O_T)
        xn2T = r_x("xn2T", [128, 2, K, P], F32)
        stats2 = r_x("stats2", [128, BLK, 12], F32)
        mv2 = r_x("mv2", [128, BLK, 2], F32)
        sd2 = r_x("sd2", [128, BLK], F32)
        cmpk = r_x("cmpk", [128, BLK, 16], F32)
        cmpe = r_x("cmpe", [128, NE, BLK], F32)
        cmpb = r_x("cmpb", [1, SB, NE], F32)
        sume = r_x("sume", [128, BLK, NE], F32)
        qtok = r_x("qtok", [128, BLK, SB], F32)
        onehot = r_x("onehot", [128, BLK, NE], F32)
        carry = r_x("carry", [128, BLK + 1, NE], F32)

        w12raw = [at("w12raw0", [128, K, 2 * FH], F32, O_X), None]
        w3raw = [at("w3raw0", [128, FC, D], F32, O_X + 12288), None]
        w12h = [at("w12h0", [128, K, 2 * FH], F32R, O_X + 18432), None]
        w12l = [at("w12l0", [128, K, 2 * FH], F32R, O_X + 30720), None]
        w3h = [at("w3h0", [128, FC, D], F32R, O_X + 43008), None]
        w3l = [at("w3l0", [128, FC, D], F32R, O_T), None]
        r_f = Region(O_T + 49152, ARENA)
        w12raw[1] = r_f("w12raw1", [128, K, 2 * FH], F32)
        w3raw[1] = r_f("w3raw1", [128, FC, D], F32)
        w12h[1] = r_f("w12h1", [128, K, 2 * FH], F32R)
        w12l[1] = r_f("w12l1", [128, K, 2 * FH], F32R)
        w3h[1] = r_f("w3h1", [128, FC, D], F32R)
        w3l[1] = r_f("w3l1", [128, FC, D], F32R)
        xg = r_f("xg", [128, 2, D], F32)
        rhot = at("rhot", [128, BLK, 128], F32, O_T + 49152 + 55296)
        xgh = r_f("xgh", [128, 2, K, 128], F32R)
        xgl = r_f("xgl", [128, 2, K, 128], F32R)
        gate = r_f("gate", [128, FH], F32)
        hid = r_f("hid", [128, FH], F32)
        hidh = r_f("hidh", [128, FC, 128], F32R)
        hidl = r_f("hidl", [128, FC, 128], F32R)
        yb = r_f("yb", [128, 2, D], BF16)
        yg = at("yg", [128, BLK, D], BF16, O_T + 49152)

        PS = ctx.enter_context(nc.psum_tensor("PS", [128, 4096], F32))
        PA = PS[:, 0:1536]
        PB = PS[:, 1536:3072]

        KBANK = (6, 7, 3, 4)

        def bank(i):
            return PS[:, 512 * i:512 * (i + 1)]

        res_d = nc.dram_tensor("res_scratch", (N, D), F32).ap()

        def blocks(ap):
            return ap.rearrange("(b p) d -> p b d", p=P)

        x_b, res_b = blocks(x), blocks(res_d)

        xn2_d = nc.dram_tensor("xn2_scratch", (N, D), F32).ap()
        y_d = nc.dram_tensor("expert_out_scratch", (SLOTS, D), BF16).ap()

        def cols_by_k(w):
            return w.rearrange("(k p) n -> p k n", p=128)

        s_x = sems("s_x", PAIRS)
        s_cst = sem("s_cst")
        s_par = sem("s_par")
        s_pre = sem("s_pre")
        EDGE_COLS, BN_ROWS, EDGE_ROWS, LIMITS, PROJ_T, MAX_T, STAB = range(1, 8)
        s_prd = sem("s_prd")
        EDGE_F, EDGE_COL_D, EDGE_MM, EDGE_EL, BN_D, LIM_I, PROJ_D, GMAX_D, MROW_D, STAB_D = 1, 3, 5, 6, 7, 8, 9, 10, 11, 12
        s_var = sem("s_var")
        s_sd = sem("s_sd")
        s_xn = sem("s_xn")
        s_xt = sem("s_xt")
        s_xth = sem("s_xth")
        s_xtl = sem("s_xtl")
        s_b2 = sem("s_b2")
        c_dve = sem("c_dve")
        c_pool = sem("c_pool")

        s_turn = sem("s_turn")
        s_wl = sem("s_wl")
        s_wsp = sem("s_wsp")
        s_wok = sem("s_wok")
        s_kps = sem("s_kps")
        s_kh = sem("s_kh")
        s_kl = sem("s_kl")
        s_vps = sem("s_vps")
        s_vt = sem("s_vt")
        s_qps = sem("s_qps")
        s_qh = sem("s_qh")
        s_ql = sem("s_ql")
        s_kd = sem("s_kd")
        s_kdc = sem("s_kdc")
        s_kdg = sem("s_kdg")
        s_ksum = sem("s_ksum")
        s_kmT = sem("s_kmT")
        s_dg = sem("s_dg")
        s_stb = sem("s_stb")
        s_kb = sem("s_kb")
        s_ke = sem("s_ke")
        s_stc = sem("s_stc")
        s_kf = sem("s_kf")
        s_vtp = sem("s_vtp")
        s_v = sem("s_v")
        s_cx = sem("s_cx")
        s_cxs = sem("s_cxs")
        s_qdg = sem("s_qdg")
        s_qd = sem("s_qd")
        s_qb = sem("s_qb")
        s_qe = sem("s_qe")
        s_qt = sem("s_qt")
        s_qp = sem("s_qp")
        s_o = sem("s_o")
        s_at = sem("s_at")
        s_aT = sem("s_aT")
        s_as = sem("s_as")
        s_out = sem("s_out")
        s_pad = sem("s_pad")
        s_e = sem("s_e")
        s_bnv = sem("s_bnv")
        s_oh = sem("s_oh")
        s_od = sem("s_od")
        s_ab = sem("s_ab")
        s_ohf = sem("s_ohf")
        s_cn = sem("s_cn")
        s_cr = sem("s_cr")
        s_ct = sem("s_ct")
        s_cs = sem("s_cs")
        s_wor = sem("s_wor")
        s_woh = sem("s_woh")
        s_wol = sem("s_wol")
        s_ath = sem("s_ath")
        s_atl = sem("s_atl")
        s_ow = sem("s_ow")
        s_rl = sems("s_rl", 2)
        s_ro = sem("s_ro")
        s_rs = sems("s_rs", 2)
        s_ml = sems("s_ml", 2)
        s_ms = sem("s_ms")
        s_ex = sem("s_ex")
        s_eh = sem("s_eh")
        s_mm = sem("s_mm")
        s_mh = sem("s_mh")
        s_ep = sem("s_ep")
        s_sum = sem("s_sum")
        s_sumr = sem("s_sumr")
        s_ag = sem("s_ag")
        s_agh = sem("s_agh")
        s_agl = sem("s_agl")
        s_w1r = sems("s_w1r", 2)
        s_w1h = sem("s_w1h")
        s_w1l = sem("s_w1l")
        s_z = sem("s_z")
        s_h = sem("s_h")
        s_w2r = sems("s_w2r", 2)
        s_w2h = sem("s_w2h")
        s_w2l = sem("s_w2l")
        s_hth = sem("s_hth")
        s_htl = sem("s_htl")
        s_o2 = sem("s_o2")
        s_r2l = sems("s_r2l", 2)
        s_r2 = sem("s_r2")
        s_r2s = sems("s_r2s", 2)
        s_x1l = sem("s_x1l")
        s_v2 = sem("s_v2")
        s_sd2 = sem("s_sd2")
        s_xn2 = sem("s_xn2")
        s_xn2s = sems("s_xn2s", 2)
        s_x2t = sem("s_x2t")
        s_x2s = sem("s_x2s")
        s_rw = sem("s_rw")
        s_lg = sem("s_lg")
        s_se = sem("s_se")
        s_route = sem("s_route")
        SHIFTED, ONE_HOT, EXPERTS, SLOTS_D = range(1, 5)
        s_rk = sem("s_rk")
        s_tt = sem("s_tt")
        s_tok = sem("s_tok")
        s_fr = sems("s_fr", 2)
        s_f3r = sems("s_f3r", 2)
        s_fh = sem("s_fh")
        s_fl = sem("s_fl")
        s_f3h = sem("s_f3h")
        s_f3 = sem("s_f3")
        s_g = sems("s_g", 2)
        s_gt = sem("s_gt")
        s_gh = sem("s_gh")
        s_gl = sem("s_gl")
        s_up = sem("s_up")
        s_sg = sem("s_sg")
        s_hd = sem("s_hd")
        s_ht = sem("s_ht")
        s_hh = sem("s_hh")
        s_hl = sem("s_hl")
        s_y = sem("s_y")
        s_yb = sem("s_yb")
        s_ys = sems("s_ys", 2)
        s_fin = sem("s_fin")

        def turn_limits(eng):
            return [0] + [eng.value_load(limi[0:1, BLK + b:BLK + b + 1], min_val=b + 1, max_val=(b + 1) * EG) for b in range(BLK)]

        def turn_offsets(eng):
            return [eng.value_load(limi[0:1, 2 * BLK + b:2 * BLK + b + 1], min_val=-b * EG, max_val=EG) for b in range(BLK)]

        block = ctx.enter_context(nc.Block())

        @block.sync
        def _(sp):
            for i in range(PAIRS):
                sp.dma_start(xin[0:112, 2 * i:2 * i + 2, :], x_b[0:112, 2 * i:2 * i + 2, :]).then_inc(s_x[i], 16)
                sp.dma_start(xin[112:P, 2 * i:2 * i + 2, :], x_b[112:P, 2 * i:2 * i + 2, :]).then_inc(s_x[i], 16)
            sp.wait_ge(s_pad, 1)
            for i, e in enumerate((dst, src)):
                full = E // 128 - 2 * ER
                sp.dma_start(edi[0:ER, i, 0:2], e[0:2 * ER * 128].rearrange("(g r e) -> r g e", g=2, r=ER)).then_inc(s_e, 16)
                sp.dma_start(edi[0:full, i, 2], e[2 * ER * 128:E // 128 * 128].rearrange("(r e) -> r e", e=128)).then_inc(s_e, 16)
                sp.dma_start(edi[full:full + 1, i, 2, 0:E % 128], e[E // 128 * 128:E].rearrange("(a e) -> a e", a=1)).then_inc(s_e, 16)

            def load_w2(i):
                if i >= 2:
                    sp.wait_ge(s_w2l, i - 1)
                sp.dma_start(w2raw[:, i % 2], cols_by_k(W2)[:, 3 * (i % 4):3 * (i % 4) + 3, HALF * (i // 4):HALF * (i // 4) + HALF])\
                    .then_inc(s_w2r[i % 2], 16)

            with sp.Fori(0, HP) as j:
                sp.wait_ge(s_wsp, j + 1)
                for n, w in enumerate((Wk, Wv, Wq)):
                    sp.dma_start(wraw[:, n], cols_by_k(w)[:, :, bass.ds(j * 128, 128)]).then_inc(s_wl, 16)
            sp.wait_ge(s_cst, 16)
            sp.dma_start(rw[:], router_w.rearrange("(k p) e -> p k e", p=128)).then_inc(s_rw, 16)
            sp.dma_start(rb[:], router_b.rearrange("(a e) -> a e", a=1)).then_inc(s_rw, 16)
            sp.wait_ge(s_qps, 3 * HP)
            sp.dma_start(woraw[:], cols_by_k(Wo)[:, :, 0:HALF]).then_inc(s_wor, 16)

            def residual(n, source, tile, landed, stored):
                if n < 2 * BLK:
                    h, b = n // BLK, n % BLK
                    if n >= 2:
                        sp.wait_ge(stored[n % 2], 16 * (n // 2))
                    sp.dma_start(tile[0:P, n % 2], source[:, b, HALF * h:HALF * h + HALF]).then_inc(landed[n % 2], 16)

            sp.wait_ge(s_wol, 1)
            sp.dma_start(woraw[:], cols_by_k(Wo)[:, :, HALF:D]).then_inc(s_wor, 16)
            sp.wait_ge(s_as, HP * BLK)
            sp.dma_start(b2row[0:P, :], b2.rearrange("(a n) -> a n", a=1).to_broadcast([P, D])).then_inc(s_b2, 16)
            residual(0, x_b, rtile, s_rl, s_rs)
            for n in range(2 * BLK):
                h, b = n // BLK, n % BLK
                residual(n + 1, x_b, rtile, s_rl, s_rs)
                sp.wait_ge(s_ro, n + 1)
                sp.dma_start(res_b[:, b, HALF * h:HALF * h + HALF], rtile[0:P, n % 2]).then_inc(s_rs[n % 2], 16)
            sp.wait_ge(s_ow, 2 * BLK)
            for c in range(K):
                if c >= 2:
                    sp.wait_ge(s_ep, c - 1)
                sp.dma_start(msg[0:P, c % 2], x_b[:, :, 128 * c:128 * c + 128]).then_inc(s_ml[c % 2], 16)
                if c < 2:
                    sp.dma_start(w1raw[:, c], cols_by_k(W1)[:, :, 128 * c:128 * c + 128]).then_inc(s_w1r[c], 16)
            for m in range(2, HC):
                sp.wait_ge(s_w1l, m - 1)
                sp.dma_start(w1raw[:, m % 2], cols_by_k(W1)[:, :, 128 * m:128 * m + 128]).then_inc(s_w1r[m % 2], 16)
                if m == 4:
                    for i in range(2):
                        load_w2(i)
                if 5 <= m < 7:
                    load_w2(m - 3)
            for i in range(2):
                sp.wait_ge(s_rs[i], 16 * BLK)
            for i in range(4, 6):
                load_w2(i)

            def store_norm2(b):
                sp.wait_ge(s_xn2, b + 1)
                sp.dma_start(blocks(xn2_d)[:, b], xn2[0:P, b % 2]).then_inc(s_xn2s[b % 2], 16)

            residual(0, res_b, rtile2, s_r2l, s_r2s)
            for n in range(2 * BLK):
                h, b = n // BLK, n % BLK
                if n in (1, 2):
                    load_w2(n + 5)
                if h == 0:
                    residual(n + 1, res_b, rtile2, s_r2l, s_r2s)
                elif n + 1 < 2 * BLK:
                    sp.wait_ge(s_r2, n)
                    sp.dma_start(rtile2[0:P, (n + 1) % 2], res_b[:, b + 1, HALF:D]).then_inc(s_r2l[(n + 1) % 2], 16)
                if n >= BLK + 2:
                    store_norm2(n - BLK - 2)
                if h == 0:
                    sp.wait_ge(s_r2, n + 1)
                    sp.dma_start(res_b[:, b, 0:HALF], rtile2[0:P, n % 2]).then_inc(s_r2s[n % 2], 16)
                if n == BLK:
                    for i in range(2):
                        sp.wait_ge(s_r2s[i], 16 * (BLK // 2))
                    sp.wait_ge(s_o2, BLK)
                    sp.dma_start(x1[0:P, :, 0:HALF], res_b[:, :, 0:HALF]).then_inc(s_x1l, 16)
            for b in range(BLK - 2, BLK):
                store_norm2(b)
            sp.wait_ge(s_route, EXPERTS)

            def load_up(n, u, again=True):
                e = nc.sync.value_load(expi[0:1, bass.ds(n, 1)], min_val=0, max_val=NE - 1)
                if again:
                    sp.wait_ge(s_fl, n - 1)
                sp.dma_start(w12raw[u][:, :, 0:FH], w1[bass.ds(e, 1)].rearrange("a (k p) h -> p (a k) h", p=128)).then_inc(s_fr[u], 16)
                sp.dma_start(w12raw[u][:, :, FH:2 * FH], w2[bass.ds(e, 1)].rearrange("a (k p) h -> p (a k) h", p=128)).then_inc(s_fr[u], 16)

            def load_down(n, u, again=True):
                e = nc.sync.value_load(expi[0:1, bass.ds(n, 1)], min_val=0, max_val=NE - 1)
                if again:
                    sp.wait_ge(s_f3, n - 1)
                sp.dma_start(w3raw[u][:], w3[bass.ds(e, 1)].rearrange("a (k p) h -> p (a k) h", p=128)).then_inc(s_f3r[u], 16)

            for u in range(2):
                load_up(u, u, again=False)
            load_down(0, 0, again=False)
            load_up(2, 0)
            load_down(1, 1, again=False)
            with sp.Fori(1, SB // 2) as i:
                for u in range(2):
                    n = i * 2 + 1 + u
                    load_up(n, 1 - u)
                    load_down(n - 1, u)
            load_down(SB - 1, 0)
            for b in range(BLK):
                sp.wait_ge(s_fin, b + 1)
                sp.dma_start(blocks(out)[0:112, b], x1[0:112, b]).then_inc(s_out, 16)
                sp.dma_start(blocks(out)[112:P, b], x1[112:P, b]).then_inc(s_out, 16)
            sp.wait_ge(s_out, 32 * BLK)

        @block.gpsimd
        def _(pool):
            chain = Chain(pool, c_pool)
            nc.gpsimd.memset(ident[:], 0.0).then_inc(c_pool, 1)
            nc.gpsimd.memset(ones[:], 1.0).then_inc(c_pool, 1)
            nc.gpsimd.iota(minus[:], [[-1, N]], base=0, channel_multiplier=0, allow_small_or_imprecise_dtypes=True).then_inc(s_cst, 1)
            nc.gpsimd.iota(gidx[:], [[1, EG], [0, GT]], base=0, channel_multiplier=0, allow_small_or_imprecise_dtypes=True).then_inc(s_cst, 1)
            nc.gpsimd.iota(blo[:], [[0, 1]], base=0, channel_multiplier=P, allow_small_or_imprecise_dtypes=True).then_inc(s_cst, 1)
            nc.gpsimd.memset(zeros[:], 0.0).then_inc(s_cst, 1)
            nc.gpsimd.iota(k128[:], [[128, SB]], base=0, channel_multiplier=0, allow_small_or_imprecise_dtypes=True).then_inc(s_cst, 1)
            nc.gpsimd.iota(upto[:], [[1, SB]], base=0, channel_multiplier=0, allow_small_or_imprecise_dtypes=True).then_inc(s_cst, 1)
            nc.gpsimd.iota(down[:], [[-1, NE]], base=NE, channel_multiplier=0, allow_small_or_imprecise_dtypes=True).then_inc(s_cst, 1)
            nc.gpsimd.iota(tokid[:], [[P, BLK]], base=0, channel_multiplier=1, allow_small_or_imprecise_dtypes=True).then_inc(s_cst, 1)
            nc.gpsimd.memset(eps5[:], 1e-5).then_inc(s_cst, 1)
            nc.gpsimd.memset(vsum[:, :, DH:DH + 1], RATIO * EPS * BLK).then_inc(s_cst, 1)
            pool.wait_ge(c_pool, 2)
            nc.gpsimd.affine_select(out=ident[:], in_=ident[:], compare_op=ALU.not_equal, fill=1.0, base=0,
                                    pattern=[[-1, 128]], channel_multiplier=1).then_inc(s_cst, 1)
            nc.gpsimd.affine_select(out=tri[:], in_=ones[:], compare_op=ALU.is_gt, fill=0.0, base=0,
                                    pattern=[[1, 128]], channel_multiplier=-1).then_inc(s_cst, 1)
            pool.sem_inc(s_wsp, 1)
            pool.wait_ge(s_wl, 48)
            chain.at(2)
            chain(nc.gpsimd.tensor_copy(wh[:], wraw[:]))
            nc.gpsimd.tensor_tensor(wl[:], wraw[:], wh[:].bitcast(F32), ALU.subtract).then_inc(s_wok, 1)
            pool.wait_ge(s_wok, 1)
            pool.sem_inc(s_wsp, 1)
            with pool.Fori(1, HP) as j:
                pool.wait_ge(s_wl, 48 * j + 48)
                pool.wait_ge(s_qps, 3 * j)
                pool.sem_inc(s_turn, 1)
                chain.at(2 + j)
                chain(nc.gpsimd.tensor_copy(wh[:], wraw[:]))
                nc.gpsimd.tensor_tensor(wl[:], wraw[:], wh[:].bitcast(F32), ALU.subtract).then_inc(s_wok, 1)
                pool.wait_ge(s_wok, j + 1)
                pool.sem_inc(s_wsp, 1)
            pool.wait_ge(s_wor, 16)
            nc.gpsimd.tensor_copy(woh[0][:], woraw[:]).then_inc(s_woh, 1)
            pool.wait_ge(s_woh, 1)
            nc.gpsimd.tensor_tensor(wol[0][:], woraw[:], woh[0][:].bitcast(F32), ALU.subtract).then_inc(s_wol, 1)
            def messages(c):
                u = c % 2
                pool.wait_ge(s_ml[u], 16 * (c // 2 + 1))
                for b in range(BLK):
                    ins = nc.gpsimd.tensor_scalar(msg[0:P, u, b, :], msg[0:P, u, b, :], rstd[0:P, b:b + 1], shift[0:P, b:b + 1], ALU.mult, ALU.add)
                chain(ins)
                nc.gpsimd.tensor_scalar(msg[0:P, u], msg[0:P, u], 0.0, None, ALU.max).then_inc(s_ms, 1)

            chain.at(2 + HP)
            messages(0)
            messages(1)
            for c in range(K):
                u = c % 2
                if c >= 2:
                    messages(c)
                pool.wait_ge(s_eh, c + 1)
                nc.gpsimd.tensor_tensor(parts[u][1][0:P], Ef[0:P], parts[u][0][0:P].bitcast(F32), ALU.subtract)
                pool.wait_ge(s_mh, c + 1)
                nc.gpsimd.tensor_tensor(parts[u][3][0:P], msg[0:P, u], parts[u][2][0:P].bitcast(F32), ALU.subtract).then_inc(s_ep, 1)
            for i in range(2):
                pool.wait_ge(s_xn2s[i], 16 * PAIRS)
            pool.wait_ge(s_tok, 1)

            def gather(n):
                if n < SB:
                    if n >= 2:
                        pool.wait_ge(s_gt, n - 1)
                    nc.gpsimd.indirect_dma_start(out=xg[:, n % 2, :], out_offset=None, in_=xn2_d,
                                                 in_offset=bass.IndirectOffsetOnAxis(ap=tok[:, n:n + 1], axis=0)).then_inc(s_g[n % 2], 16)

            gather(0)
            gather(1)
            for n in range(SB):
                u = n % 2
                gather(n + 2)
                pool.wait_ge(s_f3h, n + 1)
                nc.gpsimd.tensor_tensor(w3l[u][:], w3raw[u][:], w3h[u][:].bitcast(F32), ALU.subtract).then_inc(s_f3, 1)
            for i in range(2):
                pool.wait_ge(s_ys[i], 16 * (SB // 2 + 2 - i))
            for b in range(BLK):
                nc.gpsimd.indirect_dma_start(out=yg[0:P, b, :], out_offset=None, in_=y_d,
                                             in_offset=bass.IndirectOffsetOnAxis(ap=idxy[0:P, b:b + 1], axis=0)).then_inc(s_g[b // PAIRS], 16)

        @block.scalar
        def _(act):
            for dup in range(2):
                act.dma_start(praw[:, :, 64 * dup:64 * dup + 64], proj.rearrange("(c p) d -> p c d", p=128)).then_inc(s_par, 16)
            for i, row in enumerate((gamma, beta, mean, var, b1)):
                act.dma_start(bnr[HC * i:HC * i + HC, :], row.rearrange("(a n) -> a n", n=128)).then_inc(s_par, 16)
            act.dma_start(tb[:], t.rearrange("(a n) -> a n", a=1).to_broadcast([128, 1])).then_inc(s_par, 16)
            act.wait_ge(s_cst, 16)

            def deviation(h):
                act.wait_ge(s_var, PAIRS * (h + 1))
                nc.scalar.activation(stdev[0:P, PAIRS * h:PAIRS * (h + 1)], meanvar[0:P, PAIRS * h:PAIRS * (h + 1), 1],
                                     ACT.Sqrt, bias=eps5[0:P, :]).then_inc(s_sd, 1)

            deviation(0)
            for b in range(BLK):
                if b == PAIRS:
                    deviation(1)
                    act.wait_ge(s_pre, BN_ROWS)
                    nc.scalar.activation(bns[:, 0, :], bank(7)[:, 3 * HC:4 * HC], ACT.Sqrt, bias=eps5[:]).then_inc(s_bnv, 1)
                for i in range(2):
                    act.wait_ge(s_xt, 2 * b + i + 1)
                    nc.scalar.activation(XTh[:, 3 * i:3 * i + 3, P * b:P * b + P],
                                         bank(2 * (b % 2) + i)[:, 0:375].rearrange("p (k n) -> p k n", k=3),
                                         ACT.Copy).then_inc(s_xth, 1)
            act.wait_ge(s_prd, LIM_I)
            turns = turn_limits(nc.scalar)
            offsets = turn_offsets(nc.scalar)

            def norm2(b):
                act.wait_ge(s_v2, b + 1)
                nc.scalar.activation(sd2[0:P, b:b + 1], mv2[0:P, b, 1:2], ACT.Sqrt, bias=eps5[0:P, :]).then_inc(s_sd2, 1)

            def put_norm2(b):
                act.wait_ge(s_x2t, b + 1)
                if b >= 2:
                    act.wait_ge(s_lg, b - 1)
                for c in range(2):
                    ins = nc.scalar.activation(xn2T[:, b % 2, 3 * c:3 * c + 3], bank((2, 5)[b % 2] + c)[:, 0:375].rearrange("p (k n) -> p k n", k=3),
                                               ACT.Copy)
                ins.then_inc(s_x2s, 1)

            with act.Fori(0, HP) as j:
                act.wait_ge(s_vps, 3 * j + 3)
                nc.scalar.activation(VT[:], PA[:, 0:N], ACT.Copy).then_inc(s_vt, 1)
                for n, (c0, c1) in enumerate(BANKS):
                    act.wait_ge(s_kps, 3 * j + n + 1)
                    nc.scalar.activation(KTh[:, c0:c1], PB[:, c0:c1], ACT.Copy)
                    nc.scalar.activation(sq[:, c0:c1], PB[:, c0:c1], ACT.Square).then_inc(s_kh, 1)
                for b in range(BLK):
                    act.wait_ge(s_kb, BLK * j + b + 1)
                    for a in range(2):
                        ins = nc.scalar.activation(kp[0:P, a, b, :], bank(KBANK[b % 4])[0:P, M * a:M * a + M], ACT.Exp,
                                                   bias=kneg[0:P, b, a:a + 1])
                    ins.then_inc(s_ke, 1)
                act.wait_ge(s_kdg, j + 1)
                for n, (c0, c1) in enumerate(BANKS):
                    act.wait_ge(s_qps, 3 * j + n + 1)
                    nc.scalar.activation(QTh[:, c0:c1], PB[:, c0:c1], ACT.Copy)
                    nc.scalar.activation(sq[:, c0:c1], PB[:, c0:c1], ACT.Square).then_inc(s_qh, 1)
                    if n == 1:
                        act.wait_ge(s_stc, j + 1)
                        for a in range(2):
                            ins = nc.scalar.activation(kfac[0:P, :, a], kexp[0:P, :, a], ACT.Exp, bias=nstab[0:P, a:a + 1])
                        ins.then_inc(s_kf, 1)

                def put_attT(b):
                    act.wait_ge(s_aT, BLK * j + b + 1)
                    nc.scalar.activation(attT[:, bass.ds(j, 1), P * b:P * b + P],
                                         bank(4 + b % 2)[:, 0:P].rearrange("p (a n) -> p a n", a=1),
                                         ACT.Copy).then_inc(s_as, 1)

                for u in range(BLK):
                    act.wait_ge(s_qb, BLK * j + u + 1)
                    if u >= 2:
                        act.wait_ge(s_qt, BLK * j + u - 1)
                    for a in range(2):
                        ins = nc.scalar.activation(qe[0:P, u % 2, a, :], bank(6 + u % 2)[0:P, M * a:M * a + M],
                                                   ACT.Exp, bias=qbias[0:P, u % 2, a:a + 1])
                    ins.then_inc(s_qe, 1)
                    if u == 2:
                        act.wait_ge(s_cx, 2 * j + 1)
                        nc.scalar.activation(ctxT[0:DH + 1, :], bank(3)[0:DH + 1, :], ACT.Copy).then_inc(s_cxs, 1)
                    if u == 3:
                        act.wait_ge(s_cx, 2 * j + 2)
                        nc.scalar.activation(ctxs[:], bank(3)[:, 0:260].rearrange("p (a c d) -> p a c d", a=2, c=2),
                                             ACT.Copy).then_inc(s_cxs, 1)
                    if u >= 6:
                        put_attT(u - 6)
                for b in range(BLK - 6, BLK):
                    put_attT(b)

            def put_counts(b):
                for i in range(3):
                    n = min(4, BLK - 4 * i)
                    act.wait_ge(s_ct, 3 * b + i + 1)
                    nc.scalar.activation(CT[0:P, 4 * i:4 * i + n, P * b:P * b + P],
                                         bank(6 + (3 * b + i) % 2)[0:P, 0:P * n].rearrange("p (s n) -> p s n", s=n),
                                         ACT.Copy).then_inc(s_cs, 1)

            for n in range(2 * BLK):
                b = n % BLK
                if n == 2:
                    act.wait_ge(s_wor, 32)
                    nc.scalar.activation(woh[1][:], woraw[:], ACT.Copy).then_inc(s_woh, 1)
                if n >= 2:
                    act.wait_ge(s_ow, n - 1)
                nc.scalar.activation(atth[:, n % 2], attT[:, :, P * b:P * b + P], ACT.Copy).then_inc(s_ath, 1)

            def exponentials(c):
                if c >= K:
                    return
                u = c % 2
                if c >= 1:
                    act.wait_ge(s_ep, c)
                act.wait_ge(s_ms, c + 1)
                nc.scalar.activation(Ef[0:P], msg[0:P, u], ACT.Exp, bias=mbias[0:P, :], scale=tb[0:P, :]).then_inc(s_ex, 1)
                if c >= 2:
                    act.wait_ge(s_sum, 2 * (c - 1))
                act.wait_ge(s_ex, c + 1)
                nc.scalar.activation(parts[u][0][0:P], Ef[0:P], ACT.Copy).then_inc(s_eh, 1)

            def weighted(c):
                if c >= K:
                    return
                u = c % 2
                act.wait_ge(s_mm, c + 1)
                nc.scalar.activation(parts[u][2][0:P], msg[0:P, u], ACT.Copy).then_inc(s_mh, 1)

            act.wait_ge(s_prd, STAB_D)
            act.wait_ge(s_ow, 2 * BLK)

            def store_counts(b):
                act.wait_ge(s_cn, b + 1)
                if b >= 2:
                    act.wait_ge(s_ct, 3 * (b - 1))
                nc.scalar.activation(crow[0:P, b % 2, :], PS[0:P, 1536 * (b % 2):1536 * (b % 2) + N], ACT.Copy).then_inc(s_cr, 1)

            for b in range(BLK):
                if b == 1:
                    for i in range(2):
                        act.wait_ge(s_rs[i], 16 * BLK)
                if b in (2, 5):
                    exponentials(b // 3)
                if b in (4, 7):
                    weighted(b // 7)
                with act.Fori(turns[b], turns[b + 1]) as n:
                    g = nc.s_assert_within(n + offsets[b], 0, EG - 1, skip_runtime_bounds_check_because="turns map to groups first .. end - 1 of the block, all within the list")
                    for i, u in enumerate(range(0, GT, 2)):
                        act.wait_ge(s_ohf, n * GT + u + 1)
                        nc.scalar.activation(dist[:, u, :], minus[:, P * b:P * b + P], ACT.Abs, scale=-1.0,
                                             bias=dneg[:, bass.ds(g * GT + u, 1)]).then_inc(s_ab, 1)
                        act.wait_ge(s_ab, n * (GT // 2) + i + 1)
                        nc.scalar.activation(ohd[:, u, :], dist[:, u, :], ACT.Relu, bias=ones[:, 0:1], scale=-1.0).then_inc(s_od, 1)
                if b >= 1:
                    put_counts(b - 1)
                store_counts(b)
            put_counts(BLK - 1)
            for c in range(K):
                if c >= 1:
                    exponentials(c + 1)
                    weighted(c + 1)
                act.wait_ge(s_ag, c + 1)
                nc.scalar.activation(XTh[:, c, :], agg[:], ACT.Copy).then_inc(s_agh, 1)

            def w1_parts(m):
                if m < HC:
                    act.wait_ge(s_w1r[m % 2], 16 * (m // 2 + 1))
                    if m < 2:
                        act.wait_ge(s_sum, 2 * (K - 1))
                    else:
                        act.wait_ge(s_z, m - 1)
                    nc.scalar.activation(w1h[:, m % 2], w1raw[:, m % 2], ACT.Copy).then_inc(s_w1h, 1)

            def w2_parts(i):
                act.wait_ge(s_w2r[i % 2], 16 * (i // 2 + 1))
                nc.scalar.activation(w2h[i // 4][:, 3 * (i % 4):3 * (i % 4) + 3, :], w2raw[:, i % 2], ACT.Copy).then_inc(s_w2h, 1)

            w1_parts(0)
            for m in range(HC):
                w1_parts(m + 1)
                act.wait_ge(s_z, m + 1)
                nc.scalar.activation(HT[:, m, :], PS[:, 1536 * (m % 2):1536 * (m % 2) + N], ACT.Relu,
                                     bias=bns[:, 2, m:m + 1], scale=bns[:, 1, m:m + 1]).then_inc(s_h, 1)
                if 4 <= m < 8:
                    w2_parts(m - 4)

            def hidden_parts(n):
                if n < 2 * BLK:
                    b = n % BLK
                    if n >= 2:
                        act.wait_ge(s_o2, n - 1)
                    nc.scalar.activation(hth[n % 2][:], HT[:, :, P * b:P * b + P], ACT.Copy).then_inc(s_hth, 1)

            act.wait_ge(s_h, HC)
            hidden_parts(0)
            hidden_parts(1)
            for i in range(4, 8):
                w2_parts(i)
                hidden_parts(i - 2)
            for n in range(6, 2 * BLK):
                hidden_parts(n)
                if n >= BLK + 2:
                    norm2(n - BLK - 2)
                if n >= BLK + 3:
                    put_norm2(n - BLK - 3)
            norm2(BLK - 2)
            norm2(BLK - 1)
            for b in range(BLK - 3, BLK):
                put_norm2(b)
            act.wait_ge(s_route, SHIFTED)
            nc.scalar.activation(sume[0:P], sume[0:P], ACT.Exp).then_inc(s_se, 1)

            def expert_parts(n, u, i):
                act.wait_ge(s_fr[u], i * 32 + 32)
                act.wait_ge(s_up, n + 1)
                nc.scalar.activation(w12h[u][:], w12raw[u][:], ACT.Copy).then_inc(s_fh, 1)

            def rows_parts(n, u):
                act.wait_ge(s_gt, n + 1)
                act.wait_ge(s_up, n + 1)
                for c in range(2):
                    ins = nc.scalar.activation(xgh[:, u, 3 * c:3 * c + 3], bank(c)[:, 0:384].rearrange("p (k n) -> p k n", k=3), ACT.Copy)
                ins.then_inc(s_gh, 1)

            def expert(n, u):
                act.wait_ge(s_up, n + 3)
                nc.scalar.activation(gate[:], bank(2)[:, 0:FH], ACT.Silu).then_inc(s_sg, 1)

            def expert_hidden(n, u):
                act.wait_ge(s_ht, n + 1)
                act.wait_ge(s_y, n + 2)
                nc.scalar.activation(hidh[:], bank(3)[:, 0:FH].rearrange("p (k n) -> p k n", k=FC), ACT.Copy).then_inc(s_hh, 1)

            def expert_out(n, u, i):
                act.wait_ge(s_y, n + 3)
                act.wait_ge(s_ys[u], i * 16 + 16)
                for c in range(2):
                    ins = nc.scalar.activation(yb[:, u, HALF * c:HALF * c + HALF], bank(4 + c)[:, 0:HALF], ACT.Copy)
                ins.then_inc(s_yb, 1)
                act.wait_ge(s_yb, n + 1)
                act.dma_start(y_d.rearrange("(b p) d -> p b d", p=128)[:, bass.ds(n, 1), :], yb[:, u:u + 1, :]).then_inc(s_ys[u], 16)

            for i in range(2):
                act.sem_inc(s_ys[i], 16)

            def expert_turn(n, u, i, rows=True, parts=True):
                expert(n, u)
                if rows:
                    rows_parts(n + 1, 1 - u)
                expert_out(n - 1, 1 - u, i if u else i - 1)
                expert_hidden(n, u)
                if parts:
                    expert_parts(n + 2, u, i + 1)

            expert_parts(0, 0, 0)
            rows_parts(0, 0)
            expert_parts(1, 1, 0)
            expert(0, 0)
            rows_parts(1, 1)
            expert_hidden(0, 0)
            expert_parts(2, 0, 1)
            expert_turn(1, 1, 0)
            with act.Fori(1, SB // 2 - 1) as i:
                for u in range(2):
                    expert_turn(i * 2 + u, u, i)
            expert_turn(SB - 3, 0, SB // 2 - 1)
            expert_turn(SB - 2, 1, SB // 2 - 1, parts=False)
            expert_turn(SB - 1, 0, SB // 2, rows=False, parts=False)
            expert_out(SB - 1, 0, SB // 2)

        @block.vector
        def _(dve):
            chain = Chain(dve, c_dve)
            for a in range(2):
                for c in range(2):
                    nc.vector.memset(ind[64 * a:64 * a + 64, c:c + 1], 0.5 * NORM * NORM if a == c else 0.0).then_inc(s_cst, 1)

            nc.vector.memset(edi[:], PADV).then_inc(s_pad, 1)

            def edges_to_float():
                dve.wait_ge(s_e, 96)
                nc.vector.tensor_copy(edf[0:ER], edi[0:ER]).then_inc(s_prd, 1)

            def edge_columns():
                dve.wait_ge(s_pre, EDGE_COLS)
                nc.vector.tensor_scalar(dneg[:], bank(4)[:, 0:ET], -1.0, None, ALU.mult).then_inc(s_prd, 1)
                nc.vector.tensor_scalar(sneg[:], bank(5)[:, 0:ET], -1.0, None, ALU.mult).then_inc(s_prd, 1)
                nc.vector.tensor_reduce(tmm[0:ER, 0, :], edf[0:ER, 0], X_AXIS, ALU.min).then_inc(s_prd, 1)
                nc.vector.tensor_reduce(tmm[0:ER, 1, :], edf[0:ER, 0], X_AXIS, ALU.max).then_inc(s_prd, 1)

            def edge_ranges():
                dve.wait_ge(s_pre, EDGE_ROWS)
                chain(nc.vector.tensor_scalar(emask[0:BLK, 0], bank(5)[0:BLK, 0:ET], blo[0:BLK], None, ALU.is_ge))
                chain(nc.vector.tensor_scalar(emask[0:BLK, 1], bank(4)[0:BLK, 0:ET], blo[0:BLK], float(P), ALU.subtract, ALU.is_lt))
                chain(nc.vector.tensor_tensor(emask[0:BLK, 0], emask[0:BLK, 0], emask[0:BLK, 1], ALU.mult))
                g = gidx[0:BLK].rearrange("p g t -> p (g t)")
                chain(nc.vector.scalar_tensor_tensor(out=emask[0:BLK, 1], in0=g, scalar=1.0, in1=emask[0:BLK, 0],
                                                     op0=ALU.add, op1=ALU.mult))
                chain(nc.vector.reduce_max(emax[0:BLK, 0:1], emask[0:BLK, 1], X_AXIS))
                chain(nc.vector.tensor_scalar(emask[0:BLK, 1], g, -1.0, float(EG), ALU.mult, ALU.add))
                chain(nc.vector.tensor_tensor(emask[0:BLK, 1], emask[0:BLK, 1], emask[0:BLK, 0], ALU.mult))
                chain(nc.vector.reduce_max(emax[0:BLK, 1:2], emask[0:BLK, 1], X_AXIS))
                chain(nc.vector.tensor_scalar(elim[0:BLK, 1:2], emax[0:BLK, 0:1], 1.0, None, ALU.max))
                chain(nc.vector.tensor_scalar(elim[0:BLK, 0:1], emax[0:BLK, 1:2], -1.0, float(EG), ALU.mult, ALU.add))
                chain(nc.vector.tensor_scalar(elim[0:BLK, 2:3], elim[0:BLK, 1:2], -1.0, None, ALU.add))
                chain(nc.vector.tensor_tensor(elim[0:BLK, 0:1], elim[0:BLK, 0:1], elim[0:BLK, 2:3], ALU.min))
                nc.vector.tensor_tensor(elim[0:BLK, 2:3], elim[0:BLK, 1:2], elim[0:BLK, 0:1], ALU.subtract).then_inc(s_prd, 1)

            def edge_limits():
                dve.wait_ge(s_pre, LIMITS)
                chain(nc.vector.tensor_copy(limf[0:1, 0:30], bank(7)[0:1, 64:94]))
                chain(nc.vector.tensor_tensor(limf[0:1, 20:30], limf[0:1, 20:30], limf[0:1, 0:10], ALU.subtract))
                nc.vector.tensor_copy(limi[0:1, 0:30], limf[0:1, 0:30]).then_inc(s_prd, 1)

            def batch_norm():
                dve.wait_ge(s_bnv, 1)
                chain(nc.vector.tensor_copy(bnc[:], bank(7)[:, 0:5 * HC].rearrange("p (a c) -> p a c", a=5)))
                chain(nc.vector.reciprocal(bns[:, 0, :], bns[:, 0, :]))
                chain(nc.vector.tensor_tensor(bns[:, 1, :], bns[:, 0, :], bnc[:, 0, :], ALU.mult))
                chain(nc.vector.tensor_tensor(bnc[:, 4, :], bnc[:, 4, :], bnc[:, 2, :], ALU.subtract))
                chain(nc.vector.tensor_tensor(bnc[:, 4, :], bnc[:, 4, :], bns[:, 1, :], ALU.mult))
                nc.vector.tensor_tensor(bns[:, 2, :], bnc[:, 4, :], bnc[:, 1, :], ALU.add).then_inc(s_prd, 1)

            def normalise(b):
                nc.vector.tensor_scalar(xn[0:P, b], xin[0:P, b], meanvar[0:P, b, 0:1], rstd[0:P, b:b + 1],
                                        ALU.subtract, ALU.mult).then_inc(s_xn, 1)

            def low_parts(b):
                for i in range(2):
                    dve.wait_ge(s_xth, 2 * b + i + 1)
                    nc.vector.tensor_tensor(XTl[:, 3 * i:3 * i + 3, P * b:P * b + P],
                                            bank(2 * (b % 2) + i)[:, 0:375].rearrange("p (k n) -> p k n", k=3),
                                            XTh[:, 3 * i:3 * i + 3, P * b:P * b + P].bitcast(F32),
                                            ALU.subtract).then_inc(s_xtl, 1)

            for h in range(2):
                for b in range(PAIRS * h, PAIRS * (h + 1)):
                    dve.wait_ge(s_x[b // 2], 32)
                    for i in range(2):
                        ins = nc.vector.bn_stats(stats[0:P, b, 6 * i:6 * i + 6], xin[0:P, b, 384 * i:384 * i + 384])
                    chain(ins)
                    nc.vector.bn_aggr(meanvar[0:P, b, :], stats[0:P, b, :]).then_inc(s_var, 1)
                dve.wait_ge(s_sd, h + 1)
                chain(nc.vector.reciprocal(rstd[0:P, PAIRS * h:PAIRS * (h + 1)], stdev[0:P, PAIRS * h:PAIRS * (h + 1)]))
                if h == 1:
                    nc.vector.tensor_scalar(twice[0:P], rstd[0:P], 1.0, None, ALU.add)
                    chain(nc.vector.scalar_tensor_tensor(out=shift[0:P], in0=meanvar[0:P, :, 0], scalar=-1.0, in1=rstd[0:P],
                                                         op0=ALU.mult, op1=ALU.mult))
                for b in range(PAIRS * h, PAIRS * (h + 1)):
                    normalise(b)
                    if b >= 1:
                        low_parts(b - 1)
                    {0: edges_to_float, 2: edge_columns, 4: edge_ranges, 6: batch_norm, 7: edge_limits}.get(b, lambda: None)()
            low_parts(BLK - 1)
            dve.wait_ge(s_pre, PROJ_T)
            chain(nc.vector.memset(pscaled[:], 0.0))
            for a in range(2):
                chain(nc.vector.tensor_scalar(pscaled[64 * a:64 * a + 64, M * a:M * a + M], bank(6)[64 * a:64 * a + 64, 0:M],
                                              NORM, None, ALU.mult))
            chain(nc.vector.tensor_copy(projh[:], pscaled[:]))
            nc.vector.tensor_tensor(projl[:], pscaled[:], projh[:].bitcast(F32), ALU.subtract).then_inc(s_prd, 1)
            dve.wait_ge(s_prd, PROJ_D)
            nc.vector.reduce_max(gmax[:], XTh[:].bitcast(F32).rearrange("p k n -> p (k n)"), X_AXIS).then_inc(s_prd, 1)

            def route():
                grid = [P, BLK, NE]
                chain(nc.vector.reduce_max(best[0:P], logit[0:P], X_AXIS))
                chain(nc.vector.tensor_tensor(logit[0:P], logit[0:P], best[0:P].unsqueeze(2).to_broadcast(grid), ALU.subtract))
                nc.vector.tensor_copy(sume[0:P], logit[0:P]).then_inc(s_route, 1)
                chain(nc.vector.tensor_scalar(logit[0:P], logit[0:P], 0.0, None, ALU.is_equal))
                chain(nc.vector.tensor_tensor(logit[0:P], logit[0:P], down[0:P].unsqueeze(1).to_broadcast(grid), ALU.mult))
                chain(nc.vector.reduce_max(best[0:P], logit[0:P], X_AXIS))
                nc.vector.tensor_tensor(onehot[0:P], logit[0:P], best[0:P].unsqueeze(2).to_broadcast(grid), ALU.is_equal).then_inc(s_route, 1)
                dve.wait_ge(s_se, 1)
                chain(nc.vector.reduce_sum(prob[0:P], sume[0:P], X_AXIS))
                chain(nc.vector.reciprocal(prob[0:P], prob[0:P]))
                dve.wait_ge(s_rk, 1)
                chain(nc.vector.memset(carry[0:P, 0], 0.0))
                for b in range(BLK):
                    chain(nc.vector.tensor_tensor(carry[0:P, b + 1], carry[0:P, b], bank(6)[0:P, NE * b:NE * b + NE], ALU.add))
                chain(nc.vector.tensor_tensor(cmpe[0:P], carry[0:P, BLK].unsqueeze(2).to_broadcast([P, NE, BLK]),
                                              k128[0:P, 0:BLK].unsqueeze(1).to_broadcast([P, NE, BLK]), ALU.is_gt))
                chain(nc.vector.reduce_sum(nblk[0:P], cmpe[0:P], X_AXIS))
                chain(nc.vector.tensor_copy(endb[0:P, 0:1], nblk[0:P, 0:1]))
                for e in range(1, NE):
                    chain(nc.vector.tensor_tensor(endb[0:P, e:e + 1], endb[0:P, e - 1:e], nblk[0:P, e:e + 1], ALU.add))
                chain(nc.vector.tensor_tensor(cmpb[:], upto[0:1].unsqueeze(2).to_broadcast([1, SB, NE]),
                                              endb[0:1].unsqueeze(1).to_broadcast([1, SB, NE]), ALU.is_ge))
                chain(nc.vector.reduce_sum(expf[:], cmpb[:], X_AXIS))
                chain(nc.vector.tensor_scalar(expf[:], expf[:], float(NE - 1), None, ALU.min))
                nc.vector.tensor_copy(expi[:], expf[:]).then_inc(s_route, 1)
                chain(nc.vector.tensor_tensor(nblk[0:P], endb[0:P], nblk[0:P], ALU.subtract))
                chain(nc.vector.tensor_scalar(nblk[0:P], nblk[0:P], 128.0, None, ALU.mult))
                chain(nc.vector.tensor_tensor(sume[0:P], bank(5)[0:P, 0:BLK * NE].rearrange("p (b e) -> p b e", b=BLK), carry[0:P, 0:BLK], ALU.add))
                chain(nc.vector.tensor_tensor(sume[0:P], sume[0:P], nblk[0:P].unsqueeze(1).to_broadcast(grid), ALU.add))
                chain(nc.vector.tensor_tensor(sume[0:P], sume[0:P], onehot[0:P], ALU.mult))
                chain(nc.vector.reduce_sum(pos[0:P], sume[0:P], X_AXIS))
                chain(nc.vector.tensor_copy(idxy[0:P], pos[0:P]))
                chain(nc.vector.tensor_tensor(cmpk[0:P], pos[0:P].unsqueeze(2).to_broadcast([P, BLK, SB - 1]),
                                              k128[0:P, 1:SB].unsqueeze(1).to_broadcast([P, BLK, SB - 1]), ALU.is_ge))
                chain(nc.vector.reduce_sum(quo[0:P], cmpk[0:P], X_AXIS))
                chain(nc.vector.scalar_tensor_tensor(out=pos[0:P], in0=quo[0:P], scalar=128.0, in1=pos[0:P], op0=ALU.mult, op1=ALU.subtract))
                chain(nc.vector.tensor_tensor(rhot[0:P], minus[0:P, 0:128].unsqueeze(1).to_broadcast([P, BLK, 128]),
                                              pos[0:P].unsqueeze(2).to_broadcast([P, BLK, 128]), ALU.is_equal))
                chain(nc.vector.tensor_tensor(qtok[0:P], upto[0:P].unsqueeze(1).to_broadcast([P, BLK, SB]),
                                              quo[0:P].unsqueeze(2).to_broadcast([P, BLK, SB]), ALU.is_equal))
                nc.vector.tensor_tensor(qtok[0:P], qtok[0:P], tokid[0:P].unsqueeze(2).to_broadcast([P, BLK, SB]), ALU.mult).then_inc(s_route, 1)
                dve.wait_ge(s_tt, 1)
                nc.vector.tensor_copy(tok[:], bank(7)[:, 0:SB]).then_inc(s_tok, 1)

            def stabiliser():
                dve.wait_ge(s_pre, MAX_T)
                chain(nc.vector.reduce_max(mrow[0:1, 0:1], bank(7)[0:1, 0:128], X_AXIS))
                chain(nc.vector.tensor_scalar(mrow[0:1, 1:2], mrow[0:1, 0:1], 0.0, 1e-7, ALU.max, ALU.add))
                chain(nc.vector.tensor_tensor(mrow[0:1, 2:3], mrow[0:1, 1:2], tb[0:1, :], ALU.mult))
                chain(nc.vector.scalar_tensor_tensor(out=mrow[0:1, 3:4], in0=tb[0:1, :], scalar=1e-7, in1=mrow[0:1, 2:3],
                                                     op0=ALU.mult, op1=ALU.max))
                chain(nc.vector.tensor_scalar(mrow[0:1, 4:5], mrow[0:1, 3:4], -1.0, SHIFT, ALU.mult, ALU.add))
                nc.vector.scalar_tensor_tensor(out=mrow[0:1, 5:6], in0=tb[0:1, :], scalar=1e-7, in1=mrow[0:1, 4:5],
                                               op0=ALU.mult, op1=ALU.add).then_inc(s_prd, 1)

            turns = turn_limits(nc.vector)
            offsets = turn_offsets(nc.vector)
            first = chain.n
            PER = 6 + 3 * BLK

            with dve.Fori(0, HP) as j:
                chain.at(j * PER + first)

                def low_bank(low, high, ready, done, n):
                    c0, c1 = BANKS[n]
                    dve.wait_ge(ready, 3 * j + n + 1)
                    nc.vector.tensor_tensor(low[:, c0:c1], PB[:, c0:c1], high[:, c0:c1].bitcast(F32), ALU.subtract).then_inc(done, 1)

                for n in range(3):
                    low_bank(KTl, KTh, s_kh, s_kl, n)
                for u in range(BLK):
                    dve.wait_ge(s_kd, BLK * j + u + 1)
                    chain(nc.vector.reduce_max(kmax[0:P, u], bank(KBANK[u % 4])[0:P, :].rearrange("p (a m) -> p a m", a=2), X_AXIS))
                    nc.vector.tensor_scalar(kneg[0:P, u], kmax[0:P, u], -1.0, None, ALU.mult).then_inc(s_kb, 1)
                chain(nc.vector.reduce_max(km[0:P], kmax[0:P].rearrange("p b a -> p a b"), X_AXIS))
                nc.vector.sem_inc(s_ksum, 1)
                dve.wait_ge(s_kdg, j + 1)
                nc.vector.tensor_copy(kdiag[0:P], bank(5)[0:P, 256:276].rearrange("p (b a) -> p b a", a=2)).then_inc(s_kdc, 1)
                dve.wait_ge(s_kdc, j + 1)
                chain(nc.vector.tensor_tensor(kexp[0:P], kmax[0:P], kdiag[0:P], ALU.subtract))
                dve.wait_ge(s_vtp, j + 1)
                chain(nc.vector.reduce_sum(vsum[0:P, :, 0:DH], PA[0:P, 0:1280].rearrange("p (b a d) -> p a d b", b=BLK, a=2), X_AXIS))
                chain(nc.vector.tensor_scalar(vsum[0:P, :, 0:DH], vsum[0:P, :, 0:DH], RATIO * EPS, None, ALU.mult))
                low_bank(QTl, QTh, s_qh, s_ql, 0)
                dve.wait_ge(s_kmT, j + 1)
                chain(nc.vector.reduce_max(gmx[0:2, :], bank(6)[0:2, 0:P], X_AXIS))
                nc.vector.tensor_scalar(dg[0:2, :], ident[0:2, 0:2], gmx[0:2, :], None, ALU.mult).then_inc(s_dg, 1)
                low_bank(QTl, QTh, s_qh, s_ql, 1)
                dve.wait_ge(s_stb, j + 1)
                nc.vector.tensor_scalar(nstab[0:P, :], bank(7)[0:P, 0:2], -1.0, None, ALU.mult).then_inc(s_stc, 1)
                low_bank(QTl, QTh, s_qh, s_ql, 2)
                dve.wait_ge(s_kf, j + 1)
                for b0, b1 in ((0, 8), (8, BLK)):
                    nc.vector.scalar_tensor_tensor(out=V[0:P, b0:b1, :, 0:DH],
                                                   in0=PA[0:P, 128 * b0:128 * b1].rearrange("p (b a d) -> p b a d", b=b1 - b0, a=2),
                                                   scalar=RATIO, in1=kfac[0:P, b0:b1].unsqueeze(3).to_broadcast([P, b1 - b0, 2, DH]),
                                                   op0=ALU.mult, op1=ALU.mult)
                nc.vector.tensor_scalar(V[0:P, :, :, DH], kfac[0:P], RATIO, None, ALU.mult).then_inc(s_v, 1)
                dve.wait_ge(s_qdg, j + 1)
                chain(nc.vector.tensor_copy(qdiag[0:P], bank(5)[0:P, 256:276].rearrange("p (b a) -> p b a", a=2)))

                def bias(u):
                    dve.wait_ge(s_qd, BLK * j + u + 1)
                    chain(nc.vector.reduce_max(qmx[0:P, u % 2], bank(6 + u % 2)[0:P, :].rearrange("p (a m) -> p a m", a=2), X_AXIS))
                    nc.vector.scalar_tensor_tensor(out=qbias[0:P, u % 2, :], in0=qmx[0:P, u % 2], scalar=-1.0,
                                                   in1=qdiag[0:P, u, :], op0=ALU.mult,
                                                   op1=ALU.subtract).then_inc(s_qb, 1)

                def features(u):
                    dve.wait_ge(s_qt, BLK * j + u + 1)
                    if u >= 2:
                        dve.wait_ge(s_o, BLK * j + u - 1)
                    nc.vector.tensor_scalar(qpT[:, u % 2], bank(1 + u % 2)[:, 0:4 * P].rearrange("p (a c n) -> p a c n", a=2, c=2),
                                            EPS, RATIO, ALU.add, ALU.mult).then_inc(s_qp, 1)

                def normal(u):
                    o = bank(3 * (u % 2))[0:P, 0:130].rearrange("p (a d) -> p a d", a=2)
                    dve.wait_ge(s_o, BLK * j + u + 1)
                    chain(nc.vector.reciprocal(rden[0:P, u % 2], o[:, :, DH]))
                    nc.vector.tensor_tensor(att[0:P, u, :].rearrange("p (a d) -> p a d", a=2), o[:, :, 0:DH],
                                            rden[0:P, u % 2].unsqueeze(2).to_broadcast([P, 2, DH]), ALU.mult).then_inc(s_at, 1)

                for u in range(BLK + 4):
                    if u < BLK:
                        bias(u)
                    if 2 <= u < BLK + 2:
                        features(u - 2)
                    if u >= 4:
                        normal(u - 4)
                assert chain.n == PER, (chain.n, PER)
            chain.at(first + HP * PER)
            stabiliser()

            for n in range(2 * BLK + 2):
                if n == 4:
                    dve.wait_ge(s_pre, STAB)
                    nc.vector.tensor_copy(mbias[:], bank(7)[:, 0:1]).then_inc(s_prd, 1)
                if n == 3:
                    dve.wait_ge(s_woh, 2)
                    nc.vector.tensor_tensor(wol[1][:], woraw[:], woh[1][:].bitcast(F32), ALU.subtract).then_inc(s_wol, 1)
                if n < 2 * BLK:
                    b = n % BLK
                    dve.wait_ge(s_ath, n + 1)
                    nc.vector.tensor_tensor(attl[:, n % 2], attT[:, :, P * b:P * b + P], atth[:, n % 2].bitcast(F32),
                                            ALU.subtract).then_inc(s_atl, 1)
                if n >= 2:
                    o = n - 2
                    dve.wait_ge(s_ow, o + 1)
                    dve.wait_ge(s_rl[o % 2], 16 * (o // 2 + 1))
                    if o == 0:
                        dve.wait_ge(s_b2, 16)
                    h, b = o // BLK, o % BLK
                    chain(nc.vector.scalar_tensor_tensor(out=rtile[0:P, o % 2], in0=rtile[0:P, o % 2], scalar=twice[0:P, b:b + 1],
                                                         in1=bank(o % 2)[0:P, 0:HALF], op0=ALU.mult, op1=ALU.add))
                    nc.vector.scalar_tensor_tensor(out=rtile[0:P, o % 2], in0=rtile[0:P, o % 2], scalar=shift[0:P, b:b + 1],
                                                   in1=b2row[0:P, HALF * h:HALF * h + HALF], op0=ALU.add, op1=ALU.add).then_inc(s_ro, 1)

            def exponentials(c):
                if c >= K:
                    return
                u = c % 2
                if c == 0:
                    dve.wait_ge(s_ow, 2 * BLK)
                dve.wait_ge(s_ex, c + 1)
                nc.vector.scalar_tensor_tensor(out=msg[0:P, u], in0=msg[0:P, u], scalar=1e-7, in1=Ef[0:P], op0=ALU.add, op1=ALU.mult)\
                    .then_inc(s_mm, 1)

            for b in range(BLK):
                if b in (3, 6):
                    exponentials(b // 6)
                with dve.Fori(turns[b], turns[b + 1]) as n:
                    g = nc.s_assert_within(n + offsets[b], 0, EG - 1, skip_runtime_bounds_check_because="turns map to groups first .. end - 1 of the block, all within the list")
                    for u in range(GT):
                        dve.wait_ge(s_ohf, n * GT + u + 1)
                        if u % 2:
                            nc.vector.tensor_scalar(ohd[:, u, :], minus[:, P * b:P * b + P], dneg[:, bass.ds(g * GT + u, 1)], None, ALU.is_equal)
                        nc.vector.tensor_scalar(ohs[:, u, :], minus[:], sneg[:, bass.ds(g * GT + u, 1)], None, ALU.is_equal).then_inc(s_oh, 1)

            for c in range(K):
                if c >= 1:
                    exponentials(c + 1)
                dve.wait_ge(s_sum, 2 * c + 1)
                chain(nc.vector.tensor_scalar(rec[:], PS[:, 0:N], 1e-37, None, ALU.max))
                nc.vector.sem_inc(s_sumr, 1)
                chain(nc.vector.reciprocal(rec[:], rec[:]))
                dve.wait_ge(s_sum, 2 * c + 2)
                chain(nc.vector.tensor_tensor(agg[:], PS[:, 1536:1536 + N], rec[:], ALU.mult))
                nc.vector.sem_inc(s_sumr, 1)
                chain(nc.vector.tensor_tensor(agg[:], agg[:], XTh[:, c, :].bitcast(F32), ALU.add))
                nc.vector.tensor_tensor(agg[:], agg[:], XTl[:, c, :].bitcast(F32), ALU.add).then_inc(s_ag, 1)
                dve.wait_ge(s_agh, c + 1)
                nc.vector.tensor_tensor(XTl[:, c, :], agg[:], XTh[:, c, :].bitcast(F32), ALU.subtract).then_inc(s_agl, 1)
                dve.wait_ge(s_agl, c + 1)

            def w1_parts(m):
                if m < HC:
                    dve.wait_ge(s_w1h, m + 1)
                    nc.vector.tensor_tensor(w1l[:, m % 2], w1raw[:, m % 2], w1h[:, m % 2].bitcast(F32), ALU.subtract).then_inc(s_w1l, 1)

            def w2_parts(i):
                k = 3 * (i % 4)
                dve.wait_ge(s_w2h, i + 1)
                nc.vector.tensor_tensor(w2l[i // 4][:, k:k + 3, :], w2raw[:, i % 2], w2h[i // 4][:, k:k + 3, :].bitcast(F32),
                                        ALU.subtract).then_inc(s_w2l, 1)

            for m in range(HC):
                w1_parts(m)
                if 5 <= m < 9:
                    w2_parts(m - 5)

            def hidden_parts(n):
                if n < 2 * BLK:
                    b = n % BLK
                    dve.wait_ge(s_hth, n + 1)
                    nc.vector.tensor_tensor(htl[n % 2][:], HT[:, :, P * b:P * b + P], hth[n % 2][:].bitcast(F32), ALU.subtract).then_inc(s_htl, 1)

            def second_layer(n):
                h, b = n // BLK, n % BLK
                dve.wait_ge(s_o2, n + 1)
                dve.wait_ge(s_r2l[n % 2], 16 * (n // 2 + 1))
                where = rtile2[0:P, n % 2] if h == 0 else x1[0:P, b, HALF:D]
                nc.vector.tensor_tensor(where, rtile2[0:P, n % 2], bank(n % 2)[0:P, 0:HALF], ALU.add).then_inc(s_r2, 1)

            def norm2(b):
                if b == 0:
                    dve.wait_ge(s_x1l, 16)
                dve.wait_ge(s_r2, BLK + b + 1)
                for i in range(2):
                    chain(nc.vector.bn_stats(stats2[0:P, b, 6 * i:6 * i + 6], x1[0:P, b, HALF * i:HALF * i + HALF]))
                nc.vector.bn_aggr(mv2[0:P, b, :], stats2[0:P, b, :]).then_inc(s_v2, 1)

            def apply_norm2(b):
                dve.wait_ge(s_sd2, b + 1)
                chain(nc.vector.reciprocal(sd2[0:P, b:b + 1], sd2[0:P, b:b + 1]))
                if b >= 2:
                    dve.wait_ge(s_xn2s[b % 2], 16 * (b // 2))
                    dve.wait_ge(s_x2t, b - 1)
                nc.vector.tensor_scalar(xn2[0:P, b % 2], x1[0:P, b], mv2[0:P, b, 0:1], sd2[0:P, b:b + 1],
                                        ALU.subtract, ALU.mult).then_inc(s_xn2, 1)

            hidden_parts(0)
            hidden_parts(1)
            for i in range(4, 8):
                w2_parts(i)
                second_layer(i - 4)
                hidden_parts(i - 2)
            for n in range(6, 2 * BLK + 2):
                hidden_parts(n)
                second_layer(n - 2)
                if n >= BLK + 2:
                    norm2(n - BLK - 2)
                    apply_norm2(n - BLK - 2)
            dve.wait_ge(s_lg, BLK)
            chain(nc.vector.tensor_copy(logit[0:P], bank(4)[0:P, 0:NE * BLK].rearrange("p (b e) -> p b e", b=BLK)))
            route()

            def expert_parts(n, u):
                dve.wait_ge(s_fh, n + 1)
                nc.vector.tensor_tensor(w12l[u][:], w12raw[u][:], w12h[u][:].bitcast(F32), ALU.subtract).then_inc(s_fl, 1)

            def rows_parts(n, u):
                dve.wait_ge(s_gh, n + 1)
                for c in range(2):
                    ins = nc.vector.tensor_tensor(xgl[:, u, 3 * c:3 * c + 3], bank(c)[:, 0:384].rearrange("p (k n) -> p k n", k=3),
                                                  xgh[:, u, 3 * c:3 * c + 3].bitcast(F32), ALU.subtract)
                ins.then_inc(s_gl, 1)

            def expert_gate(n):
                dve.wait_ge(s_sg, n + 1)
                nc.vector.tensor_tensor(hid[:], gate[:], bank(2)[:, FH:2 * FH], ALU.mult).then_inc(s_hd, 1)

            def expert_hidden(n):
                dve.wait_ge(s_hh, n + 1)
                nc.vector.tensor_tensor(hidl[:], bank(3)[:, 0:FH].rearrange("p (k n) -> p k n", k=FC), hidh[:].bitcast(F32),
                                        ALU.subtract).then_inc(s_hl, 1)

            def expert_down_parts(n, u, i, used=True):
                dve.wait_ge(s_f3r[u], i * 16 + 16)
                if used:
                    dve.wait_ge(s_y, n + 1)
                nc.vector.tensor_copy(w3h[u][:], w3raw[u][:]).then_inc(s_f3h, 1)

            def expert_turn(n, u, i, rows=True, parts=True):
                expert_gate(n)
                if rows:
                    rows_parts(n + 1, 1 - u)
                expert_hidden(n)
                if rows:
                    expert_down_parts(n + 1, 1 - u, i + 1 if u else i)
                if parts:
                    expert_parts(n + 2, u)

            expert_parts(0, 0)
            expert_down_parts(0, 0, 0, used=False)
            rows_parts(0, 0)
            expert_parts(1, 1)
            with dve.Fori(0, SB // 2 - 1) as i:
                for u in range(2):
                    expert_turn(i * 2 + u, u, i)
            expert_turn(SB - 3, 0, SB // 2 - 1)
            expert_turn(SB - 2, 1, SB // 2 - 1, parts=False)
            expert_turn(SB - 1, 0, SB // 2, rows=False, parts=False)
            for b in range(BLK):
                dve.wait_ge(s_g[b // PAIRS], 16 * (len(range(b // PAIRS, SB, 2)) + PAIRS))
                nc.vector.scalar_tensor_tensor(out=x1[0:P, b], in0=yg[0:P, b], scalar=prob[0:P, b:b + 1], in1=x1[0:P, b],
                                               op0=ALU.mult, op1=ALU.add).then_inc(s_fin, 1)

        @block.tensor
        def _(pe):
            pe.wait_ge(s_cst, 16)
            for b in range(BLK):
                pe.wait_ge(s_xn, b + 1)
                for i in range(2):
                    if b >= 2:
                        pe.wait_ge(s_xtl, 2 * (b - 2) + i + 1)
                    for c in range(3):
                        ins = nc.tensor.transpose(bank(2 * (b % 2) + i)[:, P * c:P * c + P],
                                                  xn[0:P, b, 384 * i + 128 * c:384 * i + 128 * c + 128], ident[0:P, 0:P])
                    ins.then_inc(s_xt, 1)
                if b == 1:
                    pe.wait_ge(s_prd, EDGE_F)
                    for i in range(2):
                        for g in range(3):
                            ins = nc.tensor.transpose(bank(4 + i)[:, ER * g:ER * g + ER], edf[0:ER, i, g, :], ident[0:ER, 0:ER])
                    ins.then_inc(s_pre, 1)
                    pe.wait_ge(s_par, 128)
                    nc.tensor.transpose(bank(7)[:, 0:5 * HC], bnr[0:5 * HC, :], ident[0:5 * HC, 0:5 * HC]).then_inc(s_pre, 1)
                if b == 3:
                    pe.wait_ge(s_prd, EDGE_MM)
                    for i in range(2):
                        for g in range(3):
                            ins = nc.tensor.matmul(bank(4 + i)[0:BLK, ER * g:ER * g + ER], tmm[0:ER, i, g:g + 1].to_broadcast([ER, BLK]),
                                                   ident[0:ER, 0:ER], start=True, stop=True)
                    ins.then_inc(s_pre, 1)
                if b == 6:
                    pe.wait_ge(s_prd, EDGE_EL)
                    pe.wait_ge(s_prd, BN_D)
                    nc.tensor.matmul(bank(7)[0:1, 64:64 + BLK], elim[0:BLK, 2:3], tri[0:BLK, 0:BLK], start=True, stop=True)
                    nc.tensor.matmul(bank(7)[0:1, 64 + BLK:64 + 2 * BLK], elim[0:BLK, 2:3], tri[0:BLK, 0:BLK], start=True, stop=False)
                    nc.tensor.matmul(bank(7)[0:1, 64 + BLK:64 + 2 * BLK], elim[0:BLK, 2:3], ident[0:BLK, 0:BLK], start=False, stop=True)
                    ins = nc.tensor.matmul(bank(7)[0:1, 64 + 2 * BLK:64 + 3 * BLK], elim[0:BLK, 0:1], ident[0:BLK, 0:BLK], start=True, stop=True)
                    ins.then_inc(s_pre, 1)
            pe.wait_ge(s_par, 128)
            for c in range(2):
                ins = nc.tensor.transpose(bank(6)[:, 128 * c:128 * c + 128], praw[:, c, :], ident[:])
            ins.then_inc(s_pre, 1)
            pe.wait_ge(s_prd, LIM_I)
            turns = turn_limits(nc.tensor)
            pe.wait_ge(s_xtl, 2 * BLK)

            def project(j, n, where, done, i):
                c0, c1 = BANKS[i]
                for k in range(K):
                    for w, xt in ((wh, XTh), (wh, XTl), (wl, XTh)):
                        ins = nc.tensor.matmul(where[:, c0:c1], w[:, n, k, :], xt[:, k, c0:c1],
                                               start=(k == 0 and w is wh and xt is XTh), stop=(k == K - 1 and w is wl))
                ins.then_inc(done, 1)

            def head_pair(j, last):
                def dash(u, th, tl, where):
                    for q, w in ((th, projh), (th, projl), (tl, projh)):
                        ins = nc.tensor.matmul(bank(where)[0:P, :], q[:, P * u:P * u + P], w[:],
                                               start=(q is th and w is projh), stop=(q is tl))
                    return ins

                def diag():
                    for b in range(BLK):
                        ins = nc.tensor.matmul(bank(5)[0:P, 256 + 2 * b:258 + 2 * b], sq[:, P * b:P * b + P], ind[:], start=True, stop=True)
                    return ins

                def context(a):
                    where = bank(3)[0:DH + 1, M * a:M * a + M]
                    for b in range(BLK):
                        nc.tensor.matmul(where, V[0:P, b, a, :], kp[0:P, a, b, :], start=(b == 0), stop=False)
                    return nc.tensor.matmul(where, vsum[0:P, a, :], ones[0:P, 0:1].to_broadcast([P, M]), start=False, stop=True)

                def turn_context():
                    pe.wait_ge(s_cxs, 2 * j + 1)
                    for g in range(4):
                        ins = nc.tensor.transpose(bank(3)[:, 65 * g:65 * g + 65], ctxT[0:DH + 1, 128 * g:128 * g + 128], ident[0:DH + 1, 0:DH + 1])
                    ins.then_inc(s_cx, 1)

                def turn(u):
                    pe.wait_ge(s_qe, BLK * j + u + 1)
                    for a in range(2):
                        for c in range(2):
                            g = 2 * a + c
                            ins = nc.tensor.transpose(bank(1 + u % 2)[:, P * g:P * g + P], qe[0:P, u % 2, a, 128 * c:128 * c + 128], ident[0:P, 0:P])
                    ins.then_inc(s_qt, 1)

                def attend(u):
                    pe.wait_ge(s_qp, BLK * j + u + 1)
                    if u >= 2:
                        pe.wait_ge(s_at, BLK * j + u - 1)
                    if u == 0:
                        pe.wait_ge(s_cxs, 2 * j + 2)
                    for a in range(2):
                        for c in range(2):
                            ins = nc.tensor.matmul(bank(3 * (u % 2))[0:P, 65 * a:65 * a + 65], qpT[:, u % 2, a, c, :], ctxs[:, a, c, :], start=(c == 0), stop=(c == 1))
                    ins.then_inc(s_o, 1)

                def turn_att(b):
                    pe.wait_ge(s_at, BLK * j + b + 1)
                    if b == 1:
                        pe.wait_ge(s_qb, BLK * j + 1)
                    if b >= 2:
                        pe.wait_ge(s_as, BLK * j + b - 1)
                    nc.tensor.transpose(bank(4 + b % 2)[:, 0:P], att[0:P, b, :], ident[0:P, 0:P]).then_inc(s_aT, 1)

                def step(u, attends=True):
                    if u < BLK:
                        pe.wait_ge(s_qe, BLK * j + u - 1)
                        dash(u, QTh, QTl, 6 + u % 2).then_inc(s_qd, 1)
                    if u - 2 < BLK:
                        turn(u - 2)
                    if attends and 0 <= u - 3 < BLK:
                        attend(u - 3)
                    if u >= 5:
                        turn_att(u - 5)

                for i in range(3):
                    project(j, 0, PB, s_kps, i)
                pe.wait_ge(s_vt, j + 1)
                for b in range(BLK):
                    ins = nc.tensor.transpose(PA[0:P, 128 * b:128 * b + 128], VT[:, P * b:P * b + P], ident[:])
                ins.then_inc(s_vtp, 1)
                for u in range(BLK):
                    if u in (0, 3, 8):
                        pe.wait_ge(s_kl, 3 * j + (u + 5) // 4)
                    if u >= 4:
                        pe.wait_ge(s_ke, BLK * j + u - 3)
                    dash(u, KTh, KTl, KBANK[u % 4]).then_inc(s_kd, 1)
                diag().then_inc(s_kdg, 1)
                pe.wait_ge(s_ke, BLK * j + BLK - 2)
                project(j, 2, PB, s_qps, 0)
                pe.wait_ge(s_ksum, j + 1)
                pe.wait_ge(s_ke, BLK * j + BLK)
                nc.tensor.transpose(bank(6)[0:2, 0:P], km[0:P, :], ident[0:P, 0:P]).then_inc(s_kmT, 1)
                project(j, 2, PB, s_qps, 1)
                pe.wait_ge(s_dg, j + 1)
                nc.tensor.matmul(bank(7)[0:P, 0:2], ones[0:2, 0:P], dg[0:2, :], start=True, stop=True).then_inc(s_stb, 1)
                pe.wait_ge(s_kdc, j + 1)
                project(j, 2, PB, s_qps, 2)
                pe.wait_ge(s_stc, j + 1)
                pe.wait_ge(s_ql, 3 * j + 1)
                dash(0, QTh, QTl, 6).then_inc(s_qd, 1)
                dash(1, QTh, QTl, 7).then_inc(s_qd, 1)
                pe.wait_ge(s_ql, 3 * j + 3)
                diag().then_inc(s_qdg, 1)
                pe.wait_ge(s_v, j + 1)
                context(0)
                step(2)
                context(1).then_inc(s_cx, 1)
                step(3, attends=False)
                pe.wait_ge(s_qe, BLK * j + 3)
                dash(4, QTh, QTl, 6).then_inc(s_qd, 1)
                turn_context()
                pe.wait_ge(s_qp, BLK * j + 1)
                turn(2)
                attend(0)
                attend(1)
                for u in range(5, BLK + 3):
                    step(u)
                if not last:
                    pe.wait_ge(s_wok, j + 2)
                    project(j + 1, 1, PA, s_vps, 1)
                turn_att(BLK - 2)
                if not last:
                    project(j + 1, 1, PA, s_vps, 2)
                turn_att(BLK - 1)
                if not last:
                    project(j + 1, 1, PA, s_vps, 0)
                pe.wait_ge(s_as, BLK * j + BLK)

            pe.wait_ge(s_wok, 1)
            for i in range(3):
                project(0, 1, PA, s_vps, i)
            pe.wait_ge(s_prd, PROJ_D)
            with pe.Fori(0, HP - 1) as j:
                head_pair(j, last=False)
            head_pair(HP - 1, last=True)

            pe.wait_ge(s_prd, GMAX_D)
            nc.tensor.transpose(bank(7)[0:1, 0:128], gmax[:], ident[:]).then_inc(s_pre, 1)
            def project_attention(n, u, h, free=True):
                pe.wait_ge(s_atl, n + 1)
                if free:
                    pe.wait_ge(s_ro, n - 1)
                for k in range(K):
                    for q, w in ((atth, woh), (atth, wol), (attl, woh)):
                        ins = nc.tensor.matmul(bank(u)[0:P, 0:HALF], q[:, u, k, :], w[h][:, k, :],
                                               start=(k == 0 and q is atth and w is woh), stop=(k == K - 1 and q is attl))
                ins.then_inc(s_ow, 1)

            pe.wait_ge(s_wol, 1)
            for n in range(2):
                project_attention(n, n, 0, free=False)
            pe.wait_ge(s_prd, MROW_D)
            nc.tensor.matmul(bank(7)[:, 0:1], ones[0:1, :], mrow[0:1, 5:6], start=True, stop=True).then_inc(s_pre, 1)
            with pe.Fori(1, BLK // 2) as i:
                for u in range(2):
                    project_attention(i * 2 + u, u, 0)
            pe.wait_ge(s_wol, 2)
            with pe.Fori(BLK // 2, BLK) as i:
                for u in range(2):
                    project_attention(i * 2 + u, u, 1)

            pe.wait_ge(s_ro, 2 * BLK)
            pe.wait_ge(s_prd, STAB_D)
            pe.sem_inc(s_ohf, GT)

            def turn_counts(b):
                pe.wait_ge(s_cr, b + 1)
                for i in range(3):
                    if 3 * b + i >= 2:
                        pe.wait_ge(s_cs, 3 * b + i - 1)
                    for c in range(min(4, BLK - 4 * i)):
                        ins = nc.tensor.transpose(bank(6 + (3 * b + i) % 2)[0:P, P * c:P * c + P],
                                                  crow[0:P, b % 2, P * (4 * i + c):P * (4 * i + c) + P], ident[0:P, 0:P])
                    ins.then_inc(s_ct, 1)

            for b in range(BLK):
                if b >= 2:
                    pe.wait_ge(s_cr, b - 1)
                counts = PS[0:P, 1536 * (b % 2):1536 * (b % 2) + 1536]
                for c in range(3):
                    nc.tensor.matmul(counts[:, 512 * c:512 * c + 512], zeros[:, 0:P], zeros[:], start=True, stop=False, skip_group_check=True)
                with pe.Fori(turns[b], turns[b + 1]) as n:
                    for u in range(GT):
                        if u % 2 == 0:
                            pe.wait_ge(s_od, n * (GT // 2) + u // 2 + 1)
                        pe.wait_ge(s_oh, n * GT + u + 1)
                        for c0, c1 in BANKS:
                            ins = nc.tensor.matmul(counts[:, c0:c1], ohd[:, u, :], ohs[:, u, c0:c1], start=False, stop=False,
                                                   skip_group_check=True)
                        ins.then_inc(s_ohf, 1)
                for c in range(3):
                    ins = nc.tensor.matmul(counts[:, 512 * c:512 * c + 2], zeros[:, 0:P], zeros[:, 0:2], start=False, stop=True,
                                           skip_group_check=True)
                ins.then_inc(s_cn, 1)
                if b >= 1:
                    turn_counts(b - 1)
            turn_counts(BLK - 1)

            pe.wait_ge(s_cs, 3 * BLK)
            pe.wait_ge(s_ro, 2 * BLK)
            def aggregate(c, u, free=True):
                pe.wait_ge(s_ep, c + 1)
                for n, (high, low) in enumerate(((0, 1), (2, 3))):
                    if free:
                        pe.wait_ge(s_sumr, c * 2 - 1 + n)
                    for s in range(BLK):
                        for q in (high, low):
                            for c0, c1 in BANKS:
                                ins = nc.tensor.matmul(PS[:, 1536 * n + c0:1536 * n + c1], parts[u][q][0:P, s, :], CT[0:P, s, c0:c1],
                                                       start=(s == 0 and q == high), stop=(s == BLK - 1 and q == low))
                    ins.then_inc(s_sum, 1)

            aggregate(0, 0, free=False)
            aggregate(1, 1)
            with pe.Fori(1, K // 2) as i:
                for u in range(2):
                    aggregate(i * 2 + u, u)

            def first_layer(m, u, first=False):
                pe.wait_ge(s_w1l, m + 1)
                for k in range(K):
                    if first:
                        pe.wait_ge(s_agl, k + 1)
                    for w, q in ((w1h, XTh), (w1h, XTl), (w1l, XTh)):
                        for c0, c1 in BANKS:
                            ins = nc.tensor.matmul(PS[:, 1536 * u + c0:1536 * u + c1], w[:, u, k, :], q[:, k, c0:c1],
                                                   start=(k == 0 and w is w1h and q is XTh), stop=(k == K - 1 and w is w1l))
                ins.then_inc(s_z, 1)

            pe.wait_ge(s_sumr, 2 * K - 1)
            first_layer(0, 0, first=True)
            pe.wait_ge(s_sumr, 2 * K)
            first_layer(1, 1)
            with pe.Fori(1, HC // 2) as i:
                for u in range(2):
                    pe.wait_ge(s_h, i * 2 + u - 1)
                    first_layer(i * 2 + u, u)

            def second_layer(n, u, h, free=True):
                pe.wait_ge(s_htl, n + 1)
                if free:
                    pe.wait_ge(s_r2, n - 1)
                for k in range(HC):
                    for i, (q, w) in enumerate(((hth, w2h), (hth, w2l), (htl, w2h))):
                        ins = nc.tensor.matmul(bank(u)[0:P, 0:HALF], q[u][:, k, :], w[h][:, k, :],
                                               start=(k == 0 and i == 0), stop=(k == HC - 1 and i == 2))
                ins.then_inc(s_o2, 1)

            def turn_norm2(b):
                pe.wait_ge(s_xn2, b + 1)
                if b >= 2:
                    pe.wait_ge(s_x2s, b - 1)
                for k in range(K):
                    ins = nc.tensor.transpose(bank((2, 5)[b % 2] + k // 3)[:, P * (k % 3):P * (k % 3) + P], xn2[0:P, b % 2, 128 * k:128 * k + 128], ident[0:P, 0:P])
                ins.then_inc(s_x2t, 1)

            def router(b):
                pe.wait_ge(s_x2s, b + 1)
                where = bank(4)[0:P, NE * b:NE * b + NE]
                for k in range(K):
                    nc.tensor.matmul(where, xn2T[:, b % 2, k, :], rw[:, k, :], start=(k == 0), stop=False)
                nc.tensor.matmul(where, ones[0:1, 0:P], rb[:], start=False, stop=True).then_inc(s_lg, 1)

            pe.wait_ge(s_h, HC)
            pe.wait_ge(s_rw, 32)
            pe.wait_ge(s_w2l, 4)
            for n in range(2):
                second_layer(n, n, 0, free=False)
            with pe.Fori(1, BLK // 2) as i:
                for u in range(2):
                    second_layer(i * 2 + u, u, 0)
            pe.wait_ge(s_w2l, 8)
            for b in range(BLK):
                if b >= 2:
                    turn_norm2(b - 2)
                if b >= 3:
                    router(b - 3)
                second_layer(BLK + b, b % 2, 1)
            for b in range(BLK - 2, BLK):
                turn_norm2(b)
                router(b - 1)
            router(BLK - 1)
            pe.wait_ge(s_route, ONE_HOT)
            hot = onehot[0:P].rearrange("p b e -> p (b e)")
            nc.tensor.matmul(bank(5)[0:P, 0:BLK * NE], tri[0:P, 0:P], hot, start=True, stop=True)
            nc.tensor.matmul(bank(6)[0:P, 0:BLK * NE], ones[0:P, 0:P], hot, start=True, stop=True).then_inc(s_rk, 1)

            pe.wait_ge(s_route, SLOTS_D)
            for b in range(BLK):
                ins = nc.tensor.matmul(bank(7)[:, 0:SB], rhot[0:P, b, :], qtok[0:P, b, :], start=(b == 0), stop=(b == BLK - 1))
            ins.then_inc(s_tt, 1)

            def turn_rows(n, u, i):
                pe.wait_ge(s_g[u], i * 16 + 16)
                pe.wait_ge(s_gl, n + 1)
                for k in range(K):
                    ins = nc.tensor.transpose(bank(k // 3)[:, 128 * (k % 3):128 * (k % 3) + 128], xg[:, u, 128 * k:128 * k + 128], ident[:])
                ins.then_inc(s_gt, 1)

            def up(n, u):
                pe.wait_ge(s_gl, n + 2)
                pe.wait_ge(s_fl, n + 1)
                for k in range(K):
                    for i, (q, w) in enumerate(((xgh, w12h), (xgh, w12l), (xgl, w12h))):
                        ins = nc.tensor.matmul(bank(2)[:, :], q[:, u, k, :], w[u][:, k, :], start=(k == 0 and i == 0), stop=(k == K - 1 and i == 2))
                ins.then_inc(s_up, 1)

            def turn_hidden(n):
                pe.wait_ge(s_hd, n + 1)
                for k in range(FC):
                    ins = nc.tensor.transpose(bank(3)[:, 128 * k:128 * k + 128], hid[:, 128 * k:128 * k + 128], ident[:])
                ins.then_inc(s_ht, 1)

            def down_projection(n, u):
                pe.wait_ge(s_hl, n + 1)
                pe.wait_ge(s_f3, n + 1)
                if isinstance(n, int) and n >= 1:
                    pe.wait_ge(s_yb, n)
                for c in range(2):
                    for k in range(FC):
                        for i, (q, w) in enumerate(((hidh, w3h), (hidh, w3l), (hidl, w3h))):
                            ins = nc.tensor.matmul(bank(4 + c)[:, 0:HALF], q[:, k, :], w[u][:, k, HALF * c:HALF * c + HALF],
                                                   start=(k == 0 and i == 0), stop=(k == FC - 1 and i == 2))
                ins.then_inc(s_y, 1)

            pe.sem_inc(s_gl, 1)
            pe.sem_inc(s_up, 2)
            pe.sem_inc(s_y, 2)
            turn_rows(0, 0, 0)
            up(0, 0)
            turn_rows(1, 1, 0)
            turn_hidden(0)
            up(1, 1)
            turn_rows(2, 0, 1)
            down_projection(0, 0)
            turn_hidden(1)
            with pe.Fori(1, SB // 2) as i:
                for u in range(2):
                    n = i * 2 + u
                    up(n, u)
                    turn_rows(n + 1, 1 - u, i + u)
                    pe.wait_ge(s_yb, n - 1)
                    down_projection(n - 1, 1 - u)
                    turn_hidden(n)
            up(SB - 1, 0)
            down_projection(SB - 2, 1)
            turn_hidden(SB - 1)
            down_projection(SB - 1, 0)


_INS = ['x', 'src', 'dst', 'L0_gnn_t', 'L0_gnn_W1', 'L0_gnn_b1', 'L0_gnn_bn_gamma', 'L0_gnn_bn_beta', 'L0_gnn_bn_mean',
        'L0_gnn_bn_var', 'L0_gnn_W2', 'L0_gnn_b2', 'L0_mix_Wq', 'L0_mix_Wk', 'L0_mix_Wv', 'L0_mix_Wo', 'L0_mix_proj',
        'L0_ffn_router_w', 'L0_ffn_router_b', 'L0_ffn_w1', 'L0_ffn_w2', 'L0_ffn_w3']


def kernel(**inputs):
    import numpy as _np
    import concourse.bacc as _bacc
    from concourse import mybir as _mybir
    from concourse.bass_utils import run_bass_kernel_spmd as _run

    nc = _bacc.Bacc("TRN2", target_bir_lowering=False, num_devices=1)
    arrays, args = {}, []
    for name in _INS:
        a = _np.ascontiguousarray(inputs[name])
        if a.ndim == 0:
            a = a.reshape(1)
        arrays[f"in_{name}_dram"] = a
        args.append(nc.dram_tensor(f"in_{name}_dram", a.shape, _mybir.dt.from_np(a.dtype), kind="ExternalInput").ap())
    out = nc.dram_tensor("out_0_dram", (1250, 768), _mybir.dt.float32, kind="ExternalOutput").ap()
    build(nc, *args, out)
    r = _run(nc, [arrays], core_ids=[0])
    return r.results[0]["out_0_dram"]
```
